# Optimizing a Trainium2 kernel written in Bass

```python
import numpy as np
import jax
import jax.numpy as jnp

def _softmax(x, axis=-1):
    return jax.nn.softmax(x, axis=axis)

def _gelu(x):
    return jax.nn.gelu(x, approximate=True)

def _silu(x):
    return jax.nn.silu(x)

def _sigmoid(x):
    return jax.nn.sigmoid(x)

def _layernorm(x, axis=-1, eps=1e-05):
    m = jnp.mean(x, axis=axis, keepdims=True)
    v = jnp.var(x, axis=axis, keepdims=True)
    return (x - m) / jnp.sqrt(v + eps)

def _scatter_add(tgt, idx, src, axis=0):
    return tgt.at[idx].add(src)

def _segment_sum(src, seg, n):
    return jax.ops.segment_sum(src, seg, n)
kernel_name = 'mk_adaln_ffn_d2_seqx_r4_22ac69'

def setup_inputs(seed: int=0):
    np.random.seed(seed)
    _w = jnp.asarray

    def _rec_inputs():
        import jax
        import jax.numpy as jnp
        _rk = jax.random.key(seed)
        x = -0.0003929 + 0.9999 * jax.random.normal(jax.random.fold_in(_rk, 1), (8, 256, 512), jnp.float32)
        _lenS = 256 - jax.random.randint(jax.random.fold_in(_rk, 7), (8,), 0, max(1, 256 // 4) + 1, jnp.int32)
        _lenS2 = 256 - jax.random.randint(jax.random.fold_in(_rk, 8), (8,), 0, max(1, 256 // 4) + 1, jnp.int32)
        cond_2048 = 0.00782532 + 1.00527 * jax.random.normal(jax.random.fold_in(_rk, 11), (8, 512), jnp.float32)
        return (x, cond_2048)
    x, cond_2048 = _rec_inputs()

    def _L0_cond_setup():
        import jax, jax.numpy as jnp
        import numpy as np
        HEADS = 16
        EPS = 1e-06

        def _rms_norm(x, g):
            xf = x.astype(jnp.float32)
            y = xf * jax.lax.rsqrt(jnp.mean(xf * xf, axis=-1, keepdims=True) + EPS)
            return y.astype(x.dtype) * g
        key = jax.random.key(seed)
        ks = jax.random.split(key, 6)
        b, n, dim, emb_dim = (4, 512, 512, 512)
        d_head = dim // HEADS
        return {'x': jax.random.normal(ks[0], (b, n, dim), jnp.float32), 'emb': jax.random.normal(ks[1], (b, 1, emb_dim), jnp.float32), 'W_emb': jax.random.normal(ks[2], (emb_dim, 2 * dim), jnp.float32) * emb_dim ** (-0.5), 'b_emb': jnp.zeros((2 * dim,), jnp.float32), 'g_norm': jnp.ones((dim,), jnp.float32), 'W_qkv': jax.random.normal(ks[3], (dim, 3 * dim), jnp.float32) * dim ** (-0.5), 'g_q': jnp.ones((d_head,), jnp.float32), 'g_k': jnp.ones((d_head,), jnp.float32), 'W_out': jax.random.normal(ks[4], (dim, dim), jnp.float32) * dim ** (-0.5)}
    _L0_cond_all = _L0_cond_setup()
    _L0_cond_in = {k: v for k, v in _L0_cond_all.items() if k in ('W_emb', 'b_emb', 'g_norm', 'W_qkv', 'g_q', 'g_k', 'W_out')}
    del _L0_cond_all

    def _L0_ffn_setup():
        import jax, jax.numpy as jnp
        import numpy as np
        BLOCK = 64

        def dequant4bit(q, scale):
            return (q.astype(jnp.float32) - 7.5) * jnp.repeat(scale, BLOCK, axis=1)
        key = jax.random.key(seed)
        ks = jax.random.split(key, 11)
        B, S, D, H, R = (4, 512, 512, 2048, 16)
        return {'x1': jax.random.normal(ks[0], (B, S, D), jnp.float32), 'w_up_q': jax.random.randint(ks[1], (H, D), 0, 16, dtype=jnp.int32), 'w_up_scale': jax.random.uniform(ks[2], (H, D // BLOCK), jnp.float32) * 0.02, 'b_up': jax.random.normal(ks[3], (H,), jnp.float32) * 0.01, 'w_up_lora_a': jax.random.normal(ks[4], (D, R), jnp.float32) * 0.02, 'w_up_lora_b': jax.random.normal(ks[5], (R, H), jnp.float32) * 0.02, 'w_down_q': jax.random.randint(ks[6], (D, H), 0, 16, dtype=jnp.int32), 'w_down_scale': jax.random.uniform(ks[7], (D, H // BLOCK), jnp.float32) * 0.02, 'b_down': jax.random.normal(ks[8], (D,), jnp.float32) * 0.01, 'w_down_lora_a': jax.random.normal(ks[9], (H, R), jnp.float32) * 0.02, 'w_down_lora_b': jax.random.normal(ks[10], (R, D), jnp.float32) * 0.02}
    _L0_ffn_all = _L0_ffn_setup()
    _L0_ffn_in = {k: v for k, v in _L0_ffn_all.items() if k in ('w_up_q', 'w_up_scale', 'b_up', 'w_up_lora_a', 'w_up_lora_b', 'w_down_q', 'w_down_scale', 'b_down', 'w_down_lora_a', 'w_down_lora_b')}
    del _L0_ffn_all

    def _L1_cond_setup():
        import jax, jax.numpy as jnp
        import numpy as np
        DT = 0.01
        EPSILON = 0.08
        ALPHA = 0.7
        BETA = 0.8
        CLAMP = 20.0
        B, T, N = (64, 128, 512)

        def _derivative(q, p, drive, coupling, bias):
            i_couple = jnp.tanh(q) @ coupling.T
            dq = q - q ** 3 / 3.0 - p + drive + i_couple + bias
            dp = EPSILON * (q + ALPHA - BETA * p)
            return (dq, dp)

        def _rk4_step(q, p, drive, coupling, bias):
            dq1, dp1 = _derivative(q, p, drive, coupling, bias)
            dq2, dp2 = _derivative(q + 0.5 * DT * dq1, p + 0.5 * DT * dp1, drive, coupling, bias)
            dq3, dp3 = _derivative(q + 0.5 * DT * dq2, p + 0.5 * DT * dp2, drive, coupling, bias)
            dq4, dp4 = _derivative(q + DT * dq3, p + DT * dp3, drive, coupling, bias)
            q_next = q + DT / 6.0 * (dq1 + 2 * dq2 + 2 * dq3 + dq4)
            p_next = p + DT / 6.0 * (dp1 + 2 * dp2 + 2 * dp3 + dp4)
            q_next = jnp.clip(q_next, -CLAMP, CLAMP)
            p_next = jnp.clip(p_next, -CLAMP, CLAMP)
            return (q_next, p_next)
        key = jax.random.key(seed)
        k1, k2, k3, k4 = jax.random.split(key, 4)
        return {'q0': jax.random.normal(k1, (B, N), dtype=jnp.float32), 'p0': jax.random.normal(k2, (B, N), dtype=jnp.float32), 'input_drive_seq': jax.random.normal(k3, (B, T, N), dtype=jnp.float32), 'coupling': jax.random.normal(k4, (N, N), dtype=jnp.float32) * 0.01, 'bias': jnp.zeros((N,), dtype=jnp.float32)}
    _L1_cond_all = _L1_cond_setup()
    _L1_cond_in = {k: v for k, v in _L1_cond_all.items() if k in ('coupling', 'bias')}
    del _L1_cond_all

    def _L1_ffn_setup():
        import jax, jax.numpy as jnp
        import numpy as np
        B, S, H = (2, 256, 512)
        E, K = (8, 2)
        F = 352
        FS = 1408
        NORM_TOPK = False

        def _swiglu(x, wg, wu, wd):
            return jax.nn.silu(x @ wg) * (x @ wu) @ wd
        key = jax.random.key(seed)
        ks = jax.random.split(key, 9)
        s = 0.02
        return {'hidden_states': jax.random.normal(ks[0], (B, S, H), dtype=jnp.float32), 'Wr': jax.random.normal(ks[1], (H, E), dtype=jnp.float32) * s, 'Wg': jax.random.normal(ks[2], (E, H, F), dtype=jnp.float32) * s, 'Wu': jax.random.normal(ks[3], (E, H, F), dtype=jnp.float32) * s, 'Wd': jax.random.normal(ks[4], (E, F, H), dtype=jnp.float32) * s, 'Sg': jax.random.normal(ks[5], (H, FS), dtype=jnp.float32) * s, 'Su': jax.random.normal(ks[6], (H, FS), dtype=jnp.float32) * s, 'Sd': jax.random.normal(ks[7], (FS, H), dtype=jnp.float32) * s, 'Wsg': jax.random.normal(ks[8], (H, 1), dtype=jnp.float32) * s}
    _L1_ffn_all = _L1_ffn_setup()
    _L1_ffn_in = {k: v for k, v in _L1_ffn_all.items() if k in ('Wr', 'Wg', 'Wu', 'Wd', 'Sg', 'Su', 'Sd', 'Wsg')}
    del _L1_ffn_all
    return {'x': x, 'cond_2048': cond_2048, 'L0_cond_W_emb': _L0_cond_in['W_emb'], 'L0_cond_b_emb': _L0_cond_in['b_emb'], 'L0_cond_g_norm': _L0_cond_in['g_norm'], 'L0_cond_W_qkv': _L0_cond_in['W_qkv'], 'L0_cond_g_q': _L0_cond_in['g_q'], 'L0_cond_g_k': _L0_cond_in['g_k'], 'L0_cond_W_out': _L0_cond_in['W_out'], 'L0_ffn_w_up_q': _L0_ffn_in['w_up_q'], 'L0_ffn_w_up_scale': _L0_ffn_in['w_up_scale'], 'L0_ffn_b_up': _L0_ffn_in['b_up'], 'L0_ffn_w_up_lora_a': _L0_ffn_in['w_up_lora_a'], 'L0_ffn_w_up_lora_b': _L0_ffn_in['w_up_lora_b'], 'L0_ffn_w_down_q': _L0_ffn_in['w_down_q'], 'L0_ffn_w_down_scale': _L0_ffn_in['w_down_scale'], 'L0_ffn_b_down': _L0_ffn_in['b_down'], 'L0_ffn_w_down_lora_a': _L0_ffn_in['w_down_lora_a'], 'L0_ffn_w_down_lora_b': _L0_ffn_in['w_down_lora_b'], 'L1_cond_coupling': _L1_cond_in['coupling'], 'L1_cond_bias': _L1_cond_in['bias'], 'L1_ffn_Wr': _L1_ffn_in['Wr'], 'L1_ffn_Wg': _L1_ffn_in['Wg'], 'L1_ffn_Wu': _L1_ffn_in['Wu'], 'L1_ffn_Wd': _L1_ffn_in['Wd'], 'L1_ffn_Sg': _L1_ffn_in['Sg'], 'L1_ffn_Su': _L1_ffn_in['Su'], 'L1_ffn_Sd': _L1_ffn_in['Sd'], 'L1_ffn_Wsg': _L1_ffn_in['Wsg']}

def reference(x, cond_2048, L0_cond_W_emb, L0_cond_b_emb, L0_cond_g_norm, L0_cond_W_qkv, L0_cond_g_q, L0_cond_g_k, L0_cond_W_out, L0_ffn_w_up_q, L0_ffn_w_up_scale, L0_ffn_b_up, L0_ffn_w_up_lora_a, L0_ffn_w_up_lora_b, L0_ffn_w_down_q, L0_ffn_w_down_scale, L0_ffn_b_down, L0_ffn_w_down_lora_a, L0_ffn_w_down_lora_b, L1_cond_coupling, L1_cond_bias, L1_ffn_Wr, L1_ffn_Wg, L1_ffn_Wu, L1_ffn_Wd, L1_ffn_Sg, L1_ffn_Su, L1_ffn_Sd, L1_ffn_Wsg):
    import jax
    import jax.numpy as jnp

    def _L0_cond_ref(x, emb, W_emb, b_emb, g_norm, W_qkv, g_q, g_k, W_out):
        import jax, jax.numpy as jnp
        import numpy as np
        HEADS = 16
        EPS = 1e-06

        def _rms_norm(x, g):
            xf = x.astype(jnp.float32)
            y = xf * jax.lax.rsqrt(jnp.mean(xf * xf, axis=-1, keepdims=True) + EPS)
            return y.astype(x.dtype) * g
        b, n, dim = x.shape
        h = HEADS
        d = dim // h
        scale_shift = emb @ W_emb + b_emb
        scale, shift = jnp.split(scale_shift, 2, axis=-1)
        xn = _rms_norm(x, g_norm) * (1.0 + scale) + shift
        qkv = xn @ W_qkv
        qkv = qkv.reshape(b, n, 3, h, d)
        q, k, v = jnp.moveaxis(qkv, 2, 0)
        q = jnp.swapaxes(q, 1, 2)
        k = jnp.swapaxes(k, 1, 2)
        v = jnp.swapaxes(v, 1, 2)
        q = _rms_norm(q, g_q)
        k = _rms_norm(k, g_k)
        logits = jnp.einsum('bhqd,bhkd->bhqk', q, k) * d ** (-0.5)
        attn = jax.nn.softmax(logits, axis=-1)
        o = jnp.einsum('bhqk,bhkd->bhqd', attn, v)
        o = jnp.swapaxes(o, 1, 2).reshape(b, n, dim)
        return o + o @ W_out

    def _L0_ffn_ref(x1, w_up_q, w_up_scale, b_up, w_up_lora_a, w_up_lora_b, w_down_q, w_down_scale, b_down, w_down_lora_a, w_down_lora_b):
        import jax, jax.numpy as jnp
        import numpy as np
        BLOCK = 64

        def dequant4bit(q, scale):
            return (q.astype(jnp.float32) - 7.5) * jnp.repeat(scale, BLOCK, axis=1)
        w_up = dequant4bit(w_up_q, w_up_scale).T
        y1 = x1 @ w_up + b_up + x1 @ w_up_lora_a @ w_up_lora_b
        x2 = jax.nn.relu(y1)
        w_down = dequant4bit(w_down_q, w_down_scale).T
        y2 = x2 @ w_down + b_down + x2 @ w_down_lora_a @ w_down_lora_b
        return y2

    def _L1_cond_ref(q0, p0, input_drive_seq, coupling, bias):
        import jax, jax.numpy as jnp
        import numpy as np
        DT = 0.01
        EPSILON = 0.08
        ALPHA = 0.7
        BETA = 0.8
        CLAMP = 20.0
        B, T, N = (64, 128, 512)

        def _derivative(q, p, drive, coupling, bias):
            i_couple = jnp.tanh(q) @ coupling.T
            dq = q - q ** 3 / 3.0 - p + drive + i_couple + bias
            dp = EPSILON * (q + ALPHA - BETA * p)
            return (dq, dp)

        def _rk4_step(q, p, drive, coupling, bias):
            dq1, dp1 = _derivative(q, p, drive, coupling, bias)
            dq2, dp2 = _derivative(q + 0.5 * DT * dq1, p + 0.5 * DT * dp1, drive, coupling, bias)
            dq3, dp3 = _derivative(q + 0.5 * DT * dq2, p + 0.5 * DT * dp2, drive, coupling, bias)
            dq4, dp4 = _derivative(q + DT * dq3, p + DT * dp3, drive, coupling, bias)
            q_next = q + DT / 6.0 * (dq1 + 2 * dq2 + 2 * dq3 + dq4)
            p_next = p + DT / 6.0 * (dp1 + 2 * dp2 + 2 * dp3 + dp4)
            q_next = jnp.clip(q_next, -CLAMP, CLAMP)
            p_next = jnp.clip(p_next, -CLAMP, CLAMP)
            return (q_next, p_next)
        drive_tbn = jnp.swapaxes(input_drive_seq, 0, 1)

        def scan_fn(carry, drive):
            q, p = carry
            q, p = _rk4_step(q, p, drive, coupling, bias)
            return ((q, p), q)
        (_, _), q_trace_tbn = jax.lax.scan(scan_fn, (q0, p0), drive_tbn)
        return jnp.swapaxes(q_trace_tbn, 0, 1)

    def _L1_ffn_ref(hidden_states, Wr, Wg, Wu, Wd, Sg, Su, Sd, Wsg):
        import jax, jax.numpy as jnp
        import numpy as np
        B, S, H = (2, 256, 512)
        E, K = (8, 2)
        F = 352
        FS = 1408
        NORM_TOPK = False

        def _swiglu(x, wg, wu, wd):
            return jax.nn.silu(x @ wg) * (x @ wu) @ wd
        b, s, h = hidden_states.shape
        x = hidden_states.reshape(-1, h)
        router_logits = x @ Wr
        probs = jax.nn.softmax(router_logits.astype(jnp.float32), axis=-1)
        routing_weights, selected = jax.lax.top_k(probs, K)
        if NORM_TOPK:
            routing_weights = routing_weights / routing_weights.sum(-1, keepdims=True)
        routing_weights = routing_weights.astype(x.dtype)
        C = jnp.einsum('tk,tke->te', routing_weights, jax.nn.one_hot(selected, E, dtype=x.dtype))
        expert_out = jax.vmap(lambda wg, wu, wd: _swiglu(x, wg, wu, wd))(Wg, Wu, Wd)
        moe_out = jnp.einsum('te,eth->th', C, expert_out)
        shared = _swiglu(x, Sg, Su, Sd)
        shared = jax.nn.sigmoid(x @ Wsg) * shared
        out = (moe_out + shared).reshape(b, s, h)
        return out
    x = x + _L0_ffn_ref(_L0_cond_ref(x, cond_2048[:, None, :], L0_cond_W_emb, L0_cond_b_emb, L0_cond_g_norm, L0_cond_W_qkv, L0_cond_g_q, L0_cond_g_k, L0_cond_W_out), L0_ffn_w_up_q, L0_ffn_w_up_scale, L0_ffn_b_up, L0_ffn_w_up_lora_a, L0_ffn_w_up_lora_b, L0_ffn_w_down_q, L0_ffn_w_down_scale, L0_ffn_b_down, L0_ffn_w_down_lora_a, L0_ffn_w_down_lora_b)
    x = x + _L1_ffn_ref(_L1_cond_ref(cond_2048, cond_2048, x, L1_cond_coupling, L1_cond_bias), L1_ffn_Wr, L1_ffn_Wg, L1_ffn_Wu, L1_ffn_Wd, L1_ffn_Sg, L1_ffn_Su, L1_ffn_Sd, L1_ffn_Wsg)
    return x

_drawn_inputs = setup_inputs


def setup_inputs(seed=0):
    import zlib

    import numpy as np

    out = dict(_drawn_inputs(seed))
    spreads = {'L0_cond_b_emb': (0.0, 0.1),
     'L0_cond_g_norm': (1.0, 0.2),
     'L0_cond_g_q': (1.0, 0.6),
     'L0_cond_g_k': (1.0, 0.6),
     'L1_cond_bias': (0.0, 0.8)}
    factors = {'L0_ffn_b_up': 8.0, 'L0_ffn_b_down': 8.0, 'L1_cond_coupling': 6.229, 'L1_ffn_Wr': 2.908}
    for name, (base, spread) in spreads.items():
        noise = np.random.default_rng([zlib.crc32(name.encode()), seed]).standard_normal(out[name].shape)
        drawn = base * np.exp(spread * noise) if base else spread * noise
        out[name] = jnp.asarray(drawn.astype(out[name].dtype))
    for name, factor in factors.items():
        out[name] = (out[name] * factor).astype(out[name].dtype)
    return out
```

```python
import concourse.bass as bass
from concourse import mybir
from contextlib import ExitStack

F32, F16, BF16, I32 = mybir.dt.float32, mybir.dt.float16, mybir.dt.bfloat16, mybir.dt.int32
ALU = mybir.AluOpType
ACT = mybir.ActivationFunctionType
AX = mybir.AxisListType
P = 128

B, T, N = 8, 256, 512
NC = N // P
HEADS, DH = 16, 32
HPC = P // DH
H0 = 2048
HC = H0 // P
QBLOCK = 64
R = 16
DT, EPSILON, ALPHA, BETA, CLAMP = 0.01, 0.08, 0.7, 0.8, 20.0


def layer0(nc, dram, xs):
    ctx = ExitStack()
    with ctx:
        sb = lambda n, s, d=F32: ctx.enter_context(nc.sbuf_tensor(n, s, d))
        sem = lambda n: ctx.enter_context(nc.semaphore(n))
        w_emb = sb("w_emb", [P, NC, 2 * N])
        early = w_emb[:].rearrange("p c n -> p (c n)")
        qk = early[:, 0:2 * NC * T].rearrange("p (c a t) -> p c a t", a=2, t=T)
        pr = early[:, 2048:3072].rearrange("p (u a t) -> p u a t", u=2, a=2)
        prT = early[:, 3072:4096].rearrange("p (u a t) -> p u a t", u=2, a=2)
        w_qkv = sb("w_qkv", [P, NC, 3 * N])
        w_out = sb("w_out", [P, NC, N])
        w_up = sb("w_up", [P, NC, H0])
        w_dn = sb("w_dn", [P, HC, N])
        hid = sb("hid", [P, HC, T])
        codes = hid[:].rearrange("p a t -> p (a t)")[:, 0:H0].bitcast(I32)
        scales = hid[:].rearrange("p a t -> p (a t)")[:, H0:2 * H0]
        work = sb("work", [P, 5 * NC * T])
        lora_a = work[0:R, 0:N + H0]
        lora_b = work[0:R, N + H0:2 * (N + H0)]
        sq = work[:, 0:1024].rearrange("p (c t) -> p c t", c=NC)
        xn = work[:, 1024:2048].rearrange("p (c t) -> p c t", c=NC)
        sqh = work[:, 2048:3072].rearrange("p (u a t) -> p u a t", u=2, a=2)
        rh = work[:, 3072:4096].rearrange("p (u a t) -> p u a t", u=2, a=2)
        v = work[:, 4096:5120].rearrange("p (a n) -> p a n", a=2)
        vecs = sb("vecs", [P, 64])
        condT = vecs[:, 0:NC * B].rearrange("p (c b) -> p c b", b=B)
        b_emb, g_norm = vecs[:, 32:40], vecs[:, 40:44]
        b_up, b_dn, b_scan, g_q, g_k = vecs[:, 44:60], sb("b_dn", [P, NC]), sb("b_scan", [P, NC]), vecs[:, 60:61], vecs[:, 61:62]
        eps = vecs[:, 62:63]
        ones = sb("ones", [P, P])
        headones = sb("headones", [P, P])
        ident = sb("ident", [P, P])
        ss = sb("ss", [P, 2 * NC, B])
        amp = sb("amp", [P, NC, B])
        bias2 = sb("bias2", [P, NC])
        rs = sb("rs", [P, 2, T])
        nmax = sb("nmax", [P, 2, 2])
        psum_e = sb("psum_e", [P, HEADS, 2])
        rinv = sb("rinv", [P, HEADS, 2])
        o = sb("o", [P, 2, N])
        oT = sb("oT", [P, NC, T])
        x1 = sb("x1", [P, NC, T])
        bank = [ctx.enter_context(nc.psum_tensor(f"l0bank{i}", [P, 512], F32)) for i in range(8)]
        G, Rb, Ob, D = bank[0:2], bank[2:4], bank[4:6], bank[6:8]
        names = ("x_in w_in emb_in qkv_in ups up_codes dn_codes lora vec_in eye mm_ss mm_lora ss_rd deq a_sqx a_rstd a_sq a_hr a_v a_exp a_up "
                 "p_nrm p_qk p_hr p_v p_s p_t p_pv p_ot p_wo p_up p_dn d_xn d_qk d_max d_pt d_o d_ot d_x1 d_x2 chain achain amps gch wo_in stage").split()
        S = {n: sem("l0_" + n) for n in names}
        block = ctx.enter_context(nc.Block())
        xv = xs[:, 0:NC * B * T].rearrange("p (c b t) -> p c b t", c=NC, b=B)
        NQ = 8

        @block.sync
        def _(sp):
            sp.dma_start(vecs[:, 0:62], dram["vecs"]).then_inc(S["vec_in"], 16)
            sp.dma_start(b_dn[:], dram["b_dn"]).then_inc(S["vec_in"], 16)
            sp.dma_start(b_scan[:], dram["b_scan"]).then_inc(S["vec_in"], 16)
            sp.dma_start(w_emb[:], dram["w_emb"]).then_inc(S["emb_in"], 16)
            sp.dma_start(lora_a, dram["lora_a"]).then_inc(S["lora"], 16)
            sp.dma_start(lora_b, dram["lora_b"]).then_inc(S["lora"], 16)
            for j in range(NQ):
                if j:
                    sp.wait_ge(S["stage"], j)
                if j < NC:
                    src, sc = dram["up_q"][:, j, :], dram["up_s"]
                    for half in range(2):
                        sp.dma_start(scales[half * 64:half * 64 + 64, :], sc[2 * j + half].partition_broadcast(64)).then_inc(S["up_codes"], 16)
                else:
                    src = dram["dn_q"][:, 4 * (j - 4):4 * (j - 4) + 4, :].rearrange("p a n -> p (a n)")
                    for a in range(4):
                        for half in range(2):
                            sp.dma_start(scales[half * 64:half * 64 + 64, a * N:(a + 1) * N],
                                         dram["dn_s"][2 * (4 * (j - 4) + a) + half].partition_broadcast(64)).then_inc(S["up_codes"], 16)
                sp.dma_start(codes, src).then_inc(S["up_codes"], 16)
            sp.dma_start(w_out[:], dram["w_out"]).then_inc(S["wo_in"], 16)

        @block.gpsimd
        def _(pl):
            pl.memset(ones[:], 1.0).then_inc(S["gch"], 1)
            pl.memset(ident[:], 0.0).then_inc(S["gch"], 1)
            pl.memset(headones[:], 1.0).then_inc(S["gch"], 1)
            pl.memset(eps, 1e-6).then_inc(S["gch"], 1)
            pl.wait_ge(S["gch"], 4)
            pl.affine_select(out=ident[:], in_=ident[:], compare_op=ALU.not_equal, fill=1.0, base=0,
                             pattern=[[-1, P]], channel_multiplier=1).then_inc(S["gch"], 1)
            hv = headones[:].rearrange("p (h d) -> p h d", d=DH)
            pl.affine_select(out=hv, in_=hv, compare_op=ALU.is_ge, fill=0.0, base=0,
                             pattern=[[-DH, HPC], [0, DH]], channel_multiplier=1).then_inc(S["gch"], 1)
            pl.wait_ge(S["gch"], 6)
            pl.affine_select(out=hv, in_=hv, compare_op=ALU.is_ge, fill=0.0, base=DH - 1,
                             pattern=[[DH, HPC], [0, DH]], channel_multiplier=-1).then_inc(S["eye"], 1)

        @block.scalar
        def _(act):
            act.dma_start(xv, dram["x"]).then_inc(S["x_in"], 16)
            act.dma_start(w_qkv[:], dram["w_qkv"]).then_inc(S["qkv_in"], 16)
            act.wait_ge(S["eye"], 1)
            act.wait_ge(S["vec_in"], 48)
            act.wait_ge(S["x_in"], 16)
            act.wait_ge(S["stage"], NQ)
            nc.scalar.preload_act_table_set("natural_log_exp_and_others")
            with act.Fori(0, B) as b:
                act.activation(sq[:], xv[:, :, bass.ds(b, 1), :].rearrange("p c o t -> p c (o t)"), ACT.Square).then_inc(S["a_sqx"], 1)
                act.wait_ge(S["p_nrm"], b + 1)
                act.activation(rs[:, 0, :], Rb[0][:, 0:T], ACT.Ln, scale=1.0 / N, bias=eps).then_inc(S["achain"], 1)
                act.wait_ge(S["achain"], b * 5 + 1)
                act.activation(rs[:, 1, :], rs[:, 0, :], ACT.Exp, scale=-0.5).then_inc(S["a_rstd"], 1)
                def square(c):
                    act.wait_ge(S["p_qk"], b * NC + c + 1)
                    act.activation(sqh[:, c % 2], G[c % 2][:].rearrange("p (a t) -> p a t", a=2), ACT.Square).then_inc(S["a_sq"], 1)
                square(0)
                for c in range(NC):
                    if c + 1 < NC:
                        square(c + 1)
                    act.wait_ge(S["p_hr"], b * NC + c + 1)
                    act.activation(rh[:, c % 2], Rb[c % 2][:].rearrange("p (a t) -> p a t", a=2), ACT.Ln, scale=1.0 / DH, bias=eps).then_inc(S["achain"], 1)
                    act.wait_ge(S["achain"], b * 5 + 2 + c)
                    act.activation(rh[:, c % 2], rh[:, c % 2], ACT.Exp, scale=-0.5).then_inc(S["a_hr"], 1)
                for i in range(2):
                    act.wait_ge(S["p_v"], b * 2 + i + 1)
                    act.activation(v[:, i, :], Ob[i][:], ACT.Copy).then_inc(S["a_v"], 1)
                for h in range(HEADS):
                    act.wait_ge(S["d_max"], b * HEADS + h + 1)
                    for qc in range(2):
                        ins = act.activation(pr[:, h % 2, qc, :], G[h % 2][:, qc * T:(qc + 1) * T], ACT.Exp,
                                             bias=nmax[:, h % 2, qc:qc + 1], accum_out=psum_e[:, h, qc:qc + 1])
                    ins.then_inc(S["a_exp"], 1)
                for j in range(HC // 2):
                    act.wait_ge(S["p_up"], b * (HC // 2) + j + 1)
                    src = [Rb[0], Rb[1], G[0], G[1]][j % 4]
                    for i in range(2):
                        ins = act.activation(hid[:, 2 * j + i, :], src[:, i * T:(i + 1) * T], ACT.Relu, bias=b_up[:, 2 * j + i:2 * j + i + 1])
                    ins.then_inc(S["a_up"], 1)

        @block.tensor
        def _(pe):
            mm = nc.tensor.matmul
            pe.wait_ge(S["emb_in"], 16)
            pe.wait_ge(S["vec_in"], 48)
            for m in range(2 * NC):
                for k in range(NC):
                    ins = mm(Ob[0][:, m * B:(m + 1) * B], w_emb[:, k, m * P:(m + 1) * P], condT[:, k, :], start=(k == 0), stop=(k == NC - 1))
            ins.then_inc(S["mm_ss"], 1)
            pe.wait_ge(S["lora"], 32)
            for j in range(NQ):
                if j:
                    pe.wait_ge(S["stage"], j)
                for i in range(4):
                    if j < NC:
                        a, bb = lora_a[:, j * P:(j + 1) * P], lora_b[:, i * 512:(i + 1) * 512]
                    else:
                        hc = 4 * (j - NC) + i
                        a, bb = lora_a[:, N + hc * P:N + (hc + 1) * P], lora_b[:, H0:H0 + N]
                    ins = mm(bank[i][:], a, bb, start=True, stop=True)
                ins.then_inc(S["mm_lora"], 1)
            pe.wait_ge(S["eye"], 1)
            pe.wait_ge(S["qkv_in"], 16)
            pe.wait_ge(S["stage"], NQ)
            pe.wait_ge(S["wo_in"], 16)
            pe.wait_ge(S["amps"], 1)
            with pe.Fori(0, B) as b:
                pe.wait_ge(S["a_sqx"], b + 1)
                for k in range(NC):
                    ins = mm(Rb[0][:, 0:T], ones[:], sq[:, k, :], start=(k == 0), stop=(k == NC - 1))
                ins.then_inc(S["p_nrm"], 1)
                pe.wait_ge(S["d_xn"], b + 1)
                def head_norm(c):
                    pe.wait_ge(S["a_sq"], b * NC + c + 1)
                    if c >= 2:
                        pe.wait_ge(S["a_hr"], b * NC + c - 1)
                    mm(Rb[c % 2][:], headones[:], sqh[:, c % 2].rearrange("p a t -> p (a t)"), start=True, stop=True).then_inc(S["p_hr"], 1)
                for c in range(NC):
                    if c >= 2:
                        pe.wait_ge(S["d_qk"], b * NC + c - 1)
                    for a in range(2):
                        for k in range(NC):
                            ins = mm(G[c % 2][:, a * T:(a + 1) * T], w_qkv[:, k, a * N + c * P:a * N + (c + 1) * P], xn[:, k, :],
                                     start=(k == 0), stop=(k == NC - 1))
                    ins.then_inc(S["p_qk"], 1)
                    if c:
                        head_norm(c - 1)
                for i in range(2):
                    for k in range(NC):
                        ins = mm(Ob[i][:], xn[:, k, i * P:(i + 1) * P], w_qkv[:, k, 2 * N:3 * N], start=(k == 0), stop=(k == NC - 1))
                    ins.then_inc(S["p_v"], 1)
                    if i == 0:
                        head_norm(NC - 1)
                def scores(h):
                    c, r = h // HPC, DH * (h % HPC)
                    if h == 0:
                        pe.wait_ge(S["d_qk"], b * NC + NC)
                    if h >= 2:
                        pe.wait_ge(S["a_exp"], b * HEADS + h - 1)
                    for qc in range(2):
                        ins = mm(G[h % 2][:, qc * T:(qc + 1) * T], qk[r:r + DH, c, 0, qc * P:(qc + 1) * P], qk[r:r + DH, c, 1, :], start=True, stop=True)
                    ins.then_inc(S["p_s"], 1)
                def transposed(h):
                    pe.wait_ge(S["a_exp"], b * HEADS + h + 1)
                    if h >= 2:
                        pe.wait_ge(S["d_pt"], b * HEADS + h - 1)
                    for kc in range(2):
                        for qc in range(2):
                            ins = nc.tensor.transpose(Rb[h % 2][:, kc * T + qc * P:kc * T + (qc + 1) * P], pr[:, h % 2, qc, kc * P:(kc + 1) * P], ident[:])
                    ins.then_inc(S["p_t"], 1)
                def weighted(h):
                    pe.wait_ge(S["d_pt"], b * HEADS + h + 1)
                    if h == 0:
                        pe.wait_ge(S["a_v"], b * 2 + 2)
                    for qc in range(2):
                        for kc in range(2):
                            ins = mm(Ob[qc][:, h * DH:(h + 1) * DH], prT[:, h % 2, kc, qc * P:(qc + 1) * P], v[:, kc, h * DH:(h + 1) * DH],
                                     start=(kc == 0), stop=(kc == 1))
                    if h == HEADS - 1:
                        ins.then_inc(S["p_pv"], 1)
                scores(0)
                for h in range(HEADS):
                    if h + 1 < HEADS:
                        scores(h + 1)
                    transposed(h)
                    if h:
                        weighted(h - 1)
                weighted(HEADS - 1)
                pe.wait_ge(S["d_o"], b + 1)
                for i in range(2):
                    for c in (2 * i, 2 * i + 1):
                        for qc in range(2):
                            ins = nc.tensor.transpose(D[i][:, (c % 2) * T + qc * P:(c % 2) * T + (qc + 1) * P], o[:, qc, c * P:(c + 1) * P], ident[:])
                    ins.then_inc(S["p_ot"], 1)
                pe.wait_ge(S["d_ot"], b * 2 + 2)
                for m in range(NC):
                    for k in range(NC):
                        ins = mm(G[m // 2][:, (m % 2) * T:(m % 2 + 1) * T], w_out[:, k, m * P:(m + 1) * P], oT[:, k, :], start=(k == 0), stop=(k == NC - 1))
                    if m % 2:
                        ins.then_inc(S["p_wo"], 1)
                pe.wait_ge(S["d_x1"], b * 2 + 2)
                for j in range(HC // 2):
                    dst = [Rb[0], Rb[1], G[0], G[1]][j % 4]
                    if j >= 4:
                        pe.wait_ge(S["a_up"], b * (HC // 2) + j - 3)
                    for i in range(2):
                        for k in range(NC):
                            ins = mm(dst[:, i * T:(i + 1) * T], w_up[:, k, (2 * j + i) * P:(2 * j + i + 1) * P], x1[:, k, :], start=(k == 0), stop=(k == NC - 1))
                    ins.then_inc(S["p_up"], 1)
                pe.wait_ge(S["a_up"], (b + 1) * (HC // 2))
                for m in range(NC):
                    for k in range(HC):
                        ins = mm(D[m // 2][:, (m % 2) * T:(m % 2 + 1) * T], w_dn[:, k, m * P:(m + 1) * P], hid[:, k, :], start=(k == 0), stop=(k == HC - 1))
                    if m % 2:
                        ins.then_inc(S["p_dn"], 1)

        @block.vector
        def _(dve):
            count = [0]
            def link(ins, at=None):
                count[0] += 1
                ins.then_inc(S["chain"], 1)
                dve.wait_ge(S["chain"], count[0] if at is None else at + count[0])
            dve.wait_ge(S["vec_in"], 48)
            dve.wait_ge(S["mm_ss"], 1)
            link(dve.tensor_tensor(ss[:], Ob[0][:, 0:2 * NC * B].rearrange("p (m b) -> p m b", b=B), b_emb.unsqueeze(2).to_broadcast([P, 2 * NC, B]), ALU.add))
            link(dve.scalar_tensor_tensor(amp[:], ss[:, 0:NC, :], 1.0, g_norm.unsqueeze(2).to_broadcast([P, NC, B]), ALU.add, ALU.mult))
            link(dve.tensor_scalar(bias2[:], b_scan[:], ALPHA / BETA, None, ALU.subtract))
            link(dve.tensor_tensor(bias2[:], bias2[:], b_dn[:], ALU.add))
            dve.scalar_tensor_tensor(g_q, g_q, DH ** -0.5, g_k, ALU.mult, ALU.mult).then_inc(S["amps"], 1)
            n = 0
            for j in range(NQ):
                n += 3 if j < NC else 9
                dve.wait_ge(S["up_codes"], 16 * n)
                link(dve.scalar_tensor_tensor(scales, codes, 7.5, scales, ALU.subtract, ALU.mult))
                dve.wait_ge(S["mm_lora"], j + 1)
                for i in range(4):
                    dst = w_up[:, j, i * 512:(i + 1) * 512] if j < NC else w_dn[:, 4 * (j - NC) + i, :]
                    ins = dve.tensor_tensor(dst, bank[i][:], scales[:, i * 512:(i + 1) * 512], ALU.add)
                ins.then_inc(S["stage"], 1)
            base = count[0]
            KD = 4
            with dve.Fori(0, B) as b:
                count[0] = 0
                at = base + b * KD
                xb = xv[:, :, bass.ds(b, 1), :].rearrange("p c o t -> p c (o t)")
                dve.wait_ge(S["a_rstd"], b + 1)
                link(dve.tensor_tensor(xn[:], xb, rs[:, 1:2, :].to_broadcast([P, NC, T]), ALU.mult), at)
                for c in range(NC):
                    ins = dve.tensor_scalar(xn[:, c, :], xn[:, c, :], amp[:, c, bass.ds(b, 1)], ss[:, NC + c, bass.ds(b, 1)], ALU.mult, ALU.add)
                ins.then_inc(S["d_xn"], 1)
                for c in range(NC):
                    dve.wait_ge(S["a_hr"], b * NC + c + 1)
                    dve.scalar_tensor_tensor(qk[:, c, 0, :], G[c % 2][:, 0:T], g_q, rh[:, c % 2, 0, :], ALU.mult, ALU.mult)
                    dve.tensor_tensor(qk[:, c, 1, :], G[c % 2][:, T:2 * T], rh[:, c % 2, 1, :], ALU.mult).then_inc(S["d_qk"], 1)
                def row_max(h):
                    dve.wait_ge(S["p_s"], b * HEADS + h + 1)
                    dve.tensor_reduce(nmax[:, h % 2, :], G[h % 2][:].rearrange("p (a t) -> p a t", a=2), AX.X, ALU.max, negate=True).then_inc(S["d_max"], 1)
                row_max(0)
                for h in range(HEADS):
                    if h + 1 < HEADS:
                        if h >= 1:
                            dve.wait_ge(S["a_exp"], b * HEADS + h)
                        row_max(h + 1)
                    dve.wait_ge(S["p_t"], b * HEADS + h + 1)
                    dve.tensor_copy(prT[:, h % 2].rearrange("p a t -> p (a t)"), Rb[h % 2][:]).then_inc(S["d_pt"], 1)
                dve.wait_ge(S["a_exp"], (b + 1) * HEADS)
                link(dve.reciprocal(rinv[:], psum_e[:]), at)
                dve.wait_ge(S["p_pv"], b + 1)
                for qc in range(2):
                    ins = dve.tensor_tensor(o[:, qc, :].rearrange("p (h d) -> p h d", d=DH), Ob[qc][:].rearrange("p (h d) -> p h d", d=DH),
                                            rinv[:, :, qc:qc + 1].to_broadcast([P, HEADS, DH]), ALU.mult)
                ins.then_inc(S["d_o"], 1)
                for i in range(2):
                    dve.wait_ge(S["p_ot"], b * 2 + i + 1)
                    dve.tensor_copy(oT[:, 2 * i:2 * i + 2, :].rearrange("p a t -> p (a t)"), D[i][:]).then_inc(S["d_ot"], 1)
                for i in range(2):
                    dve.wait_ge(S["p_wo"], b * 2 + i + 1)
                    if i == 0:
                        dve.wait_ge(S["d_ot"], b * 2 + 2)
                    dve.tensor_tensor(x1[:, 2 * i:2 * i + 2, :].rearrange("p a t -> p (a t)"), G[i][:], oT[:, 2 * i:2 * i + 2, :].rearrange("p a t -> p (a t)"), ALU.add).then_inc(S["d_x1"], 1)
                for i in range(2):
                    dve.wait_ge(S["p_dn"], b * 2 + i + 1)
                    for c in (2 * i, 2 * i + 1):
                        slot = xv[:, c, bass.ds(b, 1), :].rearrange("p o t -> p (o t)")
                        ins = dve.scalar_tensor_tensor(slot, D[i][:, (c % 2) * T:(c % 2 + 1) * T], bias2[:, c:c + 1], slot, ALU.add, ALU.add)
                    ins.then_inc(S["d_x2"], 1)
                while count[0] < KD:
                    count[0] += 1
                    dve.sem_inc(S["chain"], 1)


E1, F1, FS = 8, 352, 1408
LANES = P // E1
TE = F1 // LANES
TS = FS // P
TILES = TE + TS
G = 32
NG = T // G
GT = G * B
W = NC * B
RK = [DT / 2, DT / 2, DT, DT / 6]
SHIFT = 2.0 ** 13


def linear_terms():
    import numpy as np
    q, p, d, q2, q3, q4 = np.eye(6)
    e = EPSILON * BETA
    p2 = p + DT / 2 * e * (q - p)
    p3 = p + DT / 2 * e * (q2 - p2)
    p4 = p + DT * e * (q3 - p3)
    rows = [q + RK[0] * (d - p / BETA), q + RK[1] * (d - p2 / BETA), q + RK[2] * (d - p3 / BETA),
            (-q + q2 + 2 * q3 + q4) / 3 + RK[3] * (d - p4 / BETA),
            (-p + p2 + 2 * p3 + p4) / 3 + RK[3] * e * (q4 - p4)]
    return np.array(rows)


def layer1(nc, dram, xs, out):
    ctx = ExitStack()
    with ctx:
        sb = lambda n, s, d=F32: ctx.enter_context(nc.sbuf_tensor(n, s, d))
        sem = lambda n: ctx.enter_context(nc.semaphore(n))
        cT = sb("cT", [P, NC, N])
        chi = sb("chi", [P, NC, N], F16)
        clo = sb("clo", [P, NC, N], F16)
        kp = sb("kp", [P, 8])
        b_scan = sb("b_scan1", [P, NC])
        unshift = sb("unshift", [P, NC])
        state = [sb(f"state{s}", [P, W]) for s in range(4)]
        qraw = sb("qraw", [P, W])
        pst = sb("pst", [P, W])
        th = sb("th", [P, NC, 2, B], F16)
        t32 = sb("t32", [P, W])
        sq = sb("sq1", [P, W]); cub = sb("cub", [P, W]); base = sb("base", [P, W]); part = sb("part", [P, W])
        cq, cp, cd = (sb(n, [P, 5, W]) for n in ("coef_q", "coef_p", "coef_d"))
        c2 = sb("coef2", [P, 3, W]); c3 = sb("coef3", [P, 2, W]); c4 = sb("coef4", [P, 2, W])
        A = [sb(f"lin{u}", [P, 5, W]) for u in range(2)]
        md, mp_ = (sb(n, [P, 5, W]) for n in ("from_drive", "from_p"))
        mq = sb("from_q", [P, 4, W])
        ms, ms3, ms4 = (sb(n, [P, r, W]) for n, r in (("from_q2", 3), ("from_q3", 2), ("from_q4", 2)))
        zeros = sb("zeros", [P, 512], BF16)
        trace = sb("trace", [P, NC, G, B])
        qg = sb("qg", [P, NC, GT])
        wgu = sb("wgu", [P, 2, 2, NC, P])
        wd = sb("wd", [P, 2, N])
        wr = sb("wr", [P, NC, E1 + 1])
        ident = sb("ident1", [P, P])
        lanes = sb("lanes", [P, E1])
        rt = sb("rt", [P, 2, E1 + 1]); top = sb("top", [P, 2, 8]); topi = sb("topi", [P, 2, 8], mybir.dt.uint32); topf = sb("topf", [P, 2, 8])
        ex = sb("ex", [P, 2, E1 + 1]); es = sb("es", [P, 2, 4]); msk = sb("msk", [P, 2, 2, E1]); wide = sb("wide", [P, 2, 2, P])
        neg = sb("neg", [P, 2])
        gates = sb("gates", [P, 2, GT])
        sg = sb("sg", [P, GT]); ha = sb("ha", [P, GT]); hb = sb("hb", [P, GT]); hg = sb("hg", [P, 2, GT])
        oo = sb("oo", [P, NC, G, B])
        pscan = ctx.enter_context(nc.psum_tensor("pscan", [P, NC, 2, B], F32))
        pg = ctx.enter_context(nc.psum_tensor("pg", [P, 512], F32))
        pu = ctx.enter_context(nc.psum_tensor("pu", [P, 512], F32))
        pd = [ctx.enter_context(nc.psum_tensor(f"pd{i}", [P, 512], F32)) for i in range(2)]
        pr_ = ctx.enter_context(nc.psum_tensor("prouter", [P, 512], F32))
        names = ("cin vin eye par mx kps scale_rdy linit coef th_ready t32_ready sq_ready tl_ready ic_ready q_ready clip_ready pclip_ready e_ready "
                 "traced lin_ready copied dchain pchain wg0 wg1 wd0 wd1 up_done dn_done gate_done sg_ready ha_ready hb_ready hid_ready fin out_ready stored "
                 "spseq plseq dveseq rt_mm rt_max rt_exp rt_wide rt_tr gates_ready rchain rachain").split()
        S = {n: sem("l1_" + n) for n in names}
        wsem = [S["wg0"], S["wg1"]]; dsem = [S["wd0"], S["wd1"]]
        block = ctx.enter_context(nc.Block())
        v3 = lambda ap: ap.rearrange("p (c b) -> p c b", b=B)
        xv = xs[:, 0:NC * B * T].rearrange("p (c b t) -> p c b t", c=NC, b=B)
        def drive(t):
            return xs[:, bass.ds(t, NC * B * T)].rearrange("p (c b t) -> p c b t", c=NC, b=B)[:, :, :, 0]
        coefs = linear_terms()

        def walk(eng, before, step, after):
            with eng.Fori(0, G // 2) as i:
                for u in range(2):
                    step(None, i, u, 2 * i + u, True, False)
            with eng.Fori(0, NG - 1) as seg:
                before(seg)
                for u in range(2):
                    step(seg, 0, u, G + seg * G + u, True, True)
                with eng.Fori(1, G // 2) as i:
                    for u in range(2):
                        step(seg, i, u, G + seg * G + 2 * i + u, True, True)
                after(seg)
            before(NG - 1)
            for u in range(2):
                step(NG - 1, 0, u, None, False, True)
            with eng.Fori(1, G // 2) as i:
                for u in range(2):
                    step(NG - 1, i, u, None, False, True)
            after(NG - 1)

        def is_first(i, u):
            return isinstance(i, int) and i == 0 and u == 0

        def gate_row(i, u):
            return (i * 3) // 32 if u else (i * 3 - 3) // 32

        @block.sync
        def _(sp):
            sp.dma_start(cT[:], dram["coupling"]).then_inc(S["cin"], 16)
            sp.dma_start(b_scan[:], dram["b_scan"]).then_inc(S["vin"], 16)
            sp.dma_start(wr[:], dram["w_router"]).then_inc(S["vin"], 16)
            sp.dma_start(state[0][:], dram["cond"]).then_inc(S["vin"], 16)
            sp.dma_start(qraw[:], dram["cond"]).then_inc(S["vin"], 16)

            def load(tile, slot, done):
                sp.wait_ge(S["up_done"], done)
                sp.sem_inc(S["spseq"], 1)
                sp.dma_start(wgu[:, slot].rearrange("p a c f -> p (a c f)"),
                             dram["w_tiles"][bass.ds(tile, 1), :, 0:2 * N].rearrange("o p n -> (o p) n")).then_inc(wsem[slot], 16)
                sp.wait_ge(S["dn_done"], done)
                sp.sem_inc(S["spseq"], 1)
                sp.dma_start(wd[:, slot, :],
                             dram["w_tiles"][bass.ds(tile, 1), :, 2 * N:3 * N].rearrange("o p n -> (o p) n")).then_inc(dsem[slot], 16)

            with sp.Fori(0, NG) as seg:
                done = seg * TILES + 2
                load(0, 0, done)
                load(1, 1, done - 1)
                with sp.Fori(1, G // 2) as i:
                    for u in range(2):
                        load(2 * i + u, u, done + 2 * i + u - 1)
                load(TILES - 1, 0, done + TILES - 2)
                sp.wait_ge(S["out_ready"], seg * NC + NC + 1)
                sp.sem_inc(S["spseq"], 1)
                sp.dma_start(out[:, :, bass.ds(seg * G, G), :], oo[:]).then_inc(S["stored"], 16)
            sp.wait_ge(S["stored"], 16 * (NG + 1))

        @block.gpsimd
        def _(pl):
            pl.memset(ident[:], 0.0).then_inc(S["eye"], 1)
            pl.wait_ge(S["eye"], 1)
            pl.affine_select(out=ident[:], in_=ident[:], compare_op=ALU.not_equal, fill=1.0, base=0,
                             pattern=[[-1, P]], channel_multiplier=1).then_inc(S["eye"], 1)
            for e in range(E1):
                pl.memset(lanes[:, e:e + 1], float(e))
            for r in range(5):
                for tile, col in ((cq, 0), (cp, 1), (cd, 2)):
                    pl.memset(tile[:, r, :], float(coefs[r, col]))
                if r >= 2:
                    pl.memset(c2[:, r - 2, :], float(coefs[r, 3]))
                if r >= 3:
                    pl.memset(c3[:, r - 3, :], float(coefs[r, 4]))
                    pl.memset(c4[:, r - 3, :], float(coefs[r, 5]))
            pl.memset(xs[:, NC * B * T:], 0.0)
            pl.memset(zeros[:], 0.0).then_inc(S["coef"], 1)
            pl.wait_ge(S["mx"], 1)
            pl.partition_all_reduce(kp[:, 1:2], kp[:, 0:1], P, bass.bass_isa.ReduceOp.max).then_inc(S["par"], 1)
            pl.wait_ge(S["coef"], 1)
            rows = lambda ap, n: ap.unsqueeze(1).to_broadcast([P, n, W])
            K = 7

            def next_linear(t, u, k, at, pclips):
                dv = drive(t).unsqueeze(1).to_broadcast([P, 5, NC, B])
                pl.tensor_tensor(md[:].rearrange("p r (c b) -> p r c b", b=B), dv, cd[:].rearrange("p r (c b) -> p r c b", b=B), ALU.mult).then_inc(S["pchain"], 1)
                pl.wait_ge(S["pclip_ready"], pclips)
                pl.tensor_tensor(mp_[:], rows(pst[:], 5), cp[:], ALU.mult).then_inc(S["pchain"], 1)
                pl.wait_ge(S["pchain"], at + k + 2)
                pl.tensor_tensor(A[u][:], md[:], mp_[:], ALU.add).then_inc(S["lin_ready"], 1)
                pl.wait_ge(S["lin_ready"], t + 1)
                pl.sem_inc(S["plseq"], 1)
            next_linear(0, 0, 0, 0, 1)

            def step(seg, i, u, t, scan, tile):
                if not scan:
                    return
                at = 2 + t * K
                pl.wait_ge(S["clip_ready"], t + 1)
                pl.tensor_tensor(mq[:], rows(state[0][:], 4), cq[:, 1:5, :], ALU.mult).then_inc(S["pchain"], 1)
                pl.wait_ge(S["pchain"], at + 1)
                pl.tensor_tensor(A[u][:, 1:5, :], A[u][:, 1:5, :], mq[:], ALU.add).then_inc(S["e_ready"], 1)
                pl.wait_ge(S["q_ready"], t * 4 + 2)
                pl.tensor_tensor(ms[:], rows(state[1][:], 3), c2[:], ALU.mult).then_inc(S["pchain"], 1)
                pl.wait_ge(S["e_ready"], t * 3 + 1)
                pl.sem_inc(S["plseq"], 1)
                pl.wait_ge(S["pchain"], at + 2)
                pl.tensor_tensor(A[u][:, 2:5, :], A[u][:, 2:5, :], ms[:], ALU.add).then_inc(S["e_ready"], 1)
                pl.wait_ge(S["q_ready"], t * 4 + 3)
                pl.tensor_tensor(ms3[:], rows(state[2][:], 2), c3[:], ALU.mult).then_inc(S["pchain"], 1)
                pl.wait_ge(S["e_ready"], t * 3 + 2)
                pl.sem_inc(S["plseq"], 1)
                pl.wait_ge(S["pchain"], at + 3)
                pl.tensor_tensor(A[u][:, 3:5, :], A[u][:, 3:5, :], ms3[:], ALU.add).then_inc(S["pchain"], 1)
                pl.wait_ge(S["q_ready"], t * 4 + 4)
                pl.sem_inc(S["plseq"], 1)
                pl.wait_ge(S["pchain"], at + 4)
                pl.tensor_tensor(ms4[:], rows(state[3][:], 2), c4[:], ALU.mult).then_inc(S["pchain"], 1)
                pl.wait_ge(S["pchain"], at + 5)
                pl.tensor_tensor(A[u][:, 3:5, :], A[u][:, 3:5, :], ms4[:], ALU.add).then_inc(S["e_ready"], 1)
                pl.wait_ge(S["e_ready"], t * 3 + 3)
                pl.sem_inc(S["plseq"], 1)
                next_linear(t + 1, 1 - u, 5, at, t + 2)
            walk(pl, lambda seg: None, step, lambda seg: None)

        @block.scalar
        def _(act):
            act.wait_ge(S["scale_rdy"], 1)
            nc.scalar.preload_act_table_set("exp_and_others")

            def step(seg, i, u, t, scan, tile):
                for s in range(4):
                    if scan:
                        src = qraw if s == 0 else state[s]
                        act.wait_ge(S["q_ready"], t * 4 + s + 1)
                        act.activation(th[:, :, 0, :], v3(src[:]), ACT.Tanh).then_inc(S["th_ready"], 1)
                        act.activation(t32[:], src[:], ACT.Tanh).then_inc(S["t32_ready"], 1)
                        if s == 0:
                            act.wait_ge(S["clip_ready"], t + 1)
                        act.activation(sq[:], state[s][:], ACT.Square).then_inc(S["sq_ready"], 1)
                    if tile and s == 2:
                        silu(seg * TILES + 2 * i + u)

            def silu(n):
                act.wait_ge(S["gate_done"], n + 1)
                act.activation(sg[:], pg[:, 0:GT], ACT.Tanh, scale=0.5).then_inc(S["sg_ready"], 1)

            def before(seg):
                act.wait_ge(S["traced"], seg * G + G)
                act.wait_ge(S["up_done"], seg * TILES + 2)
                act.activation(qg[:], trace[:].rearrange("p c t b -> p c (t b)"), ACT.Copy).then_inc(S["copied"], 1)
                act.wait_ge(S["rt_max"], seg + 1)
                for c in range(2):
                    act.activation(ex[:, c, 0:E1], rt[:, c, 0:E1], ACT.Exp, bias=neg[:, c:c + 1], accum_out=es[:, c, 0:1])
                    ins = act.activation(ex[:, c, E1:E1 + 1], rt[:, c, E1:E1 + 1], ACT.Exp, scale=-1.0)
                ins.then_inc(S["rt_exp"], 1)
            walk(act, before, step, lambda seg: silu(seg * TILES + TILES - 1))

        @block.tensor
        def _(pe):
            mm = nc.tensor.matmul
            pe.wait_ge(S["eye"], 2)
            pe.wait_ge(S["vin"], 64)
            pe.wait_ge(S["scale_rdy"], 1)
            pe.wait_ge(S["coef"], 1)
            pe.sem_inc(S["up_done"], 2)
            pe.sem_inc(S["dn_done"], 2)

            def gate(slot, n, ks):
                if 0 in ks:
                    pe.wait_ge(wsem[slot], 16 * loads(slot, n))
                    pe.wait_ge(S["ha_ready"], n[0] * TILES + n[1] + 1)
                for k in ks:
                    ins = mm(pg[:, 0:GT], wgu[:, slot, 0, k, :], qg[:, k, :], start=(k == 0), stop=(k == NC - 1))
                if NC - 1 in ks:
                    ins.then_inc(S["gate_done"], 1)

            def up(slot, n, ks):
                if 0 in ks:
                    pe.wait_ge(S["hb_ready"], n[0] * TILES + n[1] + 1)
                for k in ks:
                    ins = mm(pu[:, 0:GT], wgu[:, slot, 1, k, :], qg[:, k, :], start=(k == 0), stop=(k == NC - 1))
                if NC - 1 in ks:
                    ins.then_inc(S["up_done"], 1)

            def down(slot, seg, j, dloads, ms_):
                if 0 in ms_:
                    pe.wait_ge(S["hid_ready"], seg * TILES + j + 1)
                    pe.wait_ge(dsem[slot], dloads)
                for m in ms_:
                    ins = mm(pd[m // 2][:, (m % 2) * GT:(m % 2 + 1) * GT], wd[:, slot, m * P:(m + 1) * P], hg[:, slot, :],
                             start=False, stop=False, skip_group_check=True)
                if NC - 1 in ms_:
                    ins.then_inc(S["dn_done"], 1)

            def loads(slot, n):
                seg, i = n[0], n[2]
                return seg * (17 if slot == 0 else 16) + i + 1

            def down_loads(u, seg, i):
                return 16 * (seg * 17 + i + 1) if u else 16 * (seg * 16 + i)

            def step(seg, i, u, t, scan, tile):
                if tile:
                    n = (seg, 2 * i + u, i)
                    dl = down_loads(u, seg, i)
                    before_it = lambda ms_: None if is_first(i, u) else down(1 - u, seg, 2 * i + u - 1, dl, ms_)
                    slots = [lambda: gate(u, n, [0, 1, 2]),
                             lambda: (gate(u, n, [3]), up(u, n, [0, 1])),
                             lambda: (up(u, n, [2, 3]), before_it([0])),
                             lambda: before_it([1, 2, 3])]
                for s in range(4):
                    if scan:
                        pe.wait_ge(S["th_ready"], t * 4 + s + 1)
                        for m in range(NC):
                            for k in range(NC):
                                mm(pscan[:, m, 0, :], clo[:, k, m * P:(m + 1) * P], th[:, k, 0, :], start=(m == 0 and k == 0), stop=False, skip_group_check=True)
                        pe.wait_ge(S["tl_ready"], t * 4 + s + 1)
                        for m in range(NC):
                            for k in range(NC):
                                ins = mm(pscan[:, m].rearrange("p a b -> p (a b)"), chi[:, k, m * P:(m + 1) * P], th[:, k].rearrange("p a b -> p (a b)"),
                                         start=False, stop=(k == NC - 1), skip_group_check=True)
                        ins.then_inc(S["ic_ready"], 1)
                    if tile:
                        slots[s]()

            def before(seg):
                pe.wait_ge(S["copied"], seg + 1)
                for c in range(2):
                    for k in range(NC):
                        ins = mm(pr_[:, 16 * c:16 * c + E1 + 1], qg[:, k, c * P:(c + 1) * P], wr[:, k, :], start=(k == 0), stop=(k == NC - 1))
                ins.then_inc(S["rt_mm"], 1)
                pe.wait_ge(S["out_ready"], seg * NC + 1)
                for i in range(2):
                    mm(pd[i][:], zeros[:, 0:P], zeros[:], start=True, stop=False, skip_group_check=True)
                pe.wait_ge(S["rt_wide"], seg + 1)
                for r in range(2):
                    for c in range(2):
                        ins = nc.tensor.transpose(pr_[:, r * GT + c * P:r * GT + (c + 1) * P], wide[:, c, r, :], ident[:])
                ins.then_inc(S["rt_tr"], 1)

            def after(seg):
                n = (seg, TILES - 1, 16)
                gate(0, n, [0, 1, 2, 3])
                up(0, n, [0, 1, 2, 3])
                down(1, seg, TILES - 2, down_loads(0, seg, 16), [0, 1, 2, 3])
                down(0, seg, TILES - 1, down_loads(1, seg, 16), [0, 1, 2, 3])
            walk(pe, before, step, after)

        @block.vector
        def _(dve):
            setup = [0]
            def link(ins):
                setup[0] += 1
                ins.then_inc(S["rchain"], 1)
                dve.wait_ge(S["rchain"], setup[0])
            dve.wait_ge(S["cin"], 16)
            dve.tensor_reduce(kp[:, 0:1], cT[:].rearrange("p c n -> p (c n)"), AX.X, ALU.max, apply_absolute_value=True).then_inc(S["mx"], 1)
            dve.wait_ge(S["par"], 1)
            link(dve.tensor_scalar(kp[:, 1:2], kp[:, 1:2], 2.0 ** -100, None, ALU.max))
            ki = kp[:].bitcast(I32)
            link(dve.tensor_scalar(ki[:, 2:3], ki[:, 1:2], 0x7F800000, None, ALU.bitwise_and))
            link(dve.reciprocal(kp[:, 3:4], kp[:, 2:3]))
            link(dve.tensor_scalar(kp[:, 3:4], kp[:, 3:4], SHIFT, None, ALU.mult))
            for s in range(4):
                link(dve.tensor_scalar(kp[:, 4 + s:5 + s], kp[:, 2:3], RK[s] / SHIFT, None, ALU.mult))
            link(dve.tensor_scalar(chi[:], cT[:], kp[:, 3:4], None, ALU.mult))
            link(dve.scalar_tensor_tensor(clo[:], cT[:], kp[:, 3:4], chi[:], ALU.mult, ALU.subtract))
            dve.wait_ge(S["vin"], 64)
            link(dve.tensor_scalar(unshift[:], b_scan[:], -1.0, ALPHA / BETA, ALU.mult, ALU.add))
            dve.tensor_scalar(pst[:], state[0][:], BETA, ALPHA, ALU.mult, ALU.subtract).then_inc(S["pclip_ready"], 1)
            dve.sem_inc(S["scale_rdy"], 1)
            dve.sem_inc(S["q_ready"], 1)
            dve.sem_inc(S["clip_ready"], 1)
            dve.sem_inc(S["ha_ready"], 1)
            dve.sem_inc(S["hb_ready"], 1)
            dve.sem_inc(S["out_ready"], 1)
            dve.sem_inc(S["stored"], 16)
            K = 13

            def step(seg, i, u, t, scan, tile):
                k = [0]
                def chain(ins):
                    k[0] += 1
                    ins.then_inc(S["dchain"], 1)
                    dve.wait_ge(S["dchain"], t * K + k[0])
                for s in range(4):
                    bulk = tile and not is_first(i, u)
                    if bulk and not scan and s < 2:
                        (hidden_up, hidden_gate)[s](seg, 2 * i + u - 1, 1 - u, gate_row(i, u))
                    if scan:
                        nxt = state[s + 1] if s < 3 else qraw
                        dve.wait_ge(S["t32_ready"], t * 4 + s + 1)
                        dve.tensor_tensor(th[:, :, 1, :], v3(t32[:]), th[:, :, 0, :], ALU.subtract).then_inc(S["tl_ready"], 1)
                        dve.wait_ge(S["sq_ready"], t * 4 + s + 1)
                        chain(dve.scalar_tensor_tensor(cub[:], sq[:], -3.0, state[s][:], ALU.add, ALU.mult))
                        if s == 0:
                            chain(dve.scalar_tensor_tensor(base[:], cub[:], -RK[s] / 3, state[0][:], ALU.mult, ALU.add))
                            dve.wait_ge(S["lin_ready"], t + 1)
                            chain(dve.tensor_tensor(base[:], base[:], A[u][:, 0, :], ALU.add))
                            if bulk:
                                hidden_up(seg, 2 * i + u - 1, 1 - u, None)
                        else:
                            if bulk and s == 1:
                                hidden_gate(seg, 2 * i + u - 1, 1 - u, gate_row(i, u))
                            dve.wait_ge(S["e_ready"], t * 3 + s)
                            chain(dve.scalar_tensor_tensor(base[:], cub[:], -RK[s] / 3, A[u][:, s, :], ALU.mult, ALU.add))
                        if s == 3:
                            dve.tensor_scalar(pst[:], A[u][:, 4, :], BETA * CLAMP - ALPHA, -BETA * CLAMP - ALPHA, ALU.min, ALU.max).then_inc(S["pclip_ready"], 1)
                        dve.wait_ge(S["ic_ready"], t * 4 + s + 1)
                        chain(dve.scalar_tensor_tensor(v3(part[:]), pscan[:, :, 1, :], kp[:, 4 + s:5 + s], v3(base[:]), ALU.mult, ALU.add))
                        dve.scalar_tensor_tensor(v3(nxt[:]), pscan[:, :, 0, :], kp[:, 4 + s:5 + s], v3(part[:]), ALU.mult, ALU.add).then_inc(S["q_ready"], 1)
                        if s == 3:
                            dve.wait_ge(S["q_ready"], t * 4 + 5)
                            dve.tensor_scalar(state[0][:], qraw[:], CLAMP, -CLAMP, ALU.min, ALU.max).then_inc(S["clip_ready"], 1)
                            dve.tensor_scalar(trace[:, :, bass.ds(2 * i + u, 1), :].rearrange("p c o b -> p c (o b)"), v3(qraw[:]), CLAMP, -CLAMP, ALU.min, ALU.max).then_inc(S["traced"], 1)
                    if tile and s == 2:
                        act_gate(seg * TILES + 2 * i + u)

            def act_gate(n):
                dve.wait_ge(S["sg_ready"], n + 1)
                dve.scalar_tensor_tensor(ha[:], sg[:], 1.0, pg[:, 0:GT], ALU.add, ALU.mult).then_inc(S["ha_ready"], 1)

            def hidden_up(seg, j, slot, row):
                n = seg * TILES + j
                dve.wait_ge(S["up_done"], n + 3)
                dve.wait_ge(S["ha_ready"], n + 2)
                dve.tensor_tensor(hb[:], ha[:], pu[:, 0:GT], ALU.mult).then_inc(S["hb_ready"], 1)

            def hidden_gate(seg, j, slot, row):
                n = seg * TILES + j
                dve.wait_ge(S["hb_ready"], n + 2)
                dve.wait_ge(S["dn_done"], n + 2 if isinstance(j, int) and j == 0 else n + 1)
                g = gates[:, bass.ds(row, 1), :].rearrange("p o t -> p (o t)") if not isinstance(row, int) else gates[:, row, :]
                dve.tensor_tensor(hg[:, slot, :], hb[:], g, ALU.mult).then_inc(S["hid_ready"], 1)

            RL = 10
            def before(seg):
                k = [0]
                base_ = setup[0]
                def chain(ins, wait=True):
                    k[0] += 1
                    ins.then_inc(S["rchain"], 1)
                    if wait:
                        dve.wait_ge(S["rchain"], base_ + seg * RL + k[0])
                dve.wait_ge(S["copied"], seg + 1)
                dve.wait_ge(S["rt_mm"], seg + 1)
                chain(dve.tensor_copy(rt[:], pr_[:, 0:32].rearrange("p (c e) -> p c e", c=2)[:, :, 0:E1 + 1]))
                dve.sem_inc(S["dveseq"], 1)
                for c in range(2):
                    ins = dve.max(top[:, c, :], rt[:, c, 0:E1])
                chain(ins)
                dve.sem_inc(S["dveseq"], 1)
                for c in range(2):
                    dve.max_index(topi[:, c, :], top[:, c, :], rt[:, c, 0:E1])
                dve.tensor_scalar(neg[:], top[:, :, 0:1].rearrange("p c o -> p (c o)"), -1.0, None, ALU.mult).then_inc(S["rt_max"], 1)
                dve.wait_ge(S["rt_max"], seg + 1)
                chain(dve.tensor_copy(topf[:], topi[:]))
                for c in range(2):
                    ins = dve.tensor_scalar(msk[:, c, 0, :], lanes[:], topf[:, c, 0:1], None, ALU.is_equal)
                chain(ins)
                for c in range(2):
                    ins = dve.scalar_tensor_tensor(msk[:, c, 1, :], lanes[:], topf[:, c, 1:2], msk[:, c, 0, :], ALU.is_equal, ALU.add)
                chain(ins)
                dve.wait_ge(S["rt_exp"], seg + 1)
                chain(dve.tensor_scalar(es[:, :, 1:2], es[:, :, 0:1], 2.0, None, ALU.mult), False)
                chain(dve.tensor_scalar(es[:, :, 2:3], ex[:, :, E1:E1 + 1], 1.0, 2.0, ALU.add, ALU.mult))
                chain(dve.reciprocal(es[:, :, 1:3], es[:, :, 1:3]))
                for c in range(2):
                    ins = dve.scalar_tensor_tensor(msk[:, c, 0, :], msk[:, c, 1, :], es[:, c, 1:2], ex[:, c, 0:E1], ALU.mult, ALU.mult)
                chain(ins)
                for c in range(2):
                    dve.tensor_copy(wide[:, c, 0, :].rearrange("p (e r) -> p e r", r=LANES), msk[:, c, 0, :].unsqueeze(2).to_broadcast([P, E1, LANES]))
                    ins = dve.tensor_copy(wide[:, c, 1, :], es[:, c, 2:3].to_broadcast([P, P]))
                ins.then_inc(S["rt_wide"], 1)
                dve.wait_ge(S["rt_tr"], seg + 1)
                chain(dve.tensor_copy(gates[:].rearrange("p a t -> p (a t)"), pr_[:]))
                dve.sem_inc(S["dveseq"], 1)
                assert k[0] == RL, k

            def after(seg):
                hidden_up(seg, TILES - 2, 1, 1)
                hidden_gate(seg, TILES - 2, 1, 1)
                act_gate(seg * TILES + TILES - 1)
                hidden_up(seg, TILES - 1, 0, 1)
                hidden_gate(seg, TILES - 1, 0, 1)
                dve.wait_ge(S["dn_done"], seg * TILES + TILES + 2)
                dve.wait_ge(S["stored"], 16 * seg + 16)
                for c in range(NC):
                    dve.scalar_tensor_tensor(oo[:, c], pd[c // 2][:, (c % 2) * GT:(c % 2 + 1) * GT].rearrange("p (t b) -> p t b", b=B), unshift[:, c:c + 1],
                                             xv[:, c, :, bass.ds(seg * G, G)].rearrange("p b t -> p t b"), ALU.add, ALU.add).then_inc(S["out_ready"], 1)
            walk(dve, before, step, after)


def build(nc, dram, out):
    with nc.sbuf_tensor("xs", [P, NC * B * T + T], F32) as xs:
        layer0(nc, dram, xs)
        layer1(nc, dram, xs, out)


def arranged(inputs, np):
    g = lambda n: np.asarray(inputs[n])
    rows = lambda a: a.reshape(a.shape[0] // P, P, *a.shape[1:])
    part = lambda a: np.moveaxis(rows(a), 0, 1)
    up_q, dn_q = g("L0_ffn_w_up_q").T, g("L0_ffn_w_down_q").T
    a = {
        "x": np.ascontiguousarray(part(g("x").transpose(2, 0, 1))),
        "w_emb": part(g("L0_cond_W_emb")), "w_qkv": part(g("L0_cond_W_qkv")), "w_out": part(g("L0_cond_W_out")),
        "up_q": part(up_q), "dn_q": part(dn_q), "up_s": g("L0_ffn_w_up_scale").T, "dn_s": g("L0_ffn_w_down_scale").T,
        "lora_a": np.concatenate([g("L0_ffn_w_up_lora_a").T, g("L0_ffn_w_down_lora_a").T], 1),
        "lora_b": np.concatenate([g("L0_ffn_w_up_lora_b"), g("L0_ffn_w_down_lora_b")], 1),
        "vecs": np.concatenate([part(g("cond_2048").T).reshape(P, NC * B), part(g("L0_cond_b_emb")), part(g("L0_cond_g_norm")),
                                part(g("L0_ffn_b_up")), np.tile(g("L0_cond_g_q"), HPC)[:, None], np.tile(g("L0_cond_g_k"), HPC)[:, None]], 1),
        "b_dn": part(g("L0_ffn_b_down")), "b_scan": part(g("L1_cond_bias")),
    }
    def columns(e, s):
        mixed = g(e).reshape(E1, N, TE, LANES).transpose(2, 1, 0, 3).reshape(TE, NC, P, P)
        shared = g(s).reshape(NC, P, TS, P).transpose(2, 0, 1, 3)
        return np.concatenate([mixed, shared], 0).transpose(0, 2, 1, 3).reshape(TILES, P, N)
    down = np.concatenate([g("L1_ffn_Wd").reshape(E1, TE, LANES, N).transpose(1, 0, 2, 3).reshape(TE, P, N), g("L1_ffn_Sd").reshape(TS, P, N)], 0)
    a["w_tiles"] = np.concatenate([columns("L1_ffn_Wg", "L1_ffn_Sg"), columns("L1_ffn_Wu", "L1_ffn_Su"), down], 2)
    a["coupling"] = part(g("L1_cond_coupling").T)
    a["cond"] = part(g("cond_2048").T).reshape(P, W)
    a["w_router"] = part(np.concatenate([g("L1_ffn_Wr"), g("L1_ffn_Wsg")], 1))
    return {k: np.ascontiguousarray(v) for k, v in a.items()}


def kernel(**inputs):
    import numpy as _np
    import concourse.bacc as _bacc
    from concourse import mybir as _mybir
    from concourse.bass_utils import run_bass_kernel_spmd as _run

    nc = _bacc.Bacc("TRN2", target_bir_lowering=False, num_devices=1)
    arrays, dram = {}, {}
    for name, a in arranged(inputs, _np).items():
        arrays[f"in_{name}"] = a
        dram[name] = nc.dram_tensor(f"in_{name}", a.shape, _mybir.dt.from_np(a.dtype), kind="ExternalInput").ap()
    out = nc.dram_tensor("out", (P, NC, T, B), _mybir.dt.float32, kind="ExternalOutput").ap()
    build(nc, dram, out)
    r = _run(nc, [arrays], core_ids=[0])
    return r.results[0]["out"].transpose(3, 2, 1, 0).reshape(B, T, N)
```

```python
import concourse.bass as bass
from concourse import mybir
from contextlib import ExitStack

F32, F16, BF16, I32 = mybir.dt.float32, mybir.dt.float16, mybir.dt.bfloat16, mybir.dt.int32
ALU = mybir.AluOpType
ACT = mybir.ActivationFunctionType
AX = mybir.AxisListType
P = 128

E1, F1, FS = 8, 352, 1408
LANES = P // E1
TE = F1 // LANES
TS = FS // P
TILES = TE + TS
Q_BITS = 8
B, T, N = 8, 256, 512
NC = N // P
HEADS, DH = 16, 32
HPC = P // DH
H0 = 2048
HC = H0 // P
QBLOCK = 64
R = 16
PIECE = 1024
PIECES = 2 * NC * H0 // PIECE
DT, EPSILON, ALPHA, BETA, CLAMP = 0.01, 0.08, 0.7, 0.8, 20.0


def layer0(nc, dram, xs, wk, w_split):
    ctx = ExitStack()
    with ctx:
        sb = lambda n, s, d=F32: ctx.enter_context(nc.sbuf_tensor(n, s, d))
        sem = lambda n: ctx.enter_context(nc.semaphore(n))
        w_emb = sb("w_emb", [P, NC, 2 * N])
        early = w_emb[:].rearrange("p c n -> p (c n)")
        qk = early[:, 0:2 * NC * T].rearrange("p (c a t) -> p c a t", a=2, t=T)
        pr = early[:, 2048:3072].rearrange("p (u a t) -> p u a t", u=2, a=2)
        prT = early[:, 3072:4096].rearrange("p (u a t) -> p u a t", u=2, a=2)
        w_qkv = sb("w_qkv", [P, NC, 3 * N])
        w_out = sb("w_out", [P, NC, N])
        w_up = sb("w_up", [P, NC, H0])
        w_dn = sb("w_dn", [P, HC, N])
        hid = sb("hid", [P, HC, T])
        staging = hid[:].rearrange("p a t -> p (a t)")
        codes = [staging[:, u * 2048:u * 2048 + PIECE].bitcast(I32) for u in range(2)]
        scales = [staging[:, u * 2048 + PIECE:u * 2048 + 2 * PIECE] for u in range(2)]
        work = sb("work", [P, 5 * NC * T])
        sq = work[:, 0:1024].rearrange("p (c t) -> p c t", c=NC)
        xn = work[:, 1024:2048].rearrange("p (c t) -> p c t", c=NC)
        sqh = work[:, 2048:3072].rearrange("p (u a t) -> p u a t", u=2, a=2)
        rh = work[:, 3072:4096].rearrange("p (u a t) -> p u a t", u=2, a=2)
        v = work[:, 4096:5120].rearrange("p (a n) -> p a n", a=2)
        vecs = sb("vecs", [P, 64])
        condT = vecs[:, 0:NC * B].rearrange("p (c b) -> p c b", b=B)
        b_emb, g_norm = vecs[:, 32:40], vecs[:, 40:44]
        b_up, b_dn, b_scan, g_q, g_k = vecs[:, 44:60], sb("b_dn", [P, NC]), sb("b_scan", [P, NC]), vecs[:, 60:61], vecs[:, 61:62]
        eps = vecs[:, 62:63]
        ones = sb("ones", [P, P])
        headones = sb("headones", [P, P])
        ident = sb("ident", [P, P])
        ss = sb("ss", [P, 2 * NC, B])
        amp = sb("amp", [P, NC, B])
        bias2 = sb("bias2", [P, NC])
        rs = sb("rs", [P, 2, T])
        nmax = sb("nmax", [P, 2, 2])
        psum_e = sb("psum_e", [P, HEADS, 2])
        rinv = sb("rinv", [P, HEADS, 2])
        late = sb("late", [P, 3 * NC * T])
        o = late[:, 0:1024].rearrange("p (a n) -> p a n", a=2)
        oT = late[:, 1024:2048].rearrange("p (c t) -> p c t", c=NC)
        x1 = late[:, 2048:3072].rearrange("p (c t) -> p c t", c=NC)
        lora_up, lora_dn = late[0:R, 0:N + H0], late[32:32 + R, 0:N + H0]
        half_in = [sb(f"half_in{a}", [P, N]) for a in range(2)]
        half_out = [sb(f"half_out{a}", [P, 2, N], F16) for a in range(2)]
        bank = [ctx.enter_context(nc.psum_tensor(f"l0bank{i}", [P, 512], F32)) for i in range(8)]
        G, Rb, Ob, D = bank[0:2], bank[2:4], bank[4:6], bank[6:8]
        names = ("x_in xs_in emb_in qkv_in codes0 codes1 lora vec_in eye mm_ss mm_lora a_sqx a_rstd a_sq a_hr a_v a_exp a_up "
                 "p_nrm p_qk p_hr p_v p_s p_t p_pv p_ot p_wo p_up p_dn d_xn d_qk d_max d_pt d_o d_ot d_x1 d_x2 chain achain amps gch wo_in stage scaled half_in0 half_in1 half_out0 half_out1 half_read half_split gmax seq plseq plmul summed").split()
        S = {n: sem("l0_" + n) for n in names}
        block = ctx.enter_context(nc.Block())
        xv = xs[:, 0:NC * B * T].rearrange("p (c b t) -> p c b t", c=NC, b=B)
        codes_in = [S["codes0"], S["codes1"]]
        half_loaded, half_stored = [S["half_in0"], S["half_in1"]], [S["half_out0"], S["half_out1"]]
        RELUS = HC // 2

        def ffn_schedule():
            heads, n = [], 4
            for h in range(HEADS):
                k = 2 if h < 12 else 1
                heads.append(list(range(n, n + k)))
                n += k
            assert n == 2 * HC
            return [0, 1], [2, 3], heads
        ffn_first, ffn_second, ffn_heads = ffn_schedule()

        @block.sync
        def _(sp):
            sp.dma_start(vecs[:, 0:62], dram["vecs"]).then_inc(S["vec_in"], 16)
            sp.dma_start(b_dn[:], dram["b_dn"]).then_inc(S["vec_in"], 16)
            sp.dma_start(b_scan[:], dram["b_scan"]).then_inc(S["vec_in"], 16)
            sp.dma_start(w_emb[:], dram["w_emb"]).then_inc(S["emb_in"], 16)
            for half, factors in enumerate((lora_up, lora_dn)):
                sp.dma_start(factors, dram["lora"][half]).then_inc(S["lora"], 16)
            for h in range(PIECES):
                u = h % 2
                if h >= 2:
                    sp.wait_ge(S["stage"], h - 1)
                if h < PIECES // 2:
                    cols = slice(h % 2 * PIECE, h % 2 * PIECE + PIECE)
                    sp.dma_start(codes[u], dram["up_q"][:, h // 2, cols]).then_inc(codes_in[u], 16)
                    for half in range(2):
                        sp.dma_start(scales[u][half * 64:half * 64 + 64, :],
                                     dram["up_s"][2 * (h // 2) + half, cols].partition_broadcast(64)).then_inc(codes_in[u], 16)
                else:
                    hc = 2 * (h - PIECES // 2)
                    sp.dma_start(codes[u], dram["dn_q"][:, hc:hc + 2, :].rearrange("p a n -> p (a n)")).then_inc(codes_in[u], 16)
                    for a in range(2):
                        for half in range(2):
                            sp.dma_start(scales[u][half * 64:half * 64 + 64, a * N:(a + 1) * N],
                                         dram["dn_s"][2 * (hc + a) + half].partition_broadcast(64)).then_inc(codes_in[u], 16)
                if h == 3:
                    sp.dma_start(w_out[:], dram["w_out"]).then_inc(S["wo_in"], 16)

            def load_half(tile, a, reads):
                sp.wait_ge(S["half_read"], reads)
                sp.sem_inc(S["seq"], 1)
                sp.dma_start(half_in[a][:], dram["w_tiles"][bass.ds(tile, 1), :, a * N:(a + 1) * N].rearrange("o p n -> (o p) n")).then_inc(half_loaded[a], 16)
            with sp.Fori(0, TILES) as tile:
                for a in range(2):
                    load_half(tile, a, 2 * tile + a + 1)
            with sp.Fori(0, TILES) as tile:
                for a in range(2):
                    load_half(tile, a, 2 * TILES + 2 * tile + a + 1)
                for a in range(2):
                    sp.wait_ge(S["half_split"], 2 * tile + a + 1)
                    sp.sem_inc(S["seq"], 1)
                    sp.dma_start(w_split[bass.ds(tile, 1), :, a * 2 * N:(a + 1) * 2 * N].rearrange("o p n -> (o p) n"),
                                 half_out[a][:].rearrange("p h n -> p (h n)")).then_inc(half_stored[a], 16)
            for a in range(2):
                sp.wait_ge(half_stored[a], 16 * TILES + 16)

        @block.gpsimd
        def _(pl):
            pl.sem_inc(S["half_read"], 2)
            for a in range(2):
                pl.sem_inc(half_stored[a], 16)
            pl.memset(ones[:], 1.0).then_inc(S["gch"], 1)
            pl.memset(ident[:], 0.0).then_inc(S["gch"], 1)
            pl.memset(headones[:], 1.0).then_inc(S["gch"], 1)
            pl.memset(eps, 1e-6).then_inc(S["gch"], 1)
            pl.wait_ge(S["gch"], 4)
            pl.affine_select(out=ident[:], in_=ident[:], compare_op=ALU.not_equal, fill=1.0, base=0,
                             pattern=[[-1, P]], channel_multiplier=1).then_inc(S["gch"], 1)
            hv = headones[:].rearrange("p (h d) -> p h d", d=DH)
            pl.affine_select(out=hv, in_=hv, compare_op=ALU.is_ge, fill=0.0, base=0,
                             pattern=[[-DH, HPC], [0, DH]], channel_multiplier=1).then_inc(S["gch"], 1)
            pl.wait_ge(S["gch"], 6)
            pl.affine_select(out=hv, in_=hv, compare_op=ALU.is_ge, fill=0.0, base=DH - 1,
                             pattern=[[DH, HPC], [0, DH]], channel_multiplier=-1).then_inc(S["eye"], 1)
            bound, size = half_out[0][:].rearrange("p h n -> p (h n)").bitcast(F32), half_out[1][:].rearrange("p h n -> p (h n)").bitcast(F32)
            pl.memset(bound, 0.0).then_inc(S["summed"], 1)
            with pl.Fori(0, TILES) as tile:
                for a in range(2):
                    n = 2 * tile + a
                    pl.wait_ge(half_loaded[a], 16 * tile + 16)
                    pl.wait_ge(S["summed"], n + 1)
                    pl.sem_inc(S["plseq"], 1)
                    pl.tensor_scalar(size, half_in[a][:], 0.0, 2.0, ALU.max, ALU.mult).then_inc(S["plmul"], 1)
                    pl.wait_ge(S["plmul"], n + 1)
                    pl.tensor_tensor(size, size, half_in[a][:], ALU.subtract).then_inc(S["half_read"], 1)
                    pl.wait_ge(S["half_read"], n + 3)
                    pl.tensor_tensor(bound, bound, size, ALU.add).then_inc(S["summed"], 1)
            pl.wait_ge(S["summed"], 2 * TILES + 1)
            steps = [0]
            def link(ins):
                steps[0] += 1
                ins.then_inc(S["gmax"], 1)
                pl.wait_ge(S["gmax"], steps[0])
            width = N // 2
            while width >= 1:
                one, other = bound[:, 0:width], bound[:, width:2 * width]
                link(pl.tensor_tensor(one, one, other, ALU.subtract))
                link(pl.tensor_scalar(one, one, 0.0, None, ALU.max))
                link(pl.tensor_tensor(one, one, other, ALU.add))
                width //= 2
            link(pl.tensor_copy(wk[:, 2:3], bound[:, 0:1]))
            link(pl.partition_all_reduce(wk[:, 2:3], wk[:, 2:3], P, bass.bass_isa.ReduceOp.max))
            link(pl.tensor_scalar(wk[:, 2:3], wk[:, 2:3], 2.0 ** -100, None, ALU.max))
            ki = wk[:].bitcast(I32)
            link(pl.tensor_scalar(ki[:, 2:3], ki[:, 2:3], 2.0 ** -23, None, ALU.mult))
            link(pl.tensor_scalar(ki[:, 0:1], ki[:, 2:3], -2.0 ** 23, float((254 + 13) << 23), ALU.mult, ALU.add))
            link(pl.tensor_scalar(ki[:, 1:2], ki[:, 2:3], 2.0 ** 23, float((13 + Q_BITS) << 23), ALU.mult, ALU.subtract))
            with pl.Fori(0, TILES) as tile:
                for a in range(2):
                    pl.wait_ge(half_loaded[a], 16 * (TILES + tile) + 16)
                    pl.wait_ge(half_stored[a], 16 * tile + 16)
                    pl.sem_inc(S["plseq"], 1)
                    pl.tensor_scalar(half_out[a][:, 0, :], half_in[a][:], wk[:, 0:1], None, ALU.mult)
                    pl.tensor_scalar(half_in[a][:], half_in[a][:], wk[:, 0:1], None, ALU.mult).then_inc(S["plmul"], 1)
                    pl.wait_ge(S["plmul"], 2 * TILES + 2 * tile + a + 1)
                    pl.tensor_tensor(half_out[a][:, 1, :], half_in[a][:], half_out[a][:, 0, :], ALU.subtract).then_inc(S["half_split"], 1)
                    pl.wait_ge(S["half_split"], 2 * tile + a + 1)
                    pl.sem_inc(S["half_read"], 1)

        @block.scalar
        def _(act):
            act.dma_start(xv[:, :, 0, :], dram["x"][:, :, 0, :]).then_inc(S["x_in"], 16)
            act.dma_start(w_qkv[:], dram["w_qkv"]).then_inc(S["qkv_in"], 16)
            act.dma_start(xv[:, :, 1:, :], dram["x"][:, :, 1:, :]).then_inc(S["xs_in"], 16)
            act.wait_ge(S["eye"], 1)
            act.wait_ge(S["vec_in"], 48)
            act.wait_ge(S["x_in"], 16)
            nc.scalar.preload_act_table_set("natural_log_exp_and_others")
            def relu(n, j):
                act.wait_ge(S["p_up"], n * RELUS + j + 1)
                for i in range(2):
                    ins = act.activation(hid[:, 2 * j + i, :], D[j % 2][:, i * T:(i + 1) * T], ACT.Relu, bias=b_up[:, 2 * j + i:2 * j + i + 1])
                ins.then_inc(S["a_up"], 1)

            def batch(b, ffn):
                act.activation(sq[:], xv[:, :, bass.ds(b, 1), :].rearrange("p c o t -> p c (o t)"), ACT.Square).then_inc(S["a_sqx"], 1)
                act.wait_ge(S["p_nrm"], b + 1)
                act.activation(rs[:, 0, :], Rb[0][:, 0:T], ACT.Ln, scale=1.0 / N, bias=eps).then_inc(S["achain"], 1)
                act.wait_ge(S["achain"], b * 5 + 1)
                act.activation(rs[:, 1, :], rs[:, 0, :], ACT.Exp, scale=-0.5).then_inc(S["a_rstd"], 1)
                def square(c):
                    act.wait_ge(S["p_qk"], b * NC + c + 1)
                    act.activation(sqh[:, c % 2], G[c % 2][:].rearrange("p (a t) -> p a t", a=2), ACT.Square).then_inc(S["a_sq"], 1)
                square(0)
                for c in range(NC):
                    if c + 1 < NC:
                        square(c + 1)
                    act.wait_ge(S["p_hr"], b * NC + c + 1)
                    act.activation(rh[:, c % 2], Rb[c % 2][:].rearrange("p (a t) -> p a t", a=2), ACT.Ln, scale=1.0 / DH, bias=eps).then_inc(S["achain"], 1)
                    act.wait_ge(S["achain"], b * 5 + 2 + c)
                    act.activation(rh[:, c % 2], rh[:, c % 2], ACT.Exp, scale=-0.5).then_inc(S["a_hr"], 1)
                for i in range(2):
                    act.wait_ge(S["p_v"], b * 2 + i + 1)
                    act.activation(v[:, i, :], Ob[i][:], ACT.Copy).then_inc(S["a_v"], 1)
                if ffn:
                    relu(b - 1, 0)
                    relu(b - 1, 1)
                for h in range(HEADS):
                    if ffn and h:
                        for part in ffn_heads[h - 1]:
                            if part < HC and part % 2:
                                relu(b - 1, part // 2)
                    act.wait_ge(S["d_max"], b * HEADS + h + 1)
                    for qc in range(2):
                        ins = act.activation(pr[:, h % 2, qc, :], G[h % 2][:, qc * T:(qc + 1) * T], ACT.Exp,
                                             bias=nmax[:, h % 2, qc:qc + 1], accum_out=psum_e[:, h, qc:qc + 1])
                    ins.then_inc(S["a_exp"], 1)
            batch(0, False)
            act.wait_ge(S["xs_in"], 16)
            with act.Fori(1, B) as b:
                batch(b, True)
            for j in range(RELUS):
                relu(B - 1, j)

        @block.tensor
        def _(pe):
            mm = nc.tensor.matmul
            pe.wait_ge(S["emb_in"], 16)
            pe.wait_ge(S["vec_in"], 48)
            for m in range(2 * NC):
                for k in range(NC):
                    ins = mm(Ob[0][:, m * B:(m + 1) * B], w_emb[:, k, m * P:(m + 1) * P], condT[:, k, :], start=(k == 0), stop=(k == NC - 1))
            ins.then_inc(S["mm_ss"], 1)
            pe.wait_ge(S["eye"], 1)
            pe.wait_ge(S["qkv_in"], 16)
            pe.wait_ge(S["amps"], 1)

            def lora(h):
                if h == 0:
                    pe.wait_ge(S["lora"], 32)
                else:
                    pe.wait_ge(S["stage"], h)
                for i in range(2):
                    if h < PIECES // 2:
                        c, col = h // 2, N + h % 2 * PIECE + i * 512
                        a, bb = lora_up[:, c * P:(c + 1) * P], lora_up[:, col:col + 512]
                    else:
                        hc = 2 * (h - PIECES // 2) + i
                        a, bb = lora_dn[:, hc * P:(hc + 1) * P], lora_dn[:, H0:H0 + N]
                    ins = mm(D[i][:], a, bb, start=True, stop=True)
                ins.then_inc(S["mm_lora"], 1)

            def ffn_part(n, part):
                if part < HC:
                    j = part // 2
                    if part % 2 == 0 and j >= 2:
                        pe.wait_ge(S["a_up"], n * RELUS + j - 1)
                    for k in range(NC):
                        ins = mm(D[j % 2][:, (part % 2) * T:(part % 2 + 1) * T], w_up[:, k, part * P:(part + 1) * P], x1[:, k, :], start=(k == 0), stop=(k == NC - 1))
                    if part % 2:
                        ins.then_inc(S["p_up"], 1)
                else:
                    m, quarter = (part - HC) // 4, (part - HC) % 4
                    if part == HC:
                        pe.wait_ge(S["a_up"], n * RELUS + RELUS)
                    for k in range(4 * quarter, 4 * quarter + 4):
                        ins = mm(D[m // 2][:, (m % 2) * T:(m % 2 + 1) * T], w_dn[:, k, m * P:(m + 1) * P], hid[:, k, :], start=(k == 0), stop=(k == HC - 1))
                    if m % 2 and quarter == 3:
                        ins.then_inc(S["p_dn"], 1)

            def batch(b, ffn):
                if ffn:
                    for part in ffn_first:
                        ffn_part(b - 1, part)
                pe.wait_ge(S["a_sqx"], b + 1)
                for k in range(NC):
                    ins = mm(Rb[0][:, 0:T], ones[:], sq[:, k, :], start=(k == 0), stop=(k == NC - 1))
                ins.then_inc(S["p_nrm"], 1)
                if ffn:
                    for part in ffn_second:
                        ffn_part(b - 1, part)
                pe.wait_ge(S["d_xn"], b + 1)
                def head_norm(c):
                    pe.wait_ge(S["a_sq"], b * NC + c + 1)
                    if c >= 2:
                        pe.wait_ge(S["a_hr"], b * NC + c - 1)
                    mm(Rb[c % 2][:], headones[:], sqh[:, c % 2].rearrange("p a t -> p (a t)"), start=True, stop=True).then_inc(S["p_hr"], 1)
                for c in range(NC):
                    if c >= 2:
                        pe.wait_ge(S["d_qk"], b * NC + c - 1)
                    for a in range(2):
                        for k in range(NC):
                            ins = mm(G[c % 2][:, a * T:(a + 1) * T], w_qkv[:, k, a * N + c * P:a * N + (c + 1) * P], xn[:, k, :],
                                     start=(k == 0), stop=(k == NC - 1))
                    ins.then_inc(S["p_qk"], 1)
                    if c:
                        head_norm(c - 1)
                for i in range(2):
                    for k in range(NC):
                        ins = mm(Ob[i][:], xn[:, k, i * P:(i + 1) * P], w_qkv[:, k, 2 * N:3 * N], start=(k == 0), stop=(k == NC - 1))
                    ins.then_inc(S["p_v"], 1)
                    if i == 0:
                        head_norm(NC - 1)
                def scores(h):
                    c, r = h // HPC, DH * (h % HPC)
                    if h == 0:
                        pe.wait_ge(S["d_qk"], b * NC + NC)
                    if h >= 2:
                        pe.wait_ge(S["a_exp"], b * HEADS + h - 1)
                    for qc in range(2):
                        ins = mm(G[h % 2][:, qc * T:(qc + 1) * T], qk[r:r + DH, c, 0, qc * P:(qc + 1) * P], qk[r:r + DH, c, 1, :], start=True, stop=True)
                    ins.then_inc(S["p_s"], 1)
                def transposed(h):
                    pe.wait_ge(S["a_exp"], b * HEADS + h + 1)
                    if h >= 2:
                        pe.wait_ge(S["d_pt"], b * HEADS + h - 1)
                    for kc in range(2):
                        for qc in range(2):
                            ins = nc.tensor.transpose(Rb[h % 2][:, kc * T + qc * P:kc * T + (qc + 1) * P], pr[:, h % 2, qc, kc * P:(kc + 1) * P], ident[:])
                    ins.then_inc(S["p_t"], 1)
                def weighted(h):
                    pe.wait_ge(S["d_pt"], b * HEADS + h + 1)
                    if h == 0:
                        pe.wait_ge(S["a_v"], b * 2 + 2)
                    for qc in range(2):
                        for kc in range(2):
                            ins = mm(Ob[qc][:, h * DH:(h + 1) * DH], prT[:, h % 2, kc, qc * P:(qc + 1) * P], v[:, kc, h * DH:(h + 1) * DH],
                                     start=(kc == 0), stop=(kc == 1))
                    if h == HEADS - 1:
                        ins.then_inc(S["p_pv"], 1)
                scores(0)
                for h in range(HEADS):
                    if h + 1 < HEADS:
                        scores(h + 1)
                    if ffn:
                        for part in ffn_heads[h]:
                            ffn_part(b - 1, part)
                    else:
                        lora(h)
                    transposed(h)
                    if h:
                        weighted(h - 1)
                weighted(HEADS - 1)
                pe.wait_ge(S["d_o"], b + 1)
                for i in range(2):
                    if ffn:
                        pe.wait_ge(S["d_x2"], b * 2 - 1 + i)
                    elif i == 0:
                        pe.wait_ge(S["stage"], PIECES)
                    for c in (2 * i, 2 * i + 1):
                        for qc in range(2):
                            ins = nc.tensor.transpose(D[i][:, (c % 2) * T + qc * P:(c % 2) * T + (qc + 1) * P], o[:, qc, c * P:(c + 1) * P], ident[:])
                    ins.then_inc(S["p_ot"], 1)
                if not ffn:
                    pe.wait_ge(S["wo_in"], 16)
                pe.wait_ge(S["d_ot"], b * 2 + 2)
                for m in range(NC):
                    for k in range(NC):
                        ins = mm(G[m // 2][:, (m % 2) * T:(m % 2 + 1) * T], w_out[:, k, m * P:(m + 1) * P], oT[:, k, :], start=(k == 0), stop=(k == NC - 1))
                    if m % 2:
                        ins.then_inc(S["p_wo"], 1)
                pe.wait_ge(S["d_x1"], b * 2 + 2)
            batch(0, False)
            with pe.Fori(1, B) as b:
                batch(b, True)
            for part in range(2 * HC):
                ffn_part(B - 1, part)

        @block.vector
        def _(dve):
            count = [0]
            def link(ins, at=None):
                count[0] += 1
                ins.then_inc(S["chain"], 1)
                dve.wait_ge(S["chain"], count[0] if at is None else at + count[0])
            dve.wait_ge(S["vec_in"], 48)
            dve.wait_ge(S["mm_ss"], 1)
            link(dve.tensor_tensor(ss[:], Ob[0][:, 0:2 * NC * B].rearrange("p (m b) -> p m b", b=B), b_emb.unsqueeze(2).to_broadcast([P, 2 * NC, B]), ALU.add))
            link(dve.scalar_tensor_tensor(amp[:], ss[:, 0:NC, :], 1.0, g_norm.unsqueeze(2).to_broadcast([P, NC, B]), ALU.add, ALU.mult))
            link(dve.tensor_scalar(bias2[:], b_scan[:], ALPHA / BETA, None, ALU.subtract))
            link(dve.tensor_tensor(bias2[:], bias2[:], b_dn[:], ALU.add))
            dve.scalar_tensor_tensor(g_q, g_q, DH ** -0.5, g_k, ALU.mult, ALU.mult).then_inc(S["amps"], 1)
            base = count[0]
            KD = 2

            def restore(h):
                u = h % 2
                dmas = [3 if n < PIECES // 2 else 5 for n in range(PIECES)]
                dve.wait_ge(codes_in[u], 16 * sum(dmas[u:h + 1:2]))
                dve.scalar_tensor_tensor(scales[u], codes[u], 7.5, scales[u], ALU.subtract, ALU.mult).then_inc(S["scaled"], 1)
                dve.wait_ge(S["mm_lora"], h + 1)
                dve.wait_ge(S["scaled"], h + 1)
                for i in range(2):
                    if h < PIECES // 2:
                        dst = w_up[:, h // 2, h % 2 * PIECE + i * 512:h % 2 * PIECE + (i + 1) * 512]
                    else:
                        dst = w_dn[:, 2 * (h - PIECES // 2) + i, :]
                    ins = dve.tensor_tensor(dst, D[i][:], scales[u][:, i * 512:(i + 1) * 512], ALU.add)
                ins.then_inc(S["stage"], 1)

            def second(n, i):
                dve.wait_ge(S["p_dn"], n * 2 + i + 1)
                for c in (2 * i, 2 * i + 1):
                    slot = xv[:, c, bass.ds(n, 1), :].rearrange("p o t -> p (o t)")
                    ins = dve.scalar_tensor_tensor(slot, D[i][:, (c % 2) * T:(c % 2 + 1) * T], bias2[:, c:c + 1], slot, ALU.add, ALU.add)
                ins.then_inc(S["d_x2"], 1)

            def batch(b, ffn):
                count[0] = 0
                at = base + b * KD
                xb = xv[:, :, bass.ds(b, 1), :].rearrange("p c o t -> p c (o t)")
                dve.wait_ge(S["a_rstd"], b + 1)
                link(dve.tensor_tensor(xn[:], xb, rs[:, 1:2, :].to_broadcast([P, NC, T]), ALU.mult), at)
                for c in range(NC):
                    ins = dve.tensor_scalar(xn[:, c, :], xn[:, c, :], amp[:, c, bass.ds(b, 1)], ss[:, NC + c, bass.ds(b, 1)], ALU.mult, ALU.add)
                ins.then_inc(S["d_xn"], 1)
                for c in range(NC):
                    dve.wait_ge(S["a_hr"], b * NC + c + 1)
                    dve.scalar_tensor_tensor(qk[:, c, 0, :], G[c % 2][:, 0:T], g_q, rh[:, c % 2, 0, :], ALU.mult, ALU.mult)
                    dve.tensor_tensor(qk[:, c, 1, :], G[c % 2][:, T:2 * T], rh[:, c % 2, 1, :], ALU.mult).then_inc(S["d_qk"], 1)
                def row_max(h):
                    dve.wait_ge(S["p_s"], b * HEADS + h + 1)
                    dve.tensor_reduce(nmax[:, h % 2, :], G[h % 2][:].rearrange("p (a t) -> p a t", a=2), AX.X, ALU.max, negate=True).then_inc(S["d_max"], 1)
                row_max(0)
                for h in range(HEADS):
                    if h + 1 < HEADS:
                        if h >= 1:
                            dve.wait_ge(S["a_exp"], b * HEADS + h)
                        row_max(h + 1)
                    dve.wait_ge(S["p_t"], b * HEADS + h + 1)
                    dve.tensor_copy(prT[:, h % 2].rearrange("p a t -> p (a t)"), Rb[h % 2][:]).then_inc(S["d_pt"], 1)
                    if not ffn:
                        restore(h)
                    elif h == HEADS - 2:
                        second(b - 1, 0)
                dve.wait_ge(S["a_exp"], (b + 1) * HEADS)
                link(dve.reciprocal(rinv[:], psum_e[:]), at)
                dve.wait_ge(S["p_pv"], b + 1)
                for qc in range(2):
                    ins = dve.tensor_tensor(o[:, qc, :].rearrange("p (h d) -> p h d", d=DH), Ob[qc][:].rearrange("p (h d) -> p h d", d=DH),
                                            rinv[:, :, qc:qc + 1].to_broadcast([P, HEADS, DH]), ALU.mult)
                ins.then_inc(S["d_o"], 1)
                if ffn:
                    second(b - 1, 1)
                for i in range(2):
                    dve.wait_ge(S["p_ot"], b * 2 + i + 1)
                    dve.tensor_copy(oT[:, 2 * i:2 * i + 2, :].rearrange("p a t -> p (a t)"), D[i][:]).then_inc(S["d_ot"], 1)
                for i in range(2):
                    dve.wait_ge(S["p_wo"], b * 2 + i + 1)
                    if i == 0:
                        dve.wait_ge(S["d_ot"], b * 2 + 2)
                    dve.tensor_tensor(x1[:, 2 * i:2 * i + 2, :].rearrange("p a t -> p (a t)"), G[i][:], oT[:, 2 * i:2 * i + 2, :].rearrange("p a t -> p (a t)"), ALU.add).then_inc(S["d_x1"], 1)
                assert count[0] == KD

            batch(0, False)
            with dve.Fori(1, B) as b:
                batch(b, True)
            for i in range(2):
                second(B - 1, i)


G = 32
NG = T // G
GT = G * B
W = NC * B
RK = [DT / 2, DT / 2, DT, DT / 6]
SHIFT = 2.0 ** 13


def linear_terms():
    import numpy as np
    q, p, d, q2, q3, q4 = np.eye(6)
    e = EPSILON * BETA
    p2 = p + DT / 2 * e * (q - p)
    p3 = p + DT / 2 * e * (q2 - p2)
    p4 = p + DT * e * (q3 - p3)
    rows = [q + RK[0] * (d - p / BETA), q + RK[1] * (d - p2 / BETA), q + RK[2] * (d - p3 / BETA),
            (-q + q2 + 2 * q3 + q4) / 3 + RK[3] * (d - p4 / BETA),
            (-p + p2 + 2 * p3 + p4) / 3 + RK[3] * e * (q4 - p4)]
    return np.array(rows)


def layer1(nc, dram, xs, wk, w_split, out):
    ctx = ExitStack()
    with ctx:
        sb = lambda n, s, d=F32: ctx.enter_context(nc.sbuf_tensor(n, s, d))
        sem = lambda n: ctx.enter_context(nc.semaphore(n))
        cT = sb("cT", [P, NC, N])
        chi = sb("chi", [P, NC, N], F16)
        clo = sb("clo", [P, NC, N], F16)
        kp = sb("kp", [P, 8])
        b_scan = sb("b_scan1", [P, NC])
        unshift = sb("unshift", [P, NC])
        state = [sb(f"state{s}", [P, W]) for s in range(4)]
        qraw = sb("qraw", [P, W])
        pst = sb("pst", [P, W])
        th = sb("th", [P, NC, 2, B], F16)
        t32 = sb("t32", [P, W])
        sq = sb("sq1", [P, W]); cub = sb("cub", [P, W]); base = sb("base", [P, W]); part = sb("part", [P, W])
        cq, cp, cd = (sb(n, [P, 5, W]) for n in ("coef_q", "coef_p", "coef_d"))
        c2 = sb("coef2", [P, 3, W]); c3 = sb("coef3", [P, 2, W]); c4 = sb("coef4", [P, 2, W])
        A = [sb(f"lin{u}", [P, 5, W]) for u in range(2)]
        md, mp_ = (sb(n, [P, 5, W]) for n in ("from_drive", "from_p"))
        mq = sb("from_q", [P, 4, W])
        ms, ms3, ms4 = (sb(n, [P, r, W]) for n, r in (("from_q2", 3), ("from_q3", 2), ("from_q4", 2)))
        zeros = sb("zeros", [P, 512], BF16)
        trace = sb("trace", [P, NC, G, B])
        qg = sb("qg", [P, NC, GT])
        qh = sb("qh", [P, 2, NC, GT], F16)
        wgu = sb("wgu", [P, 2, 2, 2, NC, P], F16)
        wd = sb("wd", [P, 2, N])
        wr = sb("wr", [P, NC, E1 + 1])
        ident = sb("ident1", [P, P])
        lanes = sb("lanes", [P, E1])
        rt = sb("rt", [P, 2, E1 + 1]); top = sb("top", [P, 2, 8]); topi = sb("topi", [P, 2, 8], mybir.dt.uint32); topf = sb("topf", [P, 2, 8])
        ex = sb("ex", [P, 2, E1 + 1]); es = sb("es", [P, 2, 4]); msk = sb("msk", [P, 2, 2, E1]); wide = sb("wide", [P, 2, 2, P])
        neg = sb("neg", [P, 2])
        gates = sb("gates", [P, 2, GT])
        sg = sb("sg", [P, GT]); ha = sb("ha", [P, GT]); hb = sb("hb", [P, GT]); hg = sb("hg", [P, 2, GT])
        oo = sb("oo", [P, NC, G, B])
        pscan = ctx.enter_context(nc.psum_tensor("pscan", [P, NC, 2, B], F32))
        pg = ctx.enter_context(nc.psum_tensor("pg", [P, 512], F32))
        pu = ctx.enter_context(nc.psum_tensor("pu", [P, 512], F32))
        pd = [ctx.enter_context(nc.psum_tensor(f"pd{i}", [P, 512], F32)) for i in range(2)]
        pr_ = ctx.enter_context(nc.psum_tensor("prouter", [P, 512], F32))
        names = ("cin vin eye par mx kps scale_rdy linit coef th_ready t32_ready sq_ready tl_ready ic_ready q_ready clip_ready pclip_ready e_ready "
                 "traced lin_ready copied q_high q_low dchain pchain wg0 wg1 wd0 wd1 up_done dn_done gate_done sg_ready ha_ready hb_ready hid_ready fin out_ready stored "
                 "spseq plseq dveseq rt_mm rt_max rt_exp rt_wide rt_tr gates_ready rchain rachain").split()
        S = {n: sem("l1_" + n) for n in names}
        wsem = [S["wg0"], S["wg1"]]; dsem = [S["wd0"], S["wd1"]]
        block = ctx.enter_context(nc.Block())
        v3 = lambda ap: ap.rearrange("p (c b) -> p c b", b=B)
        xv = xs[:, 0:NC * B * T].rearrange("p (c b t) -> p c b t", c=NC, b=B)
        def drive(t):
            return xs[:, bass.ds(t, NC * B * T)].rearrange("p (c b t) -> p c b t", c=NC, b=B)[:, :, :, 0]
        coefs = linear_terms()

        def walk(eng, before, step, after):
            with eng.Fori(0, G // 2) as i:
                for u in range(2):
                    step(None, i, u, 2 * i + u, True, False)
            with eng.Fori(0, NG - 1) as seg:
                before(seg)
                for u in range(2):
                    step(seg, 0, u, G + seg * G + u, True, True)
                with eng.Fori(1, G // 2) as i:
                    for u in range(2):
                        step(seg, i, u, G + seg * G + 2 * i + u, True, True)
                after(seg)
            before(NG - 1)
            for u in range(2):
                step(NG - 1, 0, u, None, False, True)
            with eng.Fori(1, G // 2) as i:
                for u in range(2):
                    step(NG - 1, i, u, None, False, True)
            after(NG - 1)

        def is_first(i, u):
            return isinstance(i, int) and i == 0 and u == 0

        def gate_row(i, u):
            return (i * 3) // 32 if u else (i * 3 - 3) // 32

        @block.sync
        def _(sp):
            sp.dma_start(cT[:], dram["coupling"]).then_inc(S["cin"], 16)
            sp.dma_start(b_scan[:], dram["b_scan"]).then_inc(S["vin"], 16)
            sp.dma_start(wr[:], dram["w_router"]).then_inc(S["vin"], 16)
            sp.dma_start(state[0][:], dram["cond"]).then_inc(S["vin"], 16)
            sp.dma_start(qraw[:], dram["cond"]).then_inc(S["vin"], 16)

            def load(tile, slot, done):
                sp.wait_ge(S["up_done"], done)
                sp.sem_inc(S["spseq"], 1)
                sp.dma_start(wgu[:, slot].rearrange("p a h c f -> p (a h c f)"),
                             w_split[bass.ds(tile, 1), :, :].rearrange("o p n -> (o p) n")).then_inc(wsem[slot], 16)
                sp.wait_ge(S["dn_done"], done)
                sp.sem_inc(S["spseq"], 1)
                sp.dma_start(wd[:, slot, :],
                             dram["w_tiles"][bass.ds(tile, 1), :, 2 * N:3 * N].rearrange("o p n -> (o p) n")).then_inc(dsem[slot], 16)

            with sp.Fori(0, NG) as seg:
                done = seg * TILES + 2
                load(0, 0, done)
                load(1, 1, done - 1)
                with sp.Fori(1, G // 2) as i:
                    for u in range(2):
                        load(2 * i + u, u, done + 2 * i + u - 1)
                load(TILES - 1, 0, done + TILES - 2)
                sp.wait_ge(S["out_ready"], seg * NC + NC + 1)
                sp.sem_inc(S["spseq"], 1)
                sp.dma_start(out[:, :, bass.ds(seg * G, G), :], oo[:]).then_inc(S["stored"], 16)
            sp.wait_ge(S["stored"], 16 * (NG + 1))

        @block.gpsimd
        def _(pl):
            pl.memset(ident[:], 0.0).then_inc(S["eye"], 1)
            pl.wait_ge(S["eye"], 1)
            pl.affine_select(out=ident[:], in_=ident[:], compare_op=ALU.not_equal, fill=1.0, base=0,
                             pattern=[[-1, P]], channel_multiplier=1).then_inc(S["eye"], 1)
            for e in range(E1):
                pl.memset(lanes[:, e:e + 1], float(e))
            for r in range(5):
                for tile, col in ((cq, 0), (cp, 1), (cd, 2)):
                    pl.memset(tile[:, r, :], float(coefs[r, col]))
                if r >= 2:
                    pl.memset(c2[:, r - 2, :], float(coefs[r, 3]))
                if r >= 3:
                    pl.memset(c3[:, r - 3, :], float(coefs[r, 4]))
                    pl.memset(c4[:, r - 3, :], float(coefs[r, 5]))
            pl.memset(xs[:, NC * B * T:], 0.0)
            pl.memset(zeros[:], 0.0).then_inc(S["coef"], 1)
            pl.wait_ge(S["mx"], 1)
            pl.partition_all_reduce(kp[:, 1:2], kp[:, 0:1], P, bass.bass_isa.ReduceOp.max).then_inc(S["par"], 1)
            pl.wait_ge(S["coef"], 1)
            rows = lambda ap, n: ap.unsqueeze(1).to_broadcast([P, n, W])
            K = 7

            def next_linear(t, u, k, at, pclips):
                dv = drive(t).unsqueeze(1).to_broadcast([P, 5, NC, B])
                pl.tensor_tensor(md[:].rearrange("p r (c b) -> p r c b", b=B), dv, cd[:].rearrange("p r (c b) -> p r c b", b=B), ALU.mult).then_inc(S["pchain"], 1)
                pl.wait_ge(S["pclip_ready"], pclips)
                pl.tensor_tensor(mp_[:], rows(pst[:], 5), cp[:], ALU.mult).then_inc(S["pchain"], 1)
                pl.wait_ge(S["pchain"], at + k + 2)
                pl.tensor_tensor(A[u][:], md[:], mp_[:], ALU.add).then_inc(S["lin_ready"], 1)
                pl.wait_ge(S["lin_ready"], t + 1)
                pl.sem_inc(S["plseq"], 1)
            next_linear(0, 0, 0, 0, 1)

            def step(seg, i, u, t, scan, tile):
                if not scan:
                    return
                at = 2 + t * K
                pl.wait_ge(S["clip_ready"], t + 1)
                pl.tensor_tensor(mq[:], rows(state[0][:], 4), cq[:, 1:5, :], ALU.mult).then_inc(S["pchain"], 1)
                pl.wait_ge(S["pchain"], at + 1)
                pl.tensor_tensor(A[u][:, 1:5, :], A[u][:, 1:5, :], mq[:], ALU.add).then_inc(S["e_ready"], 1)
                pl.wait_ge(S["q_ready"], t * 4 + 2)
                pl.tensor_tensor(ms[:], rows(state[1][:], 3), c2[:], ALU.mult).then_inc(S["pchain"], 1)
                pl.wait_ge(S["e_ready"], t * 3 + 1)
                pl.sem_inc(S["plseq"], 1)
                pl.wait_ge(S["pchain"], at + 2)
                pl.tensor_tensor(A[u][:, 2:5, :], A[u][:, 2:5, :], ms[:], ALU.add).then_inc(S["e_ready"], 1)
                pl.wait_ge(S["q_ready"], t * 4 + 3)
                pl.tensor_tensor(ms3[:], rows(state[2][:], 2), c3[:], ALU.mult).then_inc(S["pchain"], 1)
                pl.wait_ge(S["e_ready"], t * 3 + 2)
                pl.sem_inc(S["plseq"], 1)
                pl.wait_ge(S["pchain"], at + 3)
                pl.tensor_tensor(A[u][:, 3:5, :], A[u][:, 3:5, :], ms3[:], ALU.add).then_inc(S["pchain"], 1)
                pl.wait_ge(S["q_ready"], t * 4 + 4)
                pl.sem_inc(S["plseq"], 1)
                pl.wait_ge(S["pchain"], at + 4)
                pl.tensor_tensor(ms4[:], rows(state[3][:], 2), c4[:], ALU.mult).then_inc(S["pchain"], 1)
                pl.wait_ge(S["pchain"], at + 5)
                pl.tensor_tensor(A[u][:, 3:5, :], A[u][:, 3:5, :], ms4[:], ALU.add).then_inc(S["e_ready"], 1)
                pl.wait_ge(S["e_ready"], t * 3 + 3)
                pl.sem_inc(S["plseq"], 1)
                next_linear(t + 1, 1 - u, 5, at, t + 2)
            walk(pl, lambda seg: None, step, lambda seg: None)

        @block.scalar
        def _(act):
            act.wait_ge(S["scale_rdy"], 1)
            nc.scalar.preload_act_table_set("exp_and_others")

            def step(seg, i, u, t, scan, tile):
                for s in range(4):
                    if scan:
                        src = qraw if s == 0 else state[s]
                        act.wait_ge(S["q_ready"], t * 4 + s + 1)
                        act.activation(th[:, :, 0, :], v3(src[:]), ACT.Tanh).then_inc(S["th_ready"], 1)
                        act.activation(t32[:], src[:], ACT.Tanh).then_inc(S["t32_ready"], 1)
                        if s == 0:
                            act.wait_ge(S["clip_ready"], t + 1)
                        act.activation(sq[:], state[s][:], ACT.Square).then_inc(S["sq_ready"], 1)
                    if tile and s == 2:
                        silu(seg * TILES + 2 * i + u)

            def silu(n):
                act.wait_ge(S["gate_done"], n + 1)
                act.activation(sg[:], pg[:, 0:GT], ACT.Tanh, scale=wk[:, 3:4]).then_inc(S["sg_ready"], 1)

            def before(seg):
                act.wait_ge(S["traced"], seg * G + G)
                act.wait_ge(S["up_done"], seg * TILES + 2)
                act.activation(qh[:, 0], trace[:].rearrange("p c t b -> p c (t b)"), ACT.Copy, scale=2.0 ** Q_BITS).then_inc(S["q_high"], 1)
                act.activation(qg[:], trace[:].rearrange("p c t b -> p c (t b)"), ACT.Copy).then_inc(S["copied"], 1)
                act.wait_ge(S["rt_max"], seg + 1)
                for c in range(2):
                    act.activation(ex[:, c, 0:E1], rt[:, c, 0:E1], ACT.Exp, bias=neg[:, c:c + 1], accum_out=es[:, c, 0:1])
                    ins = act.activation(ex[:, c, E1:E1 + 1], rt[:, c, E1:E1 + 1], ACT.Exp, scale=-1.0)
                ins.then_inc(S["rt_exp"], 1)
            walk(act, before, step, lambda seg: silu(seg * TILES + TILES - 1))

        @block.tensor
        def _(pe):
            mm = nc.tensor.matmul
            pe.wait_ge(S["eye"], 2)
            pe.wait_ge(S["vin"], 64)
            pe.wait_ge(S["scale_rdy"], 1)
            pe.wait_ge(S["coef"], 1)
            pe.sem_inc(S["up_done"], 2)
            pe.sem_inc(S["dn_done"], 2)

            def split_product(dst, slot, a, ks):
                for k in ks:
                    for w, q in ((0, 0), (0, 1), (1, 0)):
                        ins = mm(dst[:, 0:GT], wgu[:, slot, a, w, k, :], qh[:, q, k, :],
                                 start=(k == 0 and w == q), stop=(k == NC - 1 and w == 1))
                return ins

            def gate(slot, n, ks):
                if 0 in ks:
                    pe.wait_ge(wsem[slot], 16 * loads(slot, n))
                    pe.wait_ge(S["ha_ready"], n[0] * TILES + n[1] + 1)
                    pe.wait_ge(S["q_low"], n[0] + 1)
                ins = split_product(pg, slot, 0, ks)
                if NC - 1 in ks:
                    ins.then_inc(S["gate_done"], 1)

            def up(slot, n, ks):
                if 0 in ks:
                    pe.wait_ge(S["hb_ready"], n[0] * TILES + n[1] + 1)
                ins = split_product(pu, slot, 1, ks)
                if NC - 1 in ks:
                    ins.then_inc(S["up_done"], 1)

            def down(slot, seg, j, dloads, ms_):
                if 0 in ms_:
                    pe.wait_ge(S["hid_ready"], seg * TILES + j + 1)
                    pe.wait_ge(dsem[slot], dloads)
                for m in ms_:
                    ins = mm(pd[m // 2][:, (m % 2) * GT:(m % 2 + 1) * GT], wd[:, slot, m * P:(m + 1) * P], hg[:, slot, :],
                             start=False, stop=False, skip_group_check=True)
                if NC - 1 in ms_:
                    ins.then_inc(S["dn_done"], 1)

            def loads(slot, n):
                seg, i = n[0], n[2]
                return seg * (17 if slot == 0 else 16) + i + 1

            def down_loads(u, seg, i):
                return 16 * (seg * 17 + i + 1) if u else 16 * (seg * 16 + i)

            def step(seg, i, u, t, scan, tile):
                if tile:
                    n = (seg, 2 * i + u, i)
                    dl = down_loads(u, seg, i)
                    peeled = isinstance(i, int)
                    slots = [lambda: (None if peeled else down(u, seg, 2 * i + u - 2, None, [3]), gate(u, n, [0, 1])),
                             lambda: (gate(u, n, [2, 3]), up(u, n, [0])),
                             lambda: up(u, n, [1, 2, 3]),
                             lambda: None if is_first(i, u) else down(1 - u, seg, 2 * i + u - 1, dl, [0, 1, 2])]
                for s in range(4):
                    if scan:
                        pe.wait_ge(S["th_ready"], t * 4 + s + 1)
                        for m in range(NC):
                            for k in range(NC):
                                mm(pscan[:, m, 0, :], clo[:, k, m * P:(m + 1) * P], th[:, k, 0, :], start=(m == 0 and k == 0), stop=False, skip_group_check=True)
                        pe.wait_ge(S["tl_ready"], t * 4 + s + 1)
                        for m in range(NC):
                            for k in range(NC):
                                ins = mm(pscan[:, m].rearrange("p a b -> p (a b)"), chi[:, k, m * P:(m + 1) * P], th[:, k].rearrange("p a b -> p (a b)"),
                                         start=False, stop=(k == NC - 1), skip_group_check=True)
                        ins.then_inc(S["ic_ready"], 1)
                    if tile:
                        slots[s]()

            def before(seg):
                pe.wait_ge(S["copied"], seg + 1)
                for c in range(2):
                    for k in range(NC):
                        ins = mm(pr_[:, 16 * c:16 * c + E1 + 1], qg[:, k, c * P:(c + 1) * P], wr[:, k, :], start=(k == 0), stop=(k == NC - 1))
                ins.then_inc(S["rt_mm"], 1)
                pe.wait_ge(S["out_ready"], seg * NC + 1)
                for i in range(2):
                    mm(pd[i][:], zeros[:, 0:P], zeros[:], start=True, stop=False, skip_group_check=True)
                pe.wait_ge(S["rt_wide"], seg + 1)
                for r in range(2):
                    for c in range(2):
                        ins = nc.tensor.transpose(pr_[:, r * GT + c * P:r * GT + (c + 1) * P], wide[:, c, r, :], ident[:])
                ins.then_inc(S["rt_tr"], 1)

            def after(seg):
                n = (seg, TILES - 1, 16)
                gate(0, n, [0, 1, 2, 3])
                up(0, n, [0, 1, 2, 3])
                down(0, seg, TILES - 3, None, [3])
                down(1, seg, TILES - 2, down_loads(0, seg, 16), [0, 1, 2, 3])
                down(0, seg, TILES - 1, down_loads(1, seg, 16), [0, 1, 2, 3])
            walk(pe, before, step, after)

        @block.vector
        def _(dve):
            setup = [0]
            def link(ins):
                setup[0] += 1
                ins.then_inc(S["rchain"], 1)
                dve.wait_ge(S["rchain"], setup[0])
            dve.wait_ge(S["cin"], 16)
            dve.tensor_reduce(kp[:, 0:1], cT[:].rearrange("p c n -> p (c n)"), AX.X, ALU.max, apply_absolute_value=True).then_inc(S["mx"], 1)
            dve.wait_ge(S["par"], 1)
            link(dve.tensor_scalar(kp[:, 1:2], kp[:, 1:2], 2.0 ** -100, None, ALU.max))
            ki = kp[:].bitcast(I32)
            link(dve.tensor_scalar(ki[:, 2:3], ki[:, 1:2], 0x7F800000, None, ALU.bitwise_and))
            link(dve.reciprocal(kp[:, 3:4], kp[:, 2:3]))
            link(dve.tensor_scalar(kp[:, 3:4], kp[:, 3:4], SHIFT, None, ALU.mult))
            for s in range(4):
                link(dve.tensor_scalar(kp[:, 4 + s:5 + s], kp[:, 2:3], RK[s] / SHIFT, None, ALU.mult))
            link(dve.tensor_scalar(chi[:], cT[:], kp[:, 3:4], None, ALU.mult))
            link(dve.scalar_tensor_tensor(clo[:], cT[:], kp[:, 3:4], chi[:], ALU.mult, ALU.subtract))
            dve.wait_ge(S["vin"], 64)
            link(dve.tensor_scalar(unshift[:], b_scan[:], -1.0, ALPHA / BETA, ALU.mult, ALU.add))
            dve.tensor_scalar(pst[:], state[0][:], BETA, ALPHA, ALU.mult, ALU.subtract).then_inc(S["pclip_ready"], 1)
            link(dve.tensor_scalar(wk[:, 3:4], wk[:, 1:2], 0.5, None, ALU.mult))
            dve.sem_inc(S["scale_rdy"], 1)
            dve.sem_inc(S["q_ready"], 1)
            dve.sem_inc(S["clip_ready"], 1)
            dve.sem_inc(S["ha_ready"], 1)
            dve.sem_inc(S["hb_ready"], 1)
            dve.sem_inc(S["out_ready"], 1)
            dve.sem_inc(S["stored"], 16)
            K = 13

            def step(seg, i, u, t, scan, tile):
                k = [0]
                def chain(ins, wait=True):
                    k[0] += 1
                    ins.then_inc(S["dchain"], 1)
                    if wait:
                        dve.wait_ge(S["dchain"], t * K + k[0])
                for s in range(4):
                    bulk = tile and not is_first(i, u)
                    if bulk and not scan and s in (0, 2):
                        (hidden_up if s == 0 else hidden_gate)(seg, 2 * i + u - 1, 1 - u, gate_row(i, u))
                    if scan:
                        nxt = state[s + 1] if s < 3 else qraw
                        dve.wait_ge(S["t32_ready"], t * 4 + s + 1)
                        dve.tensor_tensor(th[:, :, 1, :], v3(t32[:]), th[:, :, 0, :], ALU.subtract).then_inc(S["tl_ready"], 1)
                        dve.wait_ge(S["sq_ready"], t * 4 + s + 1)
                        if bulk and s == 0:
                            chain(dve.scalar_tensor_tensor(cub[:], sq[:], -3.0, state[s][:], ALU.add, ALU.mult), False)
                            hidden_up(seg, 2 * i + u - 1, 1 - u, None)
                            dve.wait_ge(S["dchain"], t * K + k[0])
                        else:
                            chain(dve.scalar_tensor_tensor(cub[:], sq[:], -3.0, state[s][:], ALU.add, ALU.mult))
                        if s == 0:
                            chain(dve.scalar_tensor_tensor(base[:], cub[:], -RK[s] / 3, state[0][:], ALU.mult, ALU.add))
                            dve.wait_ge(S["lin_ready"], t + 1)
                            chain(dve.tensor_tensor(base[:], base[:], A[u][:, 0, :], ALU.add))
                        else:
                            dve.wait_ge(S["e_ready"], t * 3 + s)
                            chain(dve.scalar_tensor_tensor(base[:], cub[:], -RK[s] / 3, A[u][:, s, :], ALU.mult, ALU.add), not (bulk and s == 2))
                            if bulk and s == 2:
                                hidden_gate(seg, 2 * i + u - 1, 1 - u, gate_row(i, u))
                                dve.wait_ge(S["dchain"], t * K + k[0])
                        if s == 3:
                            dve.tensor_scalar(pst[:], A[u][:, 4, :], BETA * CLAMP - ALPHA, -BETA * CLAMP - ALPHA, ALU.min, ALU.max).then_inc(S["pclip_ready"], 1)
                        dve.wait_ge(S["ic_ready"], t * 4 + s + 1)
                        chain(dve.scalar_tensor_tensor(v3(part[:]), pscan[:, :, 1, :], kp[:, 4 + s:5 + s], v3(base[:]), ALU.mult, ALU.add))
                        dve.scalar_tensor_tensor(v3(nxt[:]), pscan[:, :, 0, :], kp[:, 4 + s:5 + s], v3(part[:]), ALU.mult, ALU.add).then_inc(S["q_ready"], 1)
                        if s == 3:
                            dve.wait_ge(S["q_ready"], t * 4 + 5)
                            dve.tensor_scalar(state[0][:], qraw[:], CLAMP, -CLAMP, ALU.min, ALU.max).then_inc(S["clip_ready"], 1)
                            dve.tensor_scalar(trace[:, :, bass.ds(2 * i + u, 1), :].rearrange("p c o b -> p c (o b)"), v3(qraw[:]), CLAMP, -CLAMP, ALU.min, ALU.max).then_inc(S["traced"], 1)
                    if tile and s == 2:
                        act_gate(seg * TILES + 2 * i + u)

            def act_gate(n):
                dve.wait_ge(S["sg_ready"], n + 1)
                dve.scalar_tensor_tensor(ha[:], sg[:], 1.0, pg[:, 0:GT], ALU.add, ALU.mult).then_inc(S["ha_ready"], 1)

            def hidden_up(seg, j, slot, row):
                n = seg * TILES + j
                dve.wait_ge(S["up_done"], n + 3)
                dve.wait_ge(S["ha_ready"], n + 2)
                dve.scalar_tensor_tensor(hb[:], pu[:, 0:GT], wk[:, 1:2], ha[:], ALU.mult, ALU.mult).then_inc(S["hb_ready"], 1)

            def hidden_gate(seg, j, slot, row):
                n = seg * TILES + j
                dve.wait_ge(S["hb_ready"], n + 2)
                dve.wait_ge(S["dn_done"], n + 2 if isinstance(j, int) and j == 0 else n + 1)
                g = gates[:, bass.ds(row, 1), :].rearrange("p o t -> p (o t)") if not isinstance(row, int) else gates[:, row, :]
                dve.scalar_tensor_tensor(hg[:, slot, :], hb[:], wk[:, 1:2], g, ALU.mult, ALU.mult).then_inc(S["hid_ready"], 1)

            RL = 10
            def before(seg):
                k = [0]
                base_ = setup[0]
                def chain(ins, wait=True):
                    k[0] += 1
                    ins.then_inc(S["rchain"], 1)
                    if wait:
                        dve.wait_ge(S["rchain"], base_ + seg * RL + k[0])
                dve.wait_ge(S["q_high"], seg + 1)
                dve.wait_ge(S["up_done"], seg * TILES + 2)
                dve.scalar_tensor_tensor(qh[:, 1], trace[:].rearrange("p c t b -> p c (t b)"), 2.0 ** Q_BITS, qh[:, 0], ALU.mult, ALU.subtract).then_inc(S["q_low"], 1)
                dve.wait_ge(S["copied"], seg + 1)
                dve.wait_ge(S["rt_mm"], seg + 1)
                chain(dve.tensor_copy(rt[:], pr_[:, 0:32].rearrange("p (c e) -> p c e", c=2)[:, :, 0:E1 + 1]))
                dve.sem_inc(S["dveseq"], 1)
                for c in range(2):
                    ins = dve.max(top[:, c, :], rt[:, c, 0:E1])
                chain(ins)
                dve.sem_inc(S["dveseq"], 1)
                for c in range(2):
                    dve.max_index(topi[:, c, :], top[:, c, :], rt[:, c, 0:E1])
                dve.tensor_scalar(neg[:], top[:, :, 0:1].rearrange("p c o -> p (c o)"), -1.0, None, ALU.mult).then_inc(S["rt_max"], 1)
                dve.wait_ge(S["rt_max"], seg + 1)
                chain(dve.tensor_copy(topf[:], topi[:]))
                for c in range(2):
                    ins = dve.tensor_scalar(msk[:, c, 0, :], lanes[:], topf[:, c, 0:1], None, ALU.is_equal)
                chain(ins)
                for c in range(2):
                    ins = dve.scalar_tensor_tensor(msk[:, c, 1, :], lanes[:], topf[:, c, 1:2], msk[:, c, 0, :], ALU.is_equal, ALU.add)
                chain(ins)
                dve.wait_ge(S["rt_exp"], seg + 1)
                chain(dve.tensor_scalar(es[:, :, 1:2], es[:, :, 0:1], 2.0, None, ALU.mult), False)
                chain(dve.tensor_scalar(es[:, :, 2:3], ex[:, :, E1:E1 + 1], 1.0, 2.0, ALU.add, ALU.mult))
                chain(dve.reciprocal(es[:, :, 1:3], es[:, :, 1:3]))
                for c in range(2):
                    ins = dve.scalar_tensor_tensor(msk[:, c, 0, :], msk[:, c, 1, :], es[:, c, 1:2], ex[:, c, 0:E1], ALU.mult, ALU.mult)
                chain(ins)
                for c in range(2):
                    dve.tensor_copy(wide[:, c, 0, :].rearrange("p (e r) -> p e r", r=LANES), msk[:, c, 0, :].unsqueeze(2).to_broadcast([P, E1, LANES]))
                    ins = dve.tensor_copy(wide[:, c, 1, :], es[:, c, 2:3].to_broadcast([P, P]))
                ins.then_inc(S["rt_wide"], 1)
                dve.wait_ge(S["rt_tr"], seg + 1)
                chain(dve.tensor_copy(gates[:].rearrange("p a t -> p (a t)"), pr_[:]))
                dve.sem_inc(S["dveseq"], 1)
                assert k[0] == RL, k

            def after(seg):
                hidden_up(seg, TILES - 2, 1, 1)
                hidden_gate(seg, TILES - 2, 1, 1)
                act_gate(seg * TILES + TILES - 1)
                hidden_up(seg, TILES - 1, 0, 1)
                hidden_gate(seg, TILES - 1, 0, 1)
                dve.wait_ge(S["dn_done"], seg * TILES + TILES + 2)
                dve.wait_ge(S["stored"], 16 * seg + 16)
                for c in range(NC):
                    dve.scalar_tensor_tensor(oo[:, c], pd[c // 2][:, (c % 2) * GT:(c % 2 + 1) * GT].rearrange("p (t b) -> p t b", b=B), unshift[:, c:c + 1],
                                             xv[:, c, :, bass.ds(seg * G, G)].rearrange("p b t -> p t b"), ALU.add, ALU.add).then_inc(S["out_ready"], 1)
            walk(dve, before, step, after)


def build(nc, dram, out):
    w_split = nc.dram_tensor("w_split", (TILES, P, 4 * N), F16, kind="Internal").ap()
    with nc.sbuf_tensor("xs", [P, NC * B * T + T], F32) as xs, nc.sbuf_tensor("wk", [P, 4], F32) as wk:
        layer0(nc, dram, xs, wk, w_split)
        layer1(nc, dram, xs, wk, w_split, out)


def arranged(inputs, np):
    g = lambda n: np.asarray(inputs[n])
    rows = lambda a: a.reshape(a.shape[0] // P, P, *a.shape[1:])
    part = lambda a: np.moveaxis(rows(a), 0, 1)
    up_q, dn_q = g("L0_ffn_w_up_q").T, g("L0_ffn_w_down_q").T
    a = {
        "x": np.ascontiguousarray(part(g("x").transpose(2, 0, 1))),
        "w_emb": part(g("L0_cond_W_emb")), "w_qkv": part(g("L0_cond_W_qkv")), "w_out": part(g("L0_cond_W_out")),
        "up_q": part(up_q), "dn_q": part(dn_q), "up_s": g("L0_ffn_w_up_scale").T, "dn_s": g("L0_ffn_w_down_scale").T,
        "lora": np.stack([np.concatenate([g("L0_ffn_w_up_lora_a").T, g("L0_ffn_w_up_lora_b")], 1),
                          np.concatenate([g("L0_ffn_w_down_lora_a").T, g("L0_ffn_w_down_lora_b")], 1)]),
        "vecs": np.concatenate([part(g("cond_2048").T).reshape(P, NC * B), part(g("L0_cond_b_emb")), part(g("L0_cond_g_norm")),
                                part(g("L0_ffn_b_up")), np.tile(g("L0_cond_g_q"), HPC)[:, None], np.tile(g("L0_cond_g_k"), HPC)[:, None]], 1),
        "b_dn": part(g("L0_ffn_b_down")), "b_scan": part(g("L1_cond_bias")),
    }
    def columns(e, s):
        mixed = g(e).reshape(E1, N, TE, LANES).transpose(2, 1, 0, 3).reshape(TE, NC, P, P)
        shared = g(s).reshape(NC, P, TS, P).transpose(2, 0, 1, 3)
        return np.concatenate([mixed, shared], 0).transpose(0, 2, 1, 3).reshape(TILES, P, N)
    down = np.concatenate([g("L1_ffn_Wd").reshape(E1, TE, LANES, N).transpose(1, 0, 2, 3).reshape(TE, P, N), g("L1_ffn_Sd").reshape(TS, P, N)], 0)
    a["w_tiles"] = np.concatenate([columns("L1_ffn_Wg", "L1_ffn_Sg"), columns("L1_ffn_Wu", "L1_ffn_Su"), down], 2)
    a["coupling"] = part(g("L1_cond_coupling").T)
    a["cond"] = part(g("cond_2048").T).reshape(P, W)
    a["w_router"] = part(np.concatenate([g("L1_ffn_Wr"), g("L1_ffn_Wsg")], 1))
    return {k: np.ascontiguousarray(v) for k, v in a.items()}


def kernel(**inputs):
    import numpy as _np
    import concourse.bacc as _bacc
    from concourse import mybir as _mybir
    from concourse.bass_utils import run_bass_kernel_spmd as _run

    nc = _bacc.Bacc("TRN2", target_bir_lowering=False, num_devices=1)
    arrays, dram = {}, {}
    for name, a in arranged(inputs, _np).items():
        arrays[f"in_{name}"] = a
        dram[name] = nc.dram_tensor(f"in_{name}", a.shape, _mybir.dt.from_np(a.dtype), kind="ExternalInput").ap()
    out = nc.dram_tensor("out", (P, NC, T, B), _mybir.dt.float32, kind="ExternalOutput").ap()
    build(nc, dram, out)
    r = _run(nc, [arrays], core_ids=[0])
    return r.results[0]["out"].transpose(3, 2, 1, 0).reshape(B, T, N)
```

```python
import concourse.bass as bass
from concourse import mybir
from contextlib import ExitStack

F32, F16, BF16, I32 = mybir.dt.float32, mybir.dt.float16, mybir.dt.bfloat16, mybir.dt.int32
ALU = mybir.AluOpType
ACT = mybir.ActivationFunctionType
AX = mybir.AxisListType
P = 128

E1, F1, FS = 8, 352, 1408
LANES = P // E1
TE = F1 // LANES
TS = FS // P
TILES = TE + TS
Q_BITS = 8
B, T, N = 8, 256, 512
NC = N // P
HEADS, DH = 16, 32
HPC = P // DH
H0 = 2048
HC = H0 // P
QBLOCK = 64
R = 16
PIECE = 1024
PIECES = 2 * NC * H0 // PIECE
DT, EPSILON, ALPHA, BETA, CLAMP = 0.01, 0.08, 0.7, 0.8, 20.0


def layer0(nc, dram, xs, wk, w_qkv, w_split):
    ctx = ExitStack()
    with ctx:
        sb = lambda n, s, d=F32: ctx.enter_context(nc.sbuf_tensor(n, s, d))
        sem = lambda n: ctx.enter_context(nc.semaphore(n))
        w_emb = sb("w_emb", [P, NC, 2 * N])
        early = w_emb[:].rearrange("p c n -> p (c n)")
        qk = early[:, 0:2 * NC * T].rearrange("p (c a t) -> p c a t", a=2, t=T)
        pr = early[:, 2048:3072].rearrange("p (u a t) -> p u a t", u=2, a=2)
        prT = early[:, 3072:4096].rearrange("p (u a t) -> p u a t", u=2, a=2)
        w_out = sb("w_out", [P, NC, N])
        w_up = sb("w_up", [P, NC, H0])
        w_dn = sb("w_dn", [P, HC, N])
        hid = sb("hid", [P, HC, T])
        staging = hid[:].rearrange("p a t -> p (a t)")
        codes = [staging[:, u * 2048:u * 2048 + PIECE].bitcast(I32) for u in range(2)]
        scales = [staging[:, u * 2048 + PIECE:u * 2048 + 2 * PIECE] for u in range(2)]
        work = sb("work", [P, 5 * NC * T])
        sq = work[:, 0:1024].rearrange("p (c t) -> p c t", c=NC)
        xn = work[:, 1024:2048].rearrange("p (c t) -> p c t", c=NC)
        sqh = work[:, 2048:3072].rearrange("p (u a t) -> p u a t", u=2, a=2)
        rh = work[:, 3072:4096].rearrange("p (u a t) -> p u a t", u=2, a=2)
        v = work[:, 4096:5120].rearrange("p (a n) -> p a n", a=2)
        vecs = sb("vecs", [P, 64])
        condT = vecs[:, 0:NC * B].rearrange("p (c b) -> p c b", b=B)
        b_emb, g_norm = vecs[:, 32:40], vecs[:, 40:44]
        b_up, b_dn, b_scan, g_q, g_k = vecs[:, 44:60], sb("b_dn", [P, NC]), sb("b_scan", [P, NC]), vecs[:, 60:61], vecs[:, 61:62]
        eps = vecs[:, 62:63]
        ones = sb("ones", [P, P])
        headones = sb("headones", [P, P])
        ident = sb("ident", [P, P])
        ss = sb("ss", [P, 2 * NC, B])
        amp = sb("amp", [P, NC, B])
        bias2 = sb("bias2", [P, NC])
        rs = sb("rs", [P, 2, T])
        nmax = sb("nmax", [P, 2, 2])
        psum_e = sb("psum_e", [P, HEADS, 2])
        rinv = sb("rinv", [P, HEADS, 2])
        late = sb("late", [P, 3 * NC * T])
        o = late[:, 0:1024].rearrange("p (a n) -> p a n", a=2)
        oT = late[:, 1024:2048].rearrange("p (c t) -> p c t", c=NC)
        x1 = late[:, 2048:3072].rearrange("p (c t) -> p c t", c=NC)
        lora_up, lora_dn = late[0:R, 0:N + H0], late[32:32 + R, 0:N + H0]
        half_in = [sb(f"half_in{a}", [P, N]) for a in range(2)]
        half_out = [sb(f"half_out{a}", [P, 2, N], F16) for a in range(2)]
        bank = [ctx.enter_context(nc.psum_tensor(f"l0bank{i}", [P, 512], F32)) for i in range(8)]
        G, Rb, Ob, D = bank[0:2], bank[2:4], bank[4:6], bank[6:8]
        names = ("x_in xs_in emb_in qkv_in wo_in lora vec_in coupling_in codes0 codes1 "
                 "eye gch mm_ss amps "
                 "p_nrm p_qk p_hr p_v p_s p_t p_pv p_ot p_wo p_up p_dn "
                 "a_sqx a_rstd a_sq a_hr a_v a_exp a_up "
                 "d_xn d_qk d_max d_pt d_o d_ot d_x1 d_x2 "
                 "chain achain seq plseq "
                 "mm_lora scaled stage "
                 "half_in0 half_in1 half_out0 half_out1 half_read half_split plmul summed gmax").split()
        S = {n: sem("l0_" + n) for n in names}
        block = ctx.enter_context(nc.Block())
        xv = xs[:, 0:NC * B * T].rearrange("p (c b t) -> p c b t", c=NC, b=B)
        codes_in = [S["codes0"], S["codes1"]]
        half_loaded, half_stored = [S["half_in0"], S["half_in1"]], [S["half_out0"], S["half_out1"]]
        RELUS = HC // 2

        ffn_norm, ffn_qk, ffn_last = [0, 1, 2], [3, 4], [29, 30, 31]
        ffn_heads, n = [], 5
        for h in range(HEADS):
            ffn_heads.append(list(range(n, n + 2 - h % 2)))
            n += 2 - h % 2
        assert n == ffn_last[0] and ffn_last[-1] == 2 * HC - 1

        @block.sync
        def _(sp):
            sp.dma_start(vecs[:, 0:62], dram["vecs"]).then_inc(S["vec_in"], 16)
            sp.dma_start(b_dn[:], dram["b_dn"]).then_inc(S["vec_in"], 16)
            sp.dma_start(b_scan[:], dram["b_scan"]).then_inc(S["vec_in"], 16)
            sp.dma_start(w_emb[:], dram["w_emb"]).then_inc(S["emb_in"], 16)
            sp.wait_ge(S["qkv_in"], 16)
            for half, factors in enumerate((lora_up, lora_dn)):
                sp.dma_start(factors, dram["lora"][half]).then_inc(S["lora"], 16)
            for h in range(PIECES):
                u = h % 2
                if h >= 2:
                    sp.wait_ge(S["stage"], h - 1)
                if h < PIECES // 2:
                    cols = slice(h % 2 * PIECE, h % 2 * PIECE + PIECE)
                    sp.dma_start(codes[u], dram["up_q"][:, h // 2, cols]).then_inc(codes_in[u], 16)
                    for half in range(2):
                        sp.dma_start(scales[u][half * 64:half * 64 + 64, :],
                                     dram["up_s"][2 * (h // 2) + half, cols].partition_broadcast(64)).then_inc(codes_in[u], 16)
                else:
                    hc = 2 * (h - PIECES // 2)
                    sp.dma_start(codes[u], dram["dn_q"][:, hc:hc + 2, :].rearrange("p a n -> p (a n)")).then_inc(codes_in[u], 16)
                    for a in range(2):
                        for half in range(2):
                            sp.dma_start(scales[u][half * 64:half * 64 + 64, a * N:(a + 1) * N],
                                         dram["dn_s"][2 * (hc + a) + half].partition_broadcast(64)).then_inc(codes_in[u], 16)
                if h == 1:
                    sp.dma_start(xv[:, :, 1:, :], dram["x"][:, :, 1:, :]).then_inc(S["xs_in"], 16)
                if h == 3:
                    sp.dma_start(w_out[:], dram["w_out"]).then_inc(S["wo_in"], 16)

            def load_half(tile, a, reads):
                sp.wait_ge(S["half_read"], reads)
                sp.sem_inc(S["seq"], 1)
                sp.dma_start(half_in[a][:], dram["w_tiles"][bass.ds(tile, 1), :, a * N:(a + 1) * N].rearrange("o p n -> (o p) n")).then_inc(half_loaded[a], 16)
            with sp.Fori(0, TILES) as tile:
                for a in range(2):
                    load_half(tile, a, 2 * tile + a + 1)
            with sp.Fori(0, TILES) as tile:
                for a in range(2):
                    load_half(tile, a, 2 * TILES + 2 * tile + a + 1)
                for a in range(2):
                    sp.wait_ge(S["half_split"], 2 * tile + a + 1)
                    sp.sem_inc(S["seq"], 1)
                    sp.dma_start(w_split[bass.ds(tile, 1), :, a * 2 * N:(a + 1) * 2 * N].rearrange("o p n -> (o p) n"),
                                 half_out[a][:].rearrange("p h n -> p (h n)")).then_inc(half_stored[a], 16)
            sp.wait_ge(S["p_v"], 2 * B)
            sp.dma_start(w_qkv[:, :, 0:N], dram["coupling"]).then_inc(S["coupling_in"], 16)
            sp.wait_ge(S["coupling_in"], 16)
            for a in range(2):
                sp.wait_ge(half_stored[a], 16 * TILES + 16)

        @block.gpsimd
        def _(pl):
            pl.sem_inc(S["half_read"], 2)
            for a in range(2):
                pl.sem_inc(half_stored[a], 16)
            pl.memset(ones[:], 1.0).then_inc(S["gch"], 1)
            pl.memset(ident[:], 0.0).then_inc(S["gch"], 1)
            pl.memset(headones[:], 1.0).then_inc(S["gch"], 1)
            pl.memset(eps, 1e-6).then_inc(S["gch"], 1)
            pl.wait_ge(S["gch"], 4)
            pl.affine_select(out=ident[:], in_=ident[:], compare_op=ALU.not_equal, fill=1.0, base=0,
                             pattern=[[-1, P]], channel_multiplier=1).then_inc(S["gch"], 1)
            hv = headones[:].rearrange("p (h d) -> p h d", d=DH)
            pl.affine_select(out=hv, in_=hv, compare_op=ALU.is_ge, fill=0.0, base=0,
                             pattern=[[-DH, HPC], [0, DH]], channel_multiplier=1).then_inc(S["gch"], 1)
            pl.wait_ge(S["gch"], 6)
            pl.affine_select(out=hv, in_=hv, compare_op=ALU.is_ge, fill=0.0, base=DH - 1,
                             pattern=[[DH, HPC], [0, DH]], channel_multiplier=-1).then_inc(S["eye"], 1)
            bound, size = half_out[0][:].rearrange("p h n -> p (h n)").bitcast(F32), half_out[1][:].rearrange("p h n -> p (h n)").bitcast(F32)
            pl.memset(bound, 0.0).then_inc(S["summed"], 1)
            with pl.Fori(0, TILES) as tile:
                for a in range(2):
                    n = 2 * tile + a
                    pl.wait_ge(half_loaded[a], 16 * tile + 16)
                    pl.wait_ge(S["summed"], n + 1)
                    pl.sem_inc(S["plseq"], 1)
                    pl.tensor_scalar(size, half_in[a][:], 0.0, 2.0, ALU.max, ALU.mult).then_inc(S["plmul"], 1)
                    pl.wait_ge(S["plmul"], n + 1)
                    pl.tensor_tensor(size, size, half_in[a][:], ALU.subtract).then_inc(S["half_read"], 1)
                    pl.wait_ge(S["half_read"], n + 3)
                    pl.tensor_tensor(bound, bound, size, ALU.add).then_inc(S["summed"], 1)
            pl.wait_ge(S["summed"], 2 * TILES + 1)
            steps = [0]
            def link(ins):
                steps[0] += 1
                ins.then_inc(S["gmax"], 1)
                pl.wait_ge(S["gmax"], steps[0])
            width = N // 2
            while width >= 1:
                one, other = bound[:, 0:width], bound[:, width:2 * width]
                link(pl.tensor_tensor(one, one, other, ALU.subtract))
                link(pl.tensor_scalar(one, one, 0.0, None, ALU.max))
                link(pl.tensor_tensor(one, one, other, ALU.add))
                width //= 2
            link(pl.tensor_copy(wk[:, 2:3], bound[:, 0:1]))
            link(pl.partition_all_reduce(wk[:, 2:3], wk[:, 2:3], P, bass.bass_isa.ReduceOp.max))
            link(pl.tensor_scalar(wk[:, 2:3], wk[:, 2:3], 2.0 ** -100, None, ALU.max))
            ki = wk[:].bitcast(I32)
            link(pl.tensor_scalar(ki[:, 2:3], ki[:, 2:3], 2.0 ** -23, None, ALU.mult))
            link(pl.tensor_scalar(ki[:, 0:1], ki[:, 2:3], -2.0 ** 23, float((254 + 13) << 23), ALU.mult, ALU.add))
            link(pl.tensor_scalar(ki[:, 1:2], ki[:, 2:3], 2.0 ** 23, float((13 + Q_BITS) << 23), ALU.mult, ALU.subtract))
            with pl.Fori(0, TILES) as tile:
                for a in range(2):
                    pl.wait_ge(half_loaded[a], 16 * (TILES + tile) + 16)
                    pl.wait_ge(half_stored[a], 16 * tile + 16)
                    pl.sem_inc(S["plseq"], 1)
                    pl.tensor_scalar(half_out[a][:, 0, :], half_in[a][:], wk[:, 0:1], None, ALU.mult)
                    pl.tensor_scalar(half_in[a][:], half_in[a][:], wk[:, 0:1], None, ALU.mult).then_inc(S["plmul"], 1)
                    pl.wait_ge(S["plmul"], 2 * TILES + 2 * tile + a + 1)
                    pl.tensor_tensor(half_out[a][:, 1, :], half_in[a][:], half_out[a][:, 0, :], ALU.subtract).then_inc(S["half_split"], 1)
                    pl.wait_ge(S["half_split"], 2 * tile + a + 1)
                    pl.sem_inc(S["half_read"], 1)

        @block.scalar
        def _(act):
            act.dma_start(xv[:, :, 0, :], dram["x"][:, :, 0, :]).then_inc(S["x_in"], 16)
            act.wait_ge(S["emb_in"], 16)
            act.dma_start(w_qkv[:], dram["w_qkv"]).then_inc(S["qkv_in"], 16)
            act.wait_ge(S["eye"], 1)
            act.wait_ge(S["vec_in"], 48)
            act.wait_ge(S["x_in"], 16)
            nc.scalar.preload_act_table_set("natural_log_exp_and_others")
            def relu(n, j):
                act.wait_ge(S["p_up"], n * RELUS + j + 1)
                for i in range(2):
                    ins = act.activation(hid[:, 2 * j + i, :], D[j % 2][:, i * T:(i + 1) * T], ACT.Relu, bias=b_up[:, 2 * j + i:2 * j + i + 1])
                ins.then_inc(S["a_up"], 1)

            def batch(b, ffn):
                act.activation(sq[:], xv[:, :, bass.ds(b, 1), :].rearrange("p c o t -> p c (o t)"), ACT.Square).then_inc(S["a_sqx"], 1)
                act.wait_ge(S["p_nrm"], b + 1)
                act.activation(rs[:, 0, :], Ob[0][:, 0:T], ACT.Ln, scale=1.0 / N, bias=eps).then_inc(S["achain"], 1)
                act.wait_ge(S["achain"], b * 5 + 1)
                act.activation(rs[:, 1, :], rs[:, 0, :], ACT.Exp, scale=-0.5).then_inc(S["a_rstd"], 1)
                def square(c):
                    act.wait_ge(S["p_qk"], b * NC + c + 1)
                    act.activation(sqh[:, c % 2], G[c % 2][:].rearrange("p (a t) -> p a t", a=2), ACT.Square).then_inc(S["a_sq"], 1)
                square(0)
                for c in range(NC):
                    if c + 1 < NC:
                        square(c + 1)
                    act.wait_ge(S["p_hr"], b * NC + c + 1)
                    act.activation(rh[:, c % 2], Rb[c % 2][:].rearrange("p (a t) -> p a t", a=2), ACT.Ln, scale=1.0 / DH, bias=eps).then_inc(S["achain"], 1)
                    act.wait_ge(S["achain"], b * 5 + 2 + c)
                    act.activation(rh[:, c % 2], rh[:, c % 2], ACT.Exp, scale=-0.5).then_inc(S["a_hr"], 1)
                    if ffn and c in (0, 2):
                        relu(b - 1, c // 2)
                for i in range(2):
                    act.wait_ge(S["p_v"], b * 2 + i + 1)
                    act.activation(v[:, i, :], Ob[i][:], ACT.Copy).then_inc(S["a_v"], 1)
                for h in range(HEADS):
                    if ffn and h:
                        for part in ffn_heads[h - 1]:
                            if part < HC and part % 2:
                                relu(b - 1, part // 2)
                    act.wait_ge(S["d_max"], b * HEADS + h + 1)
                    for qc in range(2):
                        ins = act.activation(pr[:, h % 2, qc, :], G[h % 2][:, qc * T:(qc + 1) * T], ACT.Exp,
                                             bias=nmax[:, h % 2, qc:qc + 1], accum_out=psum_e[:, h, qc:qc + 1])
                    ins.then_inc(S["a_exp"], 1)
            batch(0, False)
            act.wait_ge(S["xs_in"], 16)
            with act.Fori(1, B) as b:
                batch(b, True)
            for j in range(RELUS):
                relu(B - 1, j)

        @block.tensor
        def _(pe):
            mm = nc.tensor.matmul
            pe.wait_ge(S["emb_in"], 16)
            pe.wait_ge(S["vec_in"], 48)
            for m in range(2 * NC):
                for k in range(NC):
                    ins = mm(Ob[0][:, m * B:(m + 1) * B], w_emb[:, k, m * P:(m + 1) * P], condT[:, k, :], start=(k == 0), stop=(k == NC - 1))
            ins.then_inc(S["mm_ss"], 1)
            pe.wait_ge(S["eye"], 1)
            pe.wait_ge(S["qkv_in"], 16)
            pe.wait_ge(S["amps"], 1)

            def lora(h):
                if h == 0:
                    pe.wait_ge(S["lora"], 32)
                else:
                    pe.wait_ge(S["stage"], h)
                for i in range(2):
                    if h < PIECES // 2:
                        c, col = h // 2, N + h % 2 * PIECE + i * 512
                        a, bb = lora_up[:, c * P:(c + 1) * P], lora_up[:, col:col + 512]
                    else:
                        hc = 2 * (h - PIECES // 2) + i
                        a, bb = lora_dn[:, hc * P:(hc + 1) * P], lora_dn[:, H0:H0 + N]
                    ins = mm(D[i][:], a, bb, start=True, stop=True)
                ins.then_inc(S["mm_lora"], 1)

            def ffn_part(n, part):
                if part < HC:
                    j = part // 2
                    if part in (0, 2):
                        pe.wait_ge(S["d_x2"], 2 * n + 1 + part // 2)
                    if part % 2 == 0 and j >= 2:
                        pe.wait_ge(S["a_up"], n * RELUS + j - 1)
                    for k in range(NC):
                        ins = mm(D[j % 2][:, (part % 2) * T:(part % 2 + 1) * T], w_up[:, k, part * P:(part + 1) * P], x1[:, k, :], start=(k == 0), stop=(k == NC - 1))
                    if part % 2:
                        ins.then_inc(S["p_up"], 1)
                else:
                    m, quarter = (part - HC) // 4, (part - HC) % 4
                    if part == HC:
                        pe.wait_ge(S["a_up"], n * RELUS + RELUS)
                    for k in range(4 * quarter, 4 * quarter + 4):
                        ins = mm(D[m // 2][:, (m % 2) * T:(m % 2 + 1) * T], w_dn[:, k, m * P:(m + 1) * P], hid[:, k, :], start=(k == 0), stop=(k == HC - 1))
                    if m % 2 and quarter == 3:
                        ins.then_inc(S["p_dn"], 1)

            def batch(b, ffn):
                pe.wait_ge(S["a_sqx"], b + 1)
                for k in range(NC):
                    ins = mm(Ob[0][:, 0:T], ones[:], sq[:, k, :], start=(k == 0), stop=(k == NC - 1))
                ins.then_inc(S["p_nrm"], 1)
                if ffn:
                    pe.wait_ge(S["d_x1"], b * 2)
                    for part in ffn_norm:
                        ffn_part(b - 1, part)
                pe.wait_ge(S["d_xn"], b + 1)
                def head_norm(c):
                    pe.wait_ge(S["a_sq"], b * NC + c + 1)
                    if c >= 2:
                        pe.wait_ge(S["a_hr"], b * NC + c - 1)
                    mm(Rb[c % 2][:], headones[:], sqh[:, c % 2].rearrange("p a t -> p (a t)"), start=True, stop=True).then_inc(S["p_hr"], 1)
                for c in range(NC):
                    if c >= 2:
                        pe.wait_ge(S["d_qk"], b * NC + c - 1)
                    for a in range(2):
                        for k in range(NC):
                            ins = mm(G[c % 2][:, a * T:(a + 1) * T], w_qkv[:, k, a * N + c * P:a * N + (c + 1) * P], xn[:, k, :],
                                     start=(k == 0), stop=(k == NC - 1))
                    ins.then_inc(S["p_qk"], 1)
                    if c:
                        head_norm(c - 1)
                    if ffn and c in (1, 2):
                        ffn_part(b - 1, ffn_qk[c - 1])
                for i in range(2):
                    for k in range(NC):
                        ins = mm(Ob[i][:], xn[:, k, i * P:(i + 1) * P], w_qkv[:, k, 2 * N:3 * N], start=(k == 0), stop=(k == NC - 1))
                    ins.then_inc(S["p_v"], 1)
                    if i == 0:
                        head_norm(NC - 1)
                def scores(h):
                    c, r = h // HPC, DH * (h % HPC)
                    if h == 0:
                        pe.wait_ge(S["d_qk"], b * NC + NC)
                    if h >= 2:
                        pe.wait_ge(S["a_exp"], b * HEADS + h - 1)
                    for qc in range(2):
                        ins = mm(G[h % 2][:, qc * T:(qc + 1) * T], qk[r:r + DH, c, 0, qc * P:(qc + 1) * P], qk[r:r + DH, c, 1, :], start=True, stop=True)
                    ins.then_inc(S["p_s"], 1)
                def transposed(h):
                    pe.wait_ge(S["a_exp"], b * HEADS + h + 1)
                    if h >= 2:
                        pe.wait_ge(S["d_pt"], b * HEADS + h - 1)
                    for kc in range(2):
                        for qc in range(2):
                            ins = nc.tensor.transpose(Rb[h % 2][:, kc * T + qc * P:kc * T + (qc + 1) * P], pr[:, h % 2, qc, kc * P:(kc + 1) * P], ident[:])
                    ins.then_inc(S["p_t"], 1)
                def weighted(h):
                    pe.wait_ge(S["d_pt"], b * HEADS + h + 1)
                    if h == 0:
                        pe.wait_ge(S["a_v"], b * 2 + 2)
                    for qc in range(2):
                        for kc in range(2):
                            ins = mm(Ob[qc][:, h * DH:(h + 1) * DH], prT[:, h % 2, kc, qc * P:(qc + 1) * P], v[:, kc, h * DH:(h + 1) * DH],
                                     start=(kc == 0), stop=(kc == 1))
                    if h == HEADS - 1:
                        ins.then_inc(S["p_pv"], 1)
                scores(0)
                for h in range(HEADS):
                    if h + 1 < HEADS:
                        scores(h + 1)
                    if ffn:
                        for part in ffn_heads[h]:
                            ffn_part(b - 1, part)
                    else:
                        lora(h)
                    transposed(h)
                    if h:
                        weighted(h - 1)
                weighted(HEADS - 1)
                if ffn:
                    for part in ffn_last[:2]:
                        ffn_part(b - 1, part)
                else:
                    pe.wait_ge(S["stage"], PIECES)
                pe.wait_ge(S["d_o"], b + 1)
                for i in range(2):
                    for c in (2 * i, 2 * i + 1):
                        for qc in range(2):
                            ins = nc.tensor.transpose(G[i][:, (c % 2) * T + qc * P:(c % 2) * T + (qc + 1) * P], o[:, qc, c * P:(c + 1) * P], ident[:])
                    ins.then_inc(S["p_ot"], 1)
                if not ffn:
                    pe.wait_ge(S["wo_in"], 16)
                if ffn:
                    ffn_part(b - 1, ffn_last[2])
                pe.wait_ge(S["d_ot"], b * 2 + 2)
                for m in range(NC):
                    for k in range(NC):
                        ins = mm(Rb[m // 2][:, (m % 2) * T:(m % 2 + 1) * T], w_out[:, k, m * P:(m + 1) * P], oT[:, k, :], start=(k == 0), stop=(k == NC - 1))
                    if m % 2:
                        ins.then_inc(S["p_wo"], 1)
            batch(0, False)
            with pe.Fori(1, B) as b:
                batch(b, True)
            pe.wait_ge(S["d_x1"], 2 * B)
            for part in range(2 * HC):
                ffn_part(B - 1, part)

        @block.vector
        def _(dve):
            count = [0]
            def link(ins, at=None):
                count[0] += 1
                ins.then_inc(S["chain"], 1)
                dve.wait_ge(S["chain"], count[0] if at is None else at + count[0])
            dve.sem_inc(S["d_x2"], 2)
            dve.wait_ge(S["vec_in"], 48)
            dve.wait_ge(S["mm_ss"], 1)
            link(dve.tensor_tensor(ss[:], Ob[0][:, 0:2 * NC * B].rearrange("p (m b) -> p m b", b=B), b_emb.unsqueeze(2).to_broadcast([P, 2 * NC, B]), ALU.add))
            link(dve.scalar_tensor_tensor(amp[:], ss[:, 0:NC, :], 1.0, g_norm.unsqueeze(2).to_broadcast([P, NC, B]), ALU.add, ALU.mult))
            link(dve.tensor_scalar(bias2[:], b_scan[:], ALPHA / BETA, None, ALU.subtract))
            link(dve.tensor_tensor(bias2[:], bias2[:], b_dn[:], ALU.add))
            dve.scalar_tensor_tensor(g_q, g_q, DH ** -0.5, g_k, ALU.mult, ALU.mult).then_inc(S["amps"], 1)
            base = count[0]
            KD = 2

            def restore(h):
                u = h % 2
                dmas = [3 if n < PIECES // 2 else 5 for n in range(PIECES)]
                dve.wait_ge(codes_in[u], 16 * sum(dmas[u:h + 1:2]))
                dve.scalar_tensor_tensor(scales[u], codes[u], 7.5, scales[u], ALU.subtract, ALU.mult).then_inc(S["scaled"], 1)
                dve.wait_ge(S["mm_lora"], h + 1)
                dve.wait_ge(S["scaled"], h + 1)
                for i in range(2):
                    if h < PIECES // 2:
                        dst = w_up[:, h // 2, h % 2 * PIECE + i * 512:h % 2 * PIECE + (i + 1) * 512]
                    else:
                        dst = w_dn[:, 2 * (h - PIECES // 2) + i, :]
                    ins = dve.tensor_tensor(dst, D[i][:], scales[u][:, i * 512:(i + 1) * 512], ALU.add)
                ins.then_inc(S["stage"], 1)

            def second(n, i):
                dve.wait_ge(S["p_dn"], n * 2 + i + 1)
                for c in (2 * i, 2 * i + 1):
                    slot = xv[:, c, bass.ds(n, 1), :].rearrange("p o t -> p (o t)")
                    ins = dve.scalar_tensor_tensor(slot, D[i][:, (c % 2) * T:(c % 2 + 1) * T], bias2[:, c:c + 1], slot, ALU.add, ALU.add)
                ins.then_inc(S["d_x2"], 1)

            def batch(b, ffn):
                count[0] = 0
                at = base + b * KD
                xb = xv[:, :, bass.ds(b, 1), :].rearrange("p c o t -> p c (o t)")
                dve.wait_ge(S["a_rstd"], b + 1)
                link(dve.tensor_tensor(xn[:], xb, rs[:, 1:2, :].to_broadcast([P, NC, T]), ALU.mult), at)
                for c in range(NC):
                    ins = dve.tensor_scalar(xn[:, c, :], xn[:, c, :], amp[:, c, bass.ds(b, 1)], ss[:, NC + c, bass.ds(b, 1)], ALU.mult, ALU.add)
                ins.then_inc(S["d_xn"], 1)
                for c in range(NC):
                    dve.wait_ge(S["a_hr"], b * NC + c + 1)
                    dve.scalar_tensor_tensor(qk[:, c, 0, :], G[c % 2][:, 0:T], g_q, rh[:, c % 2, 0, :], ALU.mult, ALU.mult)
                    dve.tensor_tensor(qk[:, c, 1, :], G[c % 2][:, T:2 * T], rh[:, c % 2, 1, :], ALU.mult).then_inc(S["d_qk"], 1)
                def row_max(h):
                    dve.wait_ge(S["p_s"], b * HEADS + h + 1)
                    dve.tensor_reduce(nmax[:, h % 2, :], G[h % 2][:].rearrange("p (a t) -> p a t", a=2), AX.X, ALU.max, negate=True).then_inc(S["d_max"], 1)
                row_max(0)
                for h in range(HEADS):
                    if h + 1 < HEADS:
                        if h >= 1:
                            dve.wait_ge(S["a_exp"], b * HEADS + h)
                        row_max(h + 1)
                    dve.wait_ge(S["p_t"], b * HEADS + h + 1)
                    dve.tensor_copy(prT[:, h % 2].rearrange("p a t -> p (a t)"), Rb[h % 2][:]).then_inc(S["d_pt"], 1)
                    if not ffn:
                        restore(h)
                    elif h == HEADS - 2:
                        second(b - 1, 0)
                dve.wait_ge(S["a_exp"], (b + 1) * HEADS)
                link(dve.reciprocal(rinv[:], psum_e[:]), at)
                dve.wait_ge(S["p_pv"], b + 1)
                for qc in range(2):
                    ins = dve.tensor_tensor(o[:, qc, :].rearrange("p (h d) -> p h d", d=DH), Ob[qc][:].rearrange("p (h d) -> p h d", d=DH),
                                            rinv[:, :, qc:qc + 1].to_broadcast([P, HEADS, DH]), ALU.mult)
                ins.then_inc(S["d_o"], 1)
                for i in range(2):
                    dve.wait_ge(S["p_ot"], b * 2 + i + 1)
                    dve.tensor_copy(oT[:, 2 * i:2 * i + 2, :].rearrange("p a t -> p (a t)"), G[i][:]).then_inc(S["d_ot"], 1)
                for i in range(2):
                    dve.wait_ge(S["p_wo"], b * 2 + i + 1)
                    if i == 0:
                        dve.wait_ge(S["d_ot"], b * 2 + 2)
                    dve.tensor_tensor(x1[:, 2 * i:2 * i + 2, :].rearrange("p a t -> p (a t)"), Rb[i][:], oT[:, 2 * i:2 * i + 2, :].rearrange("p a t -> p (a t)"), ALU.add).then_inc(S["d_x1"], 1)
                if ffn:
                    second(b - 1, 1)
                assert count[0] == KD

            batch(0, False)
            with dve.Fori(1, B) as b:
                batch(b, True)
            for i in range(2):
                second(B - 1, i)


G = 32
NG = T // G
GT = G * B
W = NC * B
RK = [DT / 2, DT / 2, DT, DT / 6]
SHIFT = 2.0 ** 13


def linear_terms():
    import numpy as np
    q, p, d, q2, q3, q4 = np.eye(6)
    e = EPSILON * BETA
    p2 = p + DT / 2 * e * (q - p)
    p3 = p + DT / 2 * e * (q2 - p2)
    p4 = p + DT * e * (q3 - p3)
    rows = [q + RK[0] * (d - p / BETA), q + RK[1] * (d - p2 / BETA), q + RK[2] * (d - p3 / BETA),
            (-q + q2 + 2 * q3 + q4) / 3 + RK[3] * (d - p4 / BETA),
            (-p + p2 + 2 * p3 + p4) / 3 + RK[3] * e * (q4 - p4)]
    return np.array(rows)


def layer1(nc, dram, xs, wk, cT, w_split, out):
    ctx = ExitStack()
    with ctx:
        sb = lambda n, s, d=F32: ctx.enter_context(nc.sbuf_tensor(n, s, d))
        sem = lambda n: ctx.enter_context(nc.semaphore(n))
        chi = sb("chi", [P, NC, N], F16)
        clo = sb("clo", [P, NC, N], F16)
        kp = sb("kp", [P, 12])
        b_scan = sb("b_scan1", [P, NC])
        unshift = sb("unshift", [P, NC])
        state = [sb(f"state{s}", [P, W]) for s in range(4)]
        qraw = sb("qraw", [P, W])
        pst = sb("pst", [P, W])
        th = sb("th", [P, NC, 2, B], F16)
        t32 = sb("t32", [P, W])
        sq = sb("sq1", [P, W]); cub = sb("cub", [P, W])
        cq, cp, cd = (sb(n, [P, 5, W]) for n in ("coef_q", "coef_p", "coef_d"))
        c2 = sb("coef2", [P, 3, W]); c3 = sb("coef3", [P, 2, W]); c4 = sb("coef4", [P, 2, W])
        A = [sb(f"lin{u}", [P, 5, W]) for u in range(2)]
        md, mp_ = (sb(n, [P, 5, W]) for n in ("from_drive", "from_p"))
        mq = sb("from_q", [P, 4, W])
        ms, ms3, ms4 = (sb(n, [P, r, W]) for n, r in (("from_q2", 3), ("from_q3", 2), ("from_q4", 2)))
        zeros = sb("zeros", [P, 512], BF16)
        trace = sb("trace", [P, NC, G, B])
        qg = sb("qg", [P, NC, GT])
        qh = sb("qh", [P, 2, NC, GT], F16)
        wgu = sb("wgu", [P, 2, 2, 2, NC, P], F16)
        wd = sb("wd", [P, 2, N])
        wr = sb("wr", [P, NC, E1 + 1])
        ident = sb("ident1", [P, P])
        lanes = sb("lanes", [P, E1])
        rt = sb("rt", [P, 2, E1 + 1]); top = sb("top", [P, 2, 8]); topi = sb("topi", [P, 2, 8], mybir.dt.uint32); topf = sb("topf", [P, 2, 8])
        ex = sb("ex", [P, 2, E1 + 1]); es = sb("es", [P, 2, 4]); msk = sb("msk", [P, 2, 2, E1]); wide = sb("wide", [P, 2, 2, P])
        neg = sb("neg", [P, 2])
        gates = sb("gates", [P, 2, GT])
        sg = sb("sg", [P, GT]); ha = sb("ha", [P, GT]); hb = sb("hb", [P, GT]); hg = sb("hg", [P, 2, GT])
        oo = sb("oo", [P, NC, G, B])
        pscan = ctx.enter_context(nc.psum_tensor("pscan", [P, 2, 512 // W, W], F32))
        pg = ctx.enter_context(nc.psum_tensor("pg", [P, 512], F32))
        pu = ctx.enter_context(nc.psum_tensor("pu", [P, 512], F32))
        pd = [ctx.enter_context(nc.psum_tensor(f"pd{i}", [P, 512], F32)) for i in range(2)]
        pr_ = ctx.enter_context(nc.psum_tensor("prouter", [P, 512], F32))
        names = ("vin eye par mx scale_rdy coef "
                 "th_ready t32_ready sq_ready tl_ready ic_ready q_ready clip_ready pclip_ready lin_ready e_ready "
                 "traced copied q_high q_low "
                 "wg0 wg1 wd0 wd1 gate_done up_done dn_done sg_ready ha_ready hb_ready hid_ready "
                 "out_ready stored "
                 "rt_mm rt_max rt_exp rt_wide rt_tr "
                 "dchain pchain rchain spseq plseq dveseq").split()
        S = {n: sem("l1_" + n) for n in names}
        wsem = [S["wg0"], S["wg1"]]; dsem = [S["wd0"], S["wd1"]]
        block = ctx.enter_context(nc.Block())
        v3 = lambda ap: ap.rearrange("p (c b) -> p c b", b=B)
        xv = xs[:, 0:NC * B * T].rearrange("p (c b t) -> p c b t", c=NC, b=B)
        def drive(t):
            return xs[:, bass.ds(t, NC * B * T)].rearrange("p (c b t) -> p c b t", c=NC, b=B)[:, :, :, 0]
        coefs = linear_terms()

        def walk(eng, step, last_tile):
            with eng.Fori(0, G // 2) as i:
                for u in range(2):
                    step(None, i, u, 2 * i + u, True, False, False)

            def group(seg, scan, old):
                if old:
                    last_tile(seg - 1)
                for i in range(2):
                    for u in range(2):
                        step(seg, i, u, G + seg * G + 2 * i + u, scan, True, old)
                with eng.Fori(2, G // 2) as i:
                    for u in range(2):
                        step(seg, i, u, G + seg * G + 2 * i + u, scan, True, old)
            group(0, True, False)
            with eng.Fori(1, NG - 1) as seg:
                group(seg, True, True)
            group(NG - 1, False, True)
            last_tile(NG - 1)

        def gate_row(i, u):
            return (i * 3) // 32 if u else (i * 3 - 3) // 32

        @block.sync
        def _(sp):
            sp.dma_start(b_scan[:], dram["b_scan"]).then_inc(S["vin"], 16)
            sp.dma_start(wr[:], dram["w_router"]).then_inc(S["vin"], 16)
            sp.dma_start(state[0][:], dram["cond"]).then_inc(S["vin"], 16)
            sp.dma_start(qraw[:], dram["cond"]).then_inc(S["vin"], 16)

            def load_up(tile, slot, done):
                sp.wait_ge(S["up_done"], done)
                sp.sem_inc(S["spseq"], 1)
                sp.dma_start(wgu[:, slot].rearrange("p a h c f -> p (a h c f)"),
                             w_split[bass.ds(tile, 1), :, :].rearrange("o p n -> (o p) n")).then_inc(wsem[slot], 16)

            def load_down(tile, slot, done):
                sp.wait_ge(S["dn_done"], done)
                sp.sem_inc(S["spseq"], 1)
                sp.dma_start(wd[:, slot, :],
                             dram["w_tiles"][bass.ds(tile, 1), :, 2 * N:3 * N].rearrange("o p n -> (o p) n")).then_inc(dsem[slot], 16)

            def store(seg):
                sp.wait_ge(S["out_ready"], seg * NC + NC)
                sp.sem_inc(S["spseq"], 1)
                sp.dma_start(out[:, :, bass.ds(seg * G, G), :], oo[:]).then_inc(S["stored"], 16)

            def group(seg, old):
                done = seg * TILES + 2
                load_up(0, 0, done)
                load_up(1, 1, done - 1)
                load_down(1, 1, done - 1)
                load_down(0, 0, done)
                load_up(2, 0, done + 1)
                if old:
                    store(seg - 1)
                load_up(3, 1, done + 2)
                load_down(2, 0, done + 1)
                with sp.Fori(2, G // 2) as i:
                    for u in range(2):
                        load_up(2 * i + u, u, done + 2 * i + u - 1)
                        load_down(2 * i + u - 1, 1 - u, done + 2 * i + u - 2)
                load_up(TILES - 1, 0, done + TILES - 2)
                load_down(TILES - 2, 1, done + TILES - 3)
                load_down(TILES - 1, 0, done + TILES - 2)
            group(0, False)
            with sp.Fori(1, NG) as seg:
                group(seg, True)
            store(NG - 1)
            sp.wait_ge(S["stored"], 16 * (NG + 1))

        @block.gpsimd
        def _(pl):
            pl.memset(ident[:], 0.0).then_inc(S["eye"], 1)
            pl.wait_ge(S["eye"], 1)
            pl.affine_select(out=ident[:], in_=ident[:], compare_op=ALU.not_equal, fill=1.0, base=0,
                             pattern=[[-1, P]], channel_multiplier=1).then_inc(S["eye"], 1)
            for e in range(E1):
                pl.memset(lanes[:, e:e + 1], float(e))
            for r in range(5):
                unit = RK[r] if r < 4 else 1.0
                pl.memset(cq[:, r, :], float(coefs[r, 0] * RK[3] / unit))
                for tile, col in ((cp, 1), (cd, 2)):
                    pl.memset(tile[:, r, :], float(coefs[r, col] / unit))
                if r >= 2:
                    pl.memset(c2[:, r - 2, :], float(coefs[r, 3] * RK[0] / unit))
                if r >= 3:
                    pl.memset(c3[:, r - 3, :], float(coefs[r, 4] * RK[1] / unit))
                    pl.memset(c4[:, r - 3, :], float(coefs[r, 5] * RK[2] / unit))
            pl.memset(xs[:, NC * B * T:], 0.0)
            pl.memset(zeros[:], 0.0).then_inc(S["coef"], 1)
            pl.wait_ge(S["mx"], 1)
            pl.partition_all_reduce(kp[:, 1:2], kp[:, 0:1], P, bass.bass_isa.ReduceOp.max).then_inc(S["par"], 1)
            pl.wait_ge(S["coef"], 1)
            rows = lambda ap, n: ap.unsqueeze(1).to_broadcast([P, n, W])
            K = 7

            def next_linear(t, u, k, at, pclips):
                dv = drive(t).unsqueeze(1).to_broadcast([P, 5, NC, B])
                pl.tensor_tensor(md[:].rearrange("p r (c b) -> p r c b", b=B), dv, cd[:].rearrange("p r (c b) -> p r c b", b=B), ALU.mult).then_inc(S["pchain"], 1)
                pl.wait_ge(S["pclip_ready"], pclips)
                pl.tensor_tensor(mp_[:], rows(pst[:], 5), cp[:], ALU.mult).then_inc(S["pchain"], 1)
                pl.wait_ge(S["pchain"], at + k + 2)
                pl.tensor_tensor(A[u][:], md[:], mp_[:], ALU.add).then_inc(S["lin_ready"], 1)
                pl.wait_ge(S["lin_ready"], t + 1)
                pl.sem_inc(S["plseq"], 1)
            pl.wait_ge(S["scale_rdy"], 1)
            next_linear(0, 0, 0, 0, 1)

            def step(seg, i, u, t, scan, tile, old):
                if not scan:
                    return
                at = 2 + t * K
                pl.wait_ge(S["clip_ready"], t + 1)
                pl.tensor_tensor(mq[:], rows(state[0][:], 4), cq[:, 1:5, :], ALU.mult).then_inc(S["pchain"], 1)
                pl.wait_ge(S["pchain"], at + 1)
                pl.tensor_tensor(A[u][:, 1:5, :], A[u][:, 1:5, :], mq[:], ALU.add).then_inc(S["e_ready"], 1)
                pl.wait_ge(S["q_ready"], t * 4 + 2)
                pl.tensor_tensor(ms[:], rows(state[1][:], 3), c2[:], ALU.mult).then_inc(S["pchain"], 1)
                pl.wait_ge(S["e_ready"], t * 3 + 1)
                pl.sem_inc(S["plseq"], 1)
                pl.wait_ge(S["pchain"], at + 2)
                pl.tensor_tensor(A[u][:, 2:5, :], A[u][:, 2:5, :], ms[:], ALU.add).then_inc(S["e_ready"], 1)
                pl.wait_ge(S["q_ready"], t * 4 + 3)
                pl.tensor_tensor(ms3[:], rows(state[2][:], 2), c3[:], ALU.mult).then_inc(S["pchain"], 1)
                pl.wait_ge(S["e_ready"], t * 3 + 2)
                pl.sem_inc(S["plseq"], 1)
                pl.wait_ge(S["pchain"], at + 3)
                pl.tensor_tensor(A[u][:, 3:5, :], A[u][:, 3:5, :], ms3[:], ALU.add).then_inc(S["pchain"], 1)
                pl.wait_ge(S["q_ready"], t * 4 + 4)
                pl.sem_inc(S["plseq"], 1)
                pl.wait_ge(S["pchain"], at + 4)
                pl.tensor_tensor(ms4[:], rows(state[3][:], 2), c4[:], ALU.mult).then_inc(S["pchain"], 1)
                pl.wait_ge(S["pchain"], at + 5)
                pl.tensor_tensor(A[u][:, 3:5, :], A[u][:, 3:5, :], ms4[:], ALU.add).then_inc(S["e_ready"], 1)
                pl.wait_ge(S["e_ready"], t * 3 + 3)
                pl.sem_inc(S["plseq"], 1)
                next_linear(t + 1, 1 - u, 5, at, t + 2)
            walk(pl, step, lambda seg: None)

        @block.scalar
        def _(act):
            nc.scalar.preload_act_table_set("exp_and_others")
            act.wait_ge(S["scale_rdy"], 1)

            def step(seg, i, u, t, scan, tile, old):
                for s in range(4):
                    if scan:
                        src = qraw if s == 0 else state[s]
                        act.wait_ge(S["q_ready"], t * 4 + s + 1)
                        unit = kp[:, 7:8] if s == 0 else kp[:, 3 + s:4 + s]
                        act.activation(th[:, :, 0, :], v3(src[:]), ACT.Tanh, scale=unit).then_inc(S["th_ready"], 1)
                        act.activation(t32[:], src[:], ACT.Tanh, scale=unit).then_inc(S["t32_ready"], 1)
                        if s == 0:
                            act.wait_ge(S["clip_ready"], t + 1)
                        act.activation(sq[:], state[s][:], ACT.Square, scale=unit).then_inc(S["sq_ready"], 1)
                    if tile:
                        at = (i, u, s) if isinstance(i, int) else None
                        if at == (0, 0, 0):
                            act.wait_ge(S["traced"], seg * G + G)
                            act.activation(qg[:], trace[:].rearrange("p c t b -> p c (t b)"), ACT.Identity, scale=kp[:, 7:8]).then_inc(S["copied"], 1)
                        elif at == (0, 0, 1):
                            act.wait_ge(S["up_done"], seg * TILES + 2)
                            act.activation(qh[:, 0], trace[:].rearrange("p c t b -> p c (t b)"), ACT.Identity, scale=kp[:, 10:11]).then_inc(S["q_high"], 1)
                        elif at == (0, 1, 0):
                            act.wait_ge(S["rt_max"], seg + 1)
                            for c in range(2):
                                act.activation(ex[:, c, 0:E1], rt[:, c, 0:E1], ACT.Exp, bias=neg[:, c:c + 1], accum_out=es[:, c, 0:1])
                                ins = act.activation(ex[:, c, E1:E1 + 1], rt[:, c, E1:E1 + 1], ACT.Exp, scale=-1.0)
                            ins.then_inc(S["rt_exp"], 1)
                        if at == (0, 1, 1):
                            silu(seg * TILES)
                        elif at == (0, 1, 3):
                            silu(seg * TILES + 1)
                        elif s == 2 and (at is None or at[0] > 0):
                            silu(seg * TILES + 2 * i + u)

            def silu(n):
                act.wait_ge(S["gate_done"], n + 1)
                act.activation(sg[:], pg[:, 0:GT], ACT.Tanh, scale=wk[:, 3:4]).then_inc(S["sg_ready"], 1)
            walk(act, step, lambda seg: silu(seg * TILES + TILES - 1))

        @block.tensor
        def _(pe):
            mm = nc.tensor.matmul
            pe.wait_ge(S["eye"], 2)
            pe.wait_ge(S["vin"], 64)
            pe.wait_ge(S["scale_rdy"], 1)
            pe.wait_ge(S["coef"], 1)
            pe.sem_inc(S["up_done"], 2)
            pe.sem_inc(S["dn_done"], 2)

            def split_product(dst, slot, a, ks):
                for k in ks:
                    for w, q in ((0, 0), (0, 1), (1, 0)):
                        ins = mm(dst[:, 0:GT], wgu[:, slot, a, w, k, :], qh[:, q, k, :],
                                 start=(k == 0 and w == q), stop=(k == NC - 1 and w == 1))
                return ins

            def gate(slot, n, ks):
                if 0 in ks:
                    pe.wait_ge(wsem[slot], 16 * loads(slot, n))
                    pe.wait_ge(S["ha_ready"], n[0] * TILES + n[1] + 1)
                    pe.wait_ge(S["q_low"], 2 * n[0] + 2)
                ins = split_product(pg, slot, 0, ks)
                if NC - 1 in ks:
                    ins.then_inc(S["gate_done"], 1)

            def up(slot, n, ks):
                if 0 in ks:
                    pe.wait_ge(S["hb_ready"], n[0] * TILES + n[1] + 1)
                ins = split_product(pu, slot, 1, ks)
                if NC - 1 in ks:
                    ins.then_inc(S["up_done"], 1)

            def down(slot, seg, j, dloads, ms_):
                if 0 in ms_:
                    pe.wait_ge(S["hid_ready"], seg * TILES + j + 1)
                    pe.wait_ge(dsem[slot], dloads)
                for m in ms_:
                    ins = mm(pd[m // 2][:, (m % 2) * GT:(m % 2 + 1) * GT], wd[:, slot, m * P:(m + 1) * P], hg[:, slot, :],
                             start=False, stop=False, skip_group_check=True)
                if NC - 1 in ms_:
                    ins.then_inc(S["dn_done"], 1)

            def loads(slot, n):
                seg, i = n[0], n[2]
                return seg * (17 if slot == 0 else 16) + i + 1

            def down_loads(u, seg, i):
                return 16 * (seg * 17 + i + 1) if u else 16 * (seg * 16 + i)

            def step(seg, i, u, t, scan, tile, old):
                if tile:
                    n = (seg, 2 * i + u, i)
                    def part(j, ms_):
                        g = seg if j < G // 2 else seg - 1
                        down(j % 2, g, j, down_loads((j + 1) % 2, g, (j + 1) // 2), ms_)
                    slots = [lambda: (down(u, seg, 2 * i + u - 2, None, [3]), gate(u, n, [0, 1])),
                             lambda: (gate(u, n, [2, 3]), up(u, n, [0])),
                             lambda: (up(u, n, [1, 2]), down(1 - u, seg, 2 * i + u - 1, down_loads(u, seg, i), [0])),
                             lambda: (up(u, n, [3]), down(1 - u, seg, 2 * i + u - 1, None, [1, 2]))]
                    if isinstance(i, int) and (i, u) == (0, 0):
                        slots = [lambda: (part(TILES - 3, [3]), part(TILES - 2, [0, 1])) if old else None,
                                 lambda: (part(TILES - 2, [2, 3]) if old else None, route(seg, 0)),
                                 lambda: (route(seg, 1), part(TILES - 1, [0]) if old else None),
                                 lambda: part(TILES - 1, [1, 2, 3]) if old else None]
                    elif isinstance(i, int) and (i, u) == (0, 1):
                        slots = [lambda: gate(0, (seg, 0, 0), [0, 1, 2, 3]),
                                 lambda: up(0, (seg, 0, 0), [0, 1, 2, 3]),
                                 lambda: (spread_gates(seg), gate(1, n, [0, 1, 2, 3])),
                                 lambda: up(1, n, [0, 1, 2, 3])]
                    elif isinstance(i, int) and (i, u) == (1, 0):
                        slots[0] = lambda: (clear(seg, old), part(0, [0, 1]), gate(0, n, [0, 1]))
                        slots[1] = lambda: (part(0, [2, 3]), gate(0, n, [2, 3]), up(0, n, [0]))
                for s in range(4):
                    if scan:
                        pe.wait_ge(S["th_ready"], t * 4 + s + 1)
                        for m in range(NC):
                            for k in range(NC):
                                mm(pscan[:, 0, 0, m * B:(m + 1) * B], clo[:, k, m * P:(m + 1) * P], th[:, k, 0, :], start=(m == 0 and k == 0), stop=False, skip_group_check=True)
                        pe.wait_ge(S["tl_ready"], t * 4 + s + 1)
                        for m in range(NC):
                            for k in range(NC):
                                ins = mm(pscan[:, 0, 0:2, m * B:(m + 1) * B], chi[:, k, m * P:(m + 1) * P], th[:, k],
                                         start=False, stop=(k == NC - 1), skip_group_check=True)
                        ins.then_inc(S["ic_ready"], 1)
                    if tile:
                        slots[s]()

            def route(seg, c):
                if c == 0:
                    pe.wait_ge(S["copied"], seg + 1)
                for k in range(NC):
                    ins = mm(pr_[:, 16 * c:16 * c + E1 + 1], qg[:, k, c * P:(c + 1) * P], wr[:, k, :], start=(k == 0), stop=(k == NC - 1))
                if c:
                    ins.then_inc(S["rt_mm"], 1)

            def spread_gates(seg):
                pe.wait_ge(S["rt_wide"], seg + 1)
                for r in range(2):
                    for c in range(2):
                        ins = nc.tensor.transpose(pr_[:, r * GT + c * P:r * GT + (c + 1) * P], wide[:, c, r, :], ident[:])
                ins.then_inc(S["rt_tr"], 1)

            def clear(seg, old):
                if old:
                    pe.wait_ge(S["out_ready"], seg * NC)
                for i in range(2):
                    mm(pd[i][:], zeros[:, 0:P], zeros[:], start=True, stop=False, skip_group_check=True)

            def last_tile(seg):
                n = (seg, TILES - 1, 16)
                gate(0, n, [0, 1, 2, 3])
                up(0, n, [0, 1, 2, 3])
            walk(pe, step, last_tile)
            down(0, NG - 1, TILES - 3, None, [3])
            down(1, NG - 1, TILES - 2, down_loads(0, NG - 1, 16), [0, 1, 2, 3])
            down(0, NG - 1, TILES - 1, down_loads(1, NG - 1, 16), [0, 1, 2, 3])

        @block.vector
        def _(dve):
            setup = [0]
            def link(ins, wait=True):
                setup[0] += 1
                ins.then_inc(S["rchain"], 1)
                if wait:
                    dve.wait_ge(S["rchain"], setup[0])
            dve.tensor_reduce(kp[:, 0:1], cT, AX.XY, ALU.max, apply_absolute_value=True).then_inc(S["mx"], 1)
            dve.wait_ge(S["par"], 1)
            link(dve.tensor_scalar(kp[:, 1:2], kp[:, 1:2], 2.0 ** -60, None, ALU.max))
            ki = kp[:].bitcast(I32)
            link(dve.tensor_scalar(ki[:, 2:3], ki[:, 1:2], 0x7F800000, None, ALU.bitwise_and))
            link(dve.reciprocal(kp[:, 3:4], kp[:, 2:3]))
            link(dve.tensor_scalar(kp[:, 3:4], kp[:, 3:4], SHIFT, None, ALU.mult))
            for s in range(4):
                link(dve.tensor_scalar(kp[:, 4 + s:5 + s], kp[:, 2:3], RK[s] / SHIFT, None, ALU.mult), s == 3)
            link(dve.tensor_scalar(kp[:, 8:9], kp[:, 3:4], CLAMP / RK[3], None, ALU.mult), False)
            link(dve.tensor_scalar(kp[:, 9:10], kp[:, 3:4], -CLAMP / RK[3], None, ALU.mult), False)
            link(dve.tensor_scalar(kp[:, 10:11], kp[:, 7:8], 2.0 ** Q_BITS, None, ALU.mult), False)
            link(dve.tensor_scalar(kp[:, 11:12], kp[:, 2:3], 1 / SHIFT, None, ALU.mult))
            link(dve.tensor_scalar(chi[:], cT, kp[:, 3:4], None, ALU.mult))
            link(dve.scalar_tensor_tensor(clo[:], cT, kp[:, 3:4], chi[:], ALU.mult, ALU.subtract))
            dve.wait_ge(S["coef"], 1)
            for tile in (cp, cd):
                link(dve.tensor_scalar(tile[:, 0:4, :], tile[:, 0:4, :], kp[:, 3:4], None, ALU.mult), False)
            for tile, row in ((cq, 4), (c2, 2), (c3, 1), (c4, 1)):
                link(dve.tensor_scalar(tile[:, row, :], tile[:, row, :], kp[:, 11:12], None, ALU.mult), False)
            dve.wait_ge(S["vin"], 64)
            link(dve.tensor_scalar(unshift[:], b_scan[:], -1.0, ALPHA / BETA, ALU.mult, ALU.add))
            link(dve.memset(pscan[:, 1, 1, :], 0.0), False)
            link(dve.tensor_scalar(pst[:], state[0][:], BETA, ALPHA, ALU.mult, ALU.subtract))
            for q in (state[0], qraw):
                link(dve.tensor_scalar(q[:], q[:], kp[:, 3:4], 1 / RK[3], ALU.mult, ALU.mult))
            dve.sem_inc(S["pclip_ready"], 1)
            link(dve.tensor_scalar(wk[:, 3:4], wk[:, 1:2], 0.5, None, ALU.mult))
            dve.sem_inc(S["scale_rdy"], 1)
            dve.sem_inc(S["q_ready"], 1)
            dve.sem_inc(S["clip_ready"], 1)
            dve.sem_inc(S["ha_ready"], 1)
            dve.sem_inc(S["hb_ready"], 1)
            dve.sem_inc(S["stored"], 16)
            K = 8
            router = []

            def step(seg, i, u, t, scan, tile, old):
                k = [0]
                def chain(ins, wait=True):
                    k[0] += 1
                    ins.then_inc(S["dchain"], 1)
                    if wait:
                        dve.wait_ge(S["dchain"], t * K + k[0])
                at = (i, u) if tile and isinstance(i, int) else None
                if at == (0, 0):
                    router.clear()
                    router.extend(route(seg))
                for s in range(4):
                    gap, idle, late = [], [], []
                    n = 2 * i + u
                    if at == (0, 0):
                        if old and s == 0:
                            idle.append(lambda: hidden_up(seg - 1, TILES - 1, True))
                        if old and s == 1:
                            idle.append(lambda: hidden_gate(seg - 1, TILES - 1, 0, 1))
                        if s == 2:
                            idle.append(lambda: low_parts(seg, 0))
                            late.append(lambda: low_parts(seg, 1))
                        if s == 3:
                            idle.append(router[0])
                    elif at == (0, 1):
                        idle.append(router[1 + s])
                        if old:
                            late.append(lambda: sums(seg - 1, s))
                        if s == 1:
                            late.append(lambda: act_gate(seg * TILES, True))
                        if s == 2:
                            late.append(lambda: hidden_up(seg, 0, True))
                        if s == 3:
                            late.append(lambda: act_gate(seg * TILES + 1, True))
                    elif tile:
                        if s == 0:
                            if at == (1, 0):
                                gap.append(lambda: hidden_gate(seg, 0, 0, 0))
                            gap.append(lambda: hidden_up(seg, n - 1, at == (1, 0)))
                        if s == 1:
                            gap.append(lambda: hidden_gate(seg, n - 1, 1 - u, gate_row(i, u)))
                        if s == 2:
                            late.append(lambda: act_gate(seg * TILES + n))
                    if scan:
                        nxt = state[s + 1] if s < 3 else qraw
                        dve.wait_ge(S["t32_ready"], t * 4 + s + 1)
                        dve.tensor_tensor(th[:, :, 1, :], v3(t32[:]), th[:, :, 0, :], ALU.subtract).then_inc(S["tl_ready"], 1)
                        dve.wait_ge(S["sq_ready"], t * 4 + s + 1)
                        chain(dve.scalar_tensor_tensor(cub[:], sq[:], -3.0 - 3 / RK[0] if s == 0 else -3.0, state[s][:], ALU.add, ALU.mult), False)
                        for work in gap:
                            work()
                        dve.wait_ge(S["dchain"], t * K + k[0])
                        if s == 0:
                            dve.wait_ge(S["lin_ready"], t + 1)
                        else:
                            dve.wait_ge(S["e_ready"], t * 3 + s)
                        chain(dve.scalar_tensor_tensor(pscan[:, 1, 0, :], cub[:], -RK[s - 1] / 3, A[u][:, s, :], ALU.mult, ALU.add), False)
                        if s == 3:
                            dve.tensor_scalar(pst[:], A[u][:, 4, :], BETA * CLAMP - ALPHA, -BETA * CLAMP - ALPHA, ALU.min, ALU.max).then_inc(S["pclip_ready"], 1)
                        for work in idle:
                            work()
                        dve.wait_ge(S["dchain"], t * K + k[0])
                        dve.wait_ge(S["ic_ready"], t * 4 + s + 1)
                        dve.tensor_reduce(nxt[:], pscan[:, :, 0:2, :].rearrange("p a s w -> p w a s"), AX.XY, ALU.add).then_inc(S["q_ready"], 1)
                        if s == 3:
                            dve.wait_ge(S["q_ready"], t * 4 + 5)
                            dve.tensor_scalar(state[0][:], qraw[:], kp[:, 8:9], kp[:, 9:10], ALU.min, ALU.max).then_inc(S["clip_ready"], 1)
                            if at == (0, 0):
                                dve.wait_ge(S["copied"], seg + 1)
                                dve.wait_ge(S["q_high"], seg + 1)
                            dve.tensor_scalar(trace[:, :, bass.ds(2 * i + u, 1), :].rearrange("p c o b -> p c (o b)"), v3(qraw[:]), kp[:, 8:9], kp[:, 9:10], ALU.min, ALU.max).then_inc(S["traced"], 1)
                    else:
                        for work in gap + idle:
                            work()
                    for work in late:
                        work()

            def act_gate(n, at_once=False):
                if at_once:
                    dve.wait_ge(S["hb_ready"], n + 1)
                dve.wait_ge(S["sg_ready"], n + 1)
                dve.scalar_tensor_tensor(ha[:], sg[:], 1.0, pg[:, 0:GT], ALU.add, ALU.mult).then_inc(S["ha_ready"], 1)

            def hidden_up(seg, j, at_once=False):
                n = seg * TILES + j
                if at_once and not (isinstance(n, int) and n == 0):
                    dve.wait_ge(S["hid_ready"], n)
                dve.wait_ge(S["up_done"], n + 3)
                dve.wait_ge(S["ha_ready"], n + 2)
                dve.scalar_tensor_tensor(hb[:], pu[:, 0:GT], wk[:, 1:2], ha[:], ALU.mult, ALU.mult).then_inc(S["hb_ready"], 1)

            def hidden_gate(seg, j, slot, row):
                n = seg * TILES + j
                dve.wait_ge(S["hb_ready"], n + 2)
                dve.wait_ge(S["dn_done"], n + 2 if isinstance(j, int) and j == 0 else n + 1)
                g = gates[:, bass.ds(row, 1), :].rearrange("p o t -> p (o t)") if not isinstance(row, int) else gates[:, row, :]
                dve.scalar_tensor_tensor(hg[:, slot, :], hb[:], wk[:, 1:2], g, ALU.mult, ALU.mult).then_inc(S["hid_ready"], 1)

            def low_parts(seg, half):
                if half == 0:
                    dve.wait_ge(S["q_high"], seg + 1)
                c = slice(2 * half, 2 * half + 2)
                dve.scalar_tensor_tensor(qh[:, 1, c], trace[:, c].rearrange("p c t b -> p c (t b)"), kp[:, 10:11], qh[:, 0, c], ALU.mult, ALU.subtract).then_inc(S["q_low"], 1)

            def sums(seg, c):
                dve.wait_ge(S["dn_done"], seg * TILES + TILES + 2)
                dve.wait_ge(S["stored"], 16 * seg + 16)
                dve.scalar_tensor_tensor(oo[:, c], pd[c // 2][:, (c % 2) * GT:(c % 2 + 1) * GT].rearrange("p (t b) -> p t b", b=B), unshift[:, c:c + 1],
                                         xv[:, c, :, bass.ds(seg * G, G)].rearrange("p b t -> p t b"), ALU.add, ALU.add).then_inc(S["out_ready"], 1)

            RL = 10
            def route(seg):
                k = [0]
                base_ = setup[0]
                def chain(ins, wait=True):
                    k[0] += 1
                    ins.then_inc(S["rchain"], 1)
                    if wait:
                        dve.wait_ge(S["rchain"], base_ + seg * RL + k[0])

                def largest():
                    dve.wait_ge(S["rt_mm"], seg + 1)
                    chain(dve.tensor_copy(rt[:], pr_[:, 0:32].rearrange("p (c e) -> p c e", c=2)[:, :, 0:E1 + 1]))
                    dve.sem_inc(S["dveseq"], 1)
                    for c in range(2):
                        ins = dve.max(top[:, c, :], rt[:, c, 0:E1])
                    chain(ins)
                    dve.sem_inc(S["dveseq"], 1)
                    for c in range(2):
                        dve.max_index(topi[:, c, :], top[:, c, :], rt[:, c, 0:E1])
                    dve.tensor_scalar(neg[:], top[:, :, 0:1].rearrange("p c o -> p (c o)"), -1.0, None, ALU.mult).then_inc(S["rt_max"], 1)

                def chosen():
                    dve.wait_ge(S["rt_max"], seg + 1)
                    chain(dve.tensor_copy(topf[:], topi[:]))
                    for c in range(2):
                        ins = dve.tensor_scalar(msk[:, c, 0, :], lanes[:], topf[:, c, 0:1], None, ALU.is_equal)
                    chain(ins)
                    for c in range(2):
                        ins = dve.scalar_tensor_tensor(msk[:, c, 1, :], lanes[:], topf[:, c, 1:2], msk[:, c, 0, :], ALU.is_equal, ALU.add)
                    chain(ins)

                def weights():
                    dve.wait_ge(S["rt_exp"], seg + 1)
                    chain(dve.tensor_scalar(es[:, :, 1:2], es[:, :, 0:1], 2.0, None, ALU.mult), False)
                    chain(dve.tensor_scalar(es[:, :, 2:3], ex[:, :, E1:E1 + 1], 1.0, 2.0, ALU.add, ALU.mult))
                    chain(dve.reciprocal(es[:, :, 1:3], es[:, :, 1:3]))
                    for c in range(2):
                        ins = dve.scalar_tensor_tensor(msk[:, c, 0, :], msk[:, c, 1, :], es[:, c, 1:2], ex[:, c, 0:E1], ALU.mult, ALU.mult)
                    chain(ins)

                def widened():
                    for c in range(2):
                        dve.tensor_copy(wide[:, c, 0, :].rearrange("p (e r) -> p e r", r=LANES), msk[:, c, 0, :].unsqueeze(2).to_broadcast([P, E1, LANES]))
                        ins = dve.tensor_copy(wide[:, c, 1, :], es[:, c, 2:3].to_broadcast([P, P]))
                    ins.then_inc(S["rt_wide"], 1)

                def spread():
                    dve.wait_ge(S["rt_tr"], seg + 1)
                    chain(dve.tensor_copy(gates[:].rearrange("p a t -> p (a t)"), pr_[:]))
                    dve.sem_inc(S["dveseq"], 1)
                    assert k[0] == RL, k
                return [largest, chosen, weights, widened, spread]

            def last_tile(seg):
                hidden_up(seg, TILES - 2)
                hidden_gate(seg, TILES - 2, 1, 1)
                act_gate(seg * TILES + TILES - 1)
            walk(dve, step, last_tile)
            hidden_up(NG - 1, TILES - 1, True)
            hidden_gate(NG - 1, TILES - 1, 0, 1)
            for c in range(NC):
                sums(NG - 1, c)


def build(nc, dram, out):
    w_split = nc.dram_tensor("w_split", (TILES, P, 4 * N), F16, kind="Internal").ap()
    with nc.sbuf_tensor("xs", [P, NC * B * T + T], F32) as xs, nc.sbuf_tensor("wk", [P, 4], F32) as wk, \
            nc.sbuf_tensor("w_qkv", [P, NC, 3 * N], F32) as w_qkv:
        layer0(nc, dram, xs, wk, w_qkv, w_split)
        layer1(nc, dram, xs, wk, w_qkv[:, :, 0:N], w_split, out)


def arranged(inputs, np):
    g = lambda n: np.asarray(inputs[n])
    rows = lambda a: a.reshape(a.shape[0] // P, P, *a.shape[1:])
    part = lambda a: np.moveaxis(rows(a), 0, 1)
    up_q, dn_q = g("L0_ffn_w_up_q").T, g("L0_ffn_w_down_q").T
    a = {
        "x": np.ascontiguousarray(part(g("x").transpose(2, 0, 1))),
        "w_emb": part(g("L0_cond_W_emb")), "w_qkv": part(g("L0_cond_W_qkv")), "w_out": part(g("L0_cond_W_out")),
        "up_q": part(up_q), "dn_q": part(dn_q), "up_s": g("L0_ffn_w_up_scale").T, "dn_s": g("L0_ffn_w_down_scale").T,
        "lora": np.stack([np.concatenate([g("L0_ffn_w_up_lora_a").T, g("L0_ffn_w_up_lora_b")], 1),
                          np.concatenate([g("L0_ffn_w_down_lora_a").T, g("L0_ffn_w_down_lora_b")], 1)]),
        "vecs": np.concatenate([part(g("cond_2048").T).reshape(P, NC * B), part(g("L0_cond_b_emb")), part(g("L0_cond_g_norm")),
                                part(g("L0_ffn_b_up")), np.tile(g("L0_cond_g_q"), HPC)[:, None], np.tile(g("L0_cond_g_k"), HPC)[:, None]], 1),
        "b_dn": part(g("L0_ffn_b_down")), "b_scan": part(g("L1_cond_bias")),
    }
    def columns(e, s):
        mixed = g(e).reshape(E1, N, TE, LANES).transpose(2, 1, 0, 3).reshape(TE, NC, P, P)
        shared = g(s).reshape(NC, P, TS, P).transpose(2, 0, 1, 3)
        return np.concatenate([mixed, shared], 0).transpose(0, 2, 1, 3).reshape(TILES, P, N)
    down = np.concatenate([g("L1_ffn_Wd").reshape(E1, TE, LANES, N).transpose(1, 0, 2, 3).reshape(TE, P, N), g("L1_ffn_Sd").reshape(TS, P, N)], 0)
    a["w_tiles"] = np.concatenate([columns("L1_ffn_Wg", "L1_ffn_Sg"), columns("L1_ffn_Wu", "L1_ffn_Su"), down], 2)
    a["coupling"] = part(g("L1_cond_coupling").T)
    a["cond"] = part(g("cond_2048").T).reshape(P, W)
    a["w_router"] = part(np.concatenate([g("L1_ffn_Wr"), g("L1_ffn_Wsg")], 1))
    return {k: np.ascontiguousarray(v) for k, v in a.items()}


def kernel(**inputs):
    import numpy as _np
    import concourse.bacc as _bacc
    from concourse import mybir as _mybir
    from concourse.bass_utils import run_bass_kernel_spmd as _run

    nc = _bacc.Bacc("TRN2", target_bir_lowering=False, num_devices=1)
    arrays, dram = {}, {}
    for name, a in arranged(inputs, _np).items():
        arrays[f"in_{name}"] = a
        dram[name] = nc.dram_tensor(f"in_{name}", a.shape, _mybir.dt.from_np(a.dtype), kind="ExternalInput").ap()
    out = nc.dram_tensor("out", (P, NC, T, B), _mybir.dt.float32, kind="ExternalOutput").ap()
    build(nc, dram, out)
    r = _run(nc, [arrays], core_ids=[0])
    return r.results[0]["out"].transpose(3, 2, 1, 0).reshape(B, T, N)
```
